# Optimizing a Trainium2 kernel written in Bass

```python
import numpy as np
import jax
import jax.numpy as jnp

def _softmax(x, axis=-1):
    return jax.nn.softmax(x, axis=axis)

def _gelu(x):
    return jax.nn.gelu(x, approximate=True)

def _silu(x):
    return jax.nn.silu(x)

def _sigmoid(x):
    return jax.nn.sigmoid(x)

def _layernorm(x, axis=-1, eps=1e-05):
    m = jnp.mean(x, axis=axis, keepdims=True)
    v = jnp.var(x, axis=axis, keepdims=True)
    return (x - m) / jnp.sqrt(v + eps)

def _scatter_add(tgt, idx, src, axis=0):
    return tgt.at[idx].add(src)

def _segment_sum(src, seg, n):
    return jax.ops.segment_sum(src, seg, n)
kernel_name = 'mk_macaron_d2_jaxref_r8_92c44e'

def setup_inputs(seed: int=0):
    np.random.seed(seed)
    _w = jnp.asarray

    def _L0_attn_setup():
        import jax, jax.numpy as jnp
        import numpy as np
        import math
        B, L, D, MAXL = (4, 512, 128, 2048)

        def _shift1(a):
            return jnp.concatenate([jnp.zeros_like(a[:, :1]), a[:, :-1]], axis=1)
        key = jax.random.key(seed)
        ks = jax.random.split(key, 12)
        s = 0.02

        def w(k, shape):
            return jax.random.normal(k, shape, jnp.float32) * s
        return {'x': jax.random.normal(ks[0], (B, L, D), jnp.float32), 'pos_phases': jax.random.normal(ks[1], (MAXL, D), jnp.float32) * math.pi, 'Wpv': w(ks[2], (D, D)), 'bpv': jnp.zeros((D,), jnp.float32), 'Wk': w(ks[3], (D, D)), 'bk': jnp.zeros((D,), jnp.float32), 'Wkv': w(ks[4], (D, D)), 'bkv': jnp.zeros((D,), jnp.float32), 'Wg1': w(ks[5], (2 * D, D)), 'bg1': jnp.zeros((D,), jnp.float32), 'Wg2': w(ks[6], (D, 1)), 'bg2': jnp.zeros((1,), jnp.float32), 'Wb1': w(ks[7], (D, D // 2)), 'bb1': jnp.zeros((D // 2,), jnp.float32), 'Wb2': w(ks[8], (D // 2, 2)), 'bb2': jnp.zeros((2,), jnp.float32), 'ln_g': jnp.ones((D,), jnp.float32), 'ln_b': jnp.zeros((D,), jnp.float32), 'Wo': w(ks[9], (D, D)), 'bo': jnp.zeros((D,), jnp.float32)}
    _L0_attn_in = _L0_attn_setup()

    def _L0_ffn_setup():
        import jax, jax.numpy as jnp
        import numpy as np
        THRESH_FACTOR = 0.7

        def ternary_quantize(w):
            delta = THRESH_FACTOR * jnp.mean(jnp.abs(w))
            return jnp.where(w > delta, 1.0, jnp.where(w < -delta, -1.0, 0.0)).astype(w.dtype)
        key = jax.random.key(seed)
        k1, k2, k3 = jax.random.split(key, 3)
        B, S, D_IN, D_OUT = (8, 512, 128, 128)
        inp = {'input': jax.random.normal(k1, (B, S, D_IN), dtype=jnp.float32), 'weight': jax.random.normal(k2, (D_OUT, D_IN), dtype=jnp.float32) * (1.0 / np.sqrt(D_IN)), 'alpha': jnp.ones((1,), dtype=jnp.float32), 'bias': jax.random.normal(k3, (D_OUT,), dtype=jnp.float32) * (1.0 / np.sqrt(D_IN))}
        return inp
    _L0_ffn_in = _L0_ffn_setup()

    def _L1_attn_setup():
        import jax, jax.numpy as jnp
        import numpy as np
        EPS = 1e-08

        def rms_norm_multihead(x, weight):
            x32 = x.astype(jnp.float32)
            normed = x32 * jax.lax.rsqrt(jnp.mean(x32 * x32, axis=-1, keepdims=True) + EPS)
            return normed.astype(x.dtype) * weight
        key = jax.random.key(seed)
        k0, k1, k2 = jax.random.split(key, 3)
        B, L, D, H = (2, 128, 128, 16)
        d = D // H
        X = jax.random.normal(k0, (B, L, D), dtype=jnp.float32)
        Wq = jax.random.normal(k1, (D, D), dtype=jnp.float32) * 0.02
        Wv = jax.random.normal(k2, (D, D), dtype=jnp.float32) * 0.02
        q_norm_w = jnp.ones((H, d), dtype=jnp.float32)
        v_norm_w = jnp.ones((H, d), dtype=jnp.float32)
        return {'X': X, 'Wq': Wq, 'Wv': Wv, 'q_norm_w': q_norm_w, 'v_norm_w': v_norm_w}
    _L1_attn_in = _L1_attn_setup()

    def _L1_ffn_setup():
        import jax, jax.numpy as jnp
        import numpy as np
        B, S, D, H, E, F, K = (2, 128, 128, 16, 8, 512, 2)
        EPS = 1e-05

        def _layernorm(x, g, b):
            mu = jnp.mean(x, axis=-1, keepdims=True)
            var = jnp.mean(jnp.square(x - mu), axis=-1, keepdims=True)
            return (x - mu) * jax.lax.rsqrt(var + EPS) * g + b
        key = jax.random.key(seed)
        ks = jax.random.split(key, 12)
        w = lambda k, shape: jax.random.normal(k, shape, dtype=jnp.float32) * 0.02
        return {'x': jax.random.normal(ks[0], (B, S, D), dtype=jnp.float32), 'ln1_g': jnp.ones((D,), jnp.float32), 'ln1_b': jnp.zeros((D,), jnp.float32), 'ln2_g': jnp.ones((D,), jnp.float32), 'ln2_b': jnp.zeros((D,), jnp.float32), 'Wq': w(ks[1], (D, D)), 'Wk': w(ks[2], (D, D)), 'Wv': w(ks[3], (D, D)), 'Wo': w(ks[4], (D, D)), 'Wg': w(ks[5], (D, E)), 'W1': w(ks[6], (E, D, F)), 'b1': jnp.zeros((E, F), jnp.float32), 'W2': w(ks[7], (E, F, D)), 'b2': jnp.zeros((E, D), jnp.float32)}
    _L1_ffn_in = _L1_ffn_setup()
    _d = {'L0_attn_x': _L0_attn_in['x'], 'L0_attn_pos_phases': _L0_attn_in['pos_phases'], 'L0_attn_Wpv': _L0_attn_in['Wpv'], 'L0_attn_bpv': _L0_attn_in['bpv'], 'L0_attn_Wk': _L0_attn_in['Wk'], 'L0_attn_bk': _L0_attn_in['bk'], 'L0_attn_Wkv': _L0_attn_in['Wkv'], 'L0_attn_bkv': _L0_attn_in['bkv'], 'L0_attn_Wg1': _L0_attn_in['Wg1'], 'L0_attn_bg1': _L0_attn_in['bg1'], 'L0_attn_Wg2': _L0_attn_in['Wg2'], 'L0_attn_bg2': _L0_attn_in['bg2'], 'L0_attn_Wb1': _L0_attn_in['Wb1'], 'L0_attn_bb1': _L0_attn_in['bb1'], 'L0_attn_Wb2': _L0_attn_in['Wb2'], 'L0_attn_bb2': _L0_attn_in['bb2'], 'L0_attn_ln_g': _L0_attn_in['ln_g'], 'L0_attn_ln_b': _L0_attn_in['ln_b'], 'L0_attn_Wo': _L0_attn_in['Wo'], 'L0_attn_bo': _L0_attn_in['bo'], 'L0_ffn_weight': _L0_ffn_in['weight'], 'L0_ffn_alpha': _L0_ffn_in['alpha'], 'L0_ffn_bias': _L0_ffn_in['bias'], 'L1_attn_Wq': _L1_attn_in['Wq'], 'L1_attn_Wv': _L1_attn_in['Wv'], 'L1_attn_q_norm_w': _L1_attn_in['q_norm_w'], 'L1_attn_v_norm_w': _L1_attn_in['v_norm_w'], 'L1_ffn_ln1_g': _L1_ffn_in['ln1_g'], 'L1_ffn_ln1_b': _L1_ffn_in['ln1_b'], 'L1_ffn_ln2_g': _L1_ffn_in['ln2_g'], 'L1_ffn_ln2_b': _L1_ffn_in['ln2_b'], 'L1_ffn_Wq': _L1_ffn_in['Wq'], 'L1_ffn_Wk': _L1_ffn_in['Wk'], 'L1_ffn_Wv': _L1_ffn_in['Wv'], 'L1_ffn_Wo': _L1_ffn_in['Wo'], 'L1_ffn_Wg': _L1_ffn_in['Wg'], 'L1_ffn_W1': _L1_ffn_in['W1'], 'L1_ffn_b1': _L1_ffn_in['b1'], 'L1_ffn_W2': _L1_ffn_in['W2'], 'L1_ffn_b2': _L1_ffn_in['b2']}
    _x0 = _d['L0_attn_x']
    _d['L0_attn_x'] = jax.random.normal(jax.random.fold_in(jax.random.key(seed), 1), (8, 512, 128), dtype=_x0.dtype)
    del _x0
    return _d

def reference(L0_attn_x, L0_attn_pos_phases, L0_attn_Wpv, L0_attn_bpv, L0_attn_Wk, L0_attn_bk, L0_attn_Wkv, L0_attn_bkv, L0_attn_Wg1, L0_attn_bg1, L0_attn_Wg2, L0_attn_bg2, L0_attn_Wb1, L0_attn_bb1, L0_attn_Wb2, L0_attn_bb2, L0_attn_ln_g, L0_attn_ln_b, L0_attn_Wo, L0_attn_bo, L0_ffn_weight, L0_ffn_alpha, L0_ffn_bias, L1_attn_Wq, L1_attn_Wv, L1_attn_q_norm_w, L1_attn_v_norm_w, L1_ffn_ln1_g, L1_ffn_ln1_b, L1_ffn_ln2_g, L1_ffn_ln2_b, L1_ffn_Wq, L1_ffn_Wk, L1_ffn_Wv, L1_ffn_Wo, L1_ffn_Wg, L1_ffn_W1, L1_ffn_b1, L1_ffn_W2, L1_ffn_b2):

    def _L0_attn_ref(x, pos_phases, Wpv, bpv, Wk, bk, Wkv, bkv, Wg1, bg1, Wg2, bg2, Wb1, bb1, Wb2, bb2, ln_g, ln_b, Wo, bo):
        import jax, jax.numpy as jnp
        import numpy as np
        import math
        B, L, D, MAXL = (4, 512, 128, 2048)

        def _shift1(a):
            return jnp.concatenate([jnp.zeros_like(a[:, :1]), a[:, :-1]], axis=1)
        Bq, Lq, Dq = x.shape
        sqrtD = jnp.sqrt(jnp.float32(Dq))
        pp = pos_phases[:Lq]
        pos_cos, pos_sin = (jnp.cos(pp), jnp.sin(pp))
        pos_values = x @ Wpv + bpv
        pos_mem_cos = jnp.cumsum(pos_cos * pos_values, axis=1)
        pos_mem_sin = jnp.cumsum(pos_sin * pos_values, axis=1)
        pos_ret = (pos_cos * pos_mem_cos + pos_sin * pos_mem_sin) / sqrtD
        key_ph = jnp.tanh(x @ Wk + bk) * jnp.pi
        key_cos, key_sin = (jnp.cos(key_ph), jnp.sin(key_ph))
        kv_values = x @ Wkv + bkv
        x_shifted = _shift1(x)
        gate_in = jnp.concatenate([x, x_shifted], axis=-1)
        gh = jax.nn.gelu(gate_in @ Wg1 + bg1, approximate=False)
        value_gates = jax.nn.sigmoid(gh @ Wg2 + bg2)
        kc_s = _shift1(key_cos)
        ks_s = _shift1(key_sin)
        kv_mem_cos = jnp.cumsum(kc_s * kv_values * value_gates, axis=1)
        kv_mem_sin = jnp.cumsum(ks_s * kv_values * value_gates, axis=1)
        gate_cumsum = jnp.maximum(jnp.cumsum(value_gates, axis=1), 1.0)
        kv_ret = (key_cos * kv_mem_cos + key_sin * kv_mem_sin) / (jnp.sqrt(gate_cumsum) * sqrtD)
        bh = jax.nn.gelu(x @ Wb1 + bb1, approximate=False)
        bw = jax.nn.softmax(bh @ Wb2 + bb2, axis=-1)
        blended = bw[..., 0:1] * pos_ret + bw[..., 1:2] * kv_ret
        mu = jnp.mean(blended, axis=-1, keepdims=True)
        var = jnp.var(blended, axis=-1, keepdims=True)
        ln = (blended - mu) / jnp.sqrt(var + 1e-05) * ln_g + ln_b
        return x + ln @ Wo + bo

    def _L0_ffn_ref(input, weight, alpha, bias):
        import jax, jax.numpy as jnp
        import numpy as np
        THRESH_FACTOR = 0.7

        def ternary_quantize(w):
            delta = THRESH_FACTOR * jnp.mean(jnp.abs(w))
            return jnp.where(w > delta, 1.0, jnp.where(w < -delta, -1.0, 0.0)).astype(w.dtype)
        w_ternary = ternary_quantize(weight)
        w_eff = w_ternary * alpha
        out = jnp.einsum('bsd,od->bso', input, w_eff) + bias
        return out

    def _L1_attn_ref(X, Wq, Wv, q_norm_w, v_norm_w):
        import jax, jax.numpy as jnp
        import numpy as np
        EPS = 1e-08

        def rms_norm_multihead(x, weight):
            x32 = x.astype(jnp.float32)
            normed = x32 * jax.lax.rsqrt(jnp.mean(x32 * x32, axis=-1, keepdims=True) + EPS)
            return normed.astype(x.dtype) * weight
        B, L, D = X.shape
        H, d = q_norm_w.shape
        K = X.reshape(B, L, H, d)
        Q = rms_norm_multihead((X @ Wq.T).reshape(B, L, H, d), q_norm_w)
        V = rms_norm_multihead((X @ Wv.T).reshape(B, L, H, d), v_norm_w)
        W = jnp.cumsum(jnp.einsum('blhd,blhe->blhde', K, V), axis=1)
        out = jnp.einsum('blhd,blhde->blhe', Q, W).reshape(B, L, D)
        return out

    def _L1_ffn_ref(x, ln1_g, ln1_b, ln2_g, ln2_b, Wq, Wk, Wv, Wo, Wg, W1, b1, W2, b2):
        import jax, jax.numpy as jnp
        import numpy as np
        B, S, D, H, E, F, K = (2, 128, 128, 16, 8, 512, 2)
        EPS = 1e-05

        def _layernorm(x, g, b):
            mu = jnp.mean(x, axis=-1, keepdims=True)
            var = jnp.mean(jnp.square(x - mu), axis=-1, keepdims=True)
            return (x - mu) * jax.lax.rsqrt(var + EPS) * g + b
        Bb, Ss, Dd = x.shape
        Dh = Dd // H
        h = _layernorm(x, ln1_g, ln1_b)
        q = (h @ Wq).reshape(Bb, Ss, H, Dh)
        k = (h @ Wk).reshape(Bb, Ss, H, Dh)
        v = (h @ Wv).reshape(Bb, Ss, H, Dh)
        scores = jnp.einsum('bqhd,bkhd->bhqk', q, k) / jnp.sqrt(jnp.float32(Dh))
        attn = jax.nn.softmax(scores, axis=-1)
        ctx = jnp.einsum('bhqk,bkhd->bqhd', attn, v).reshape(Bb, Ss, Dd)
        x = x + ctx @ Wo
        m = _layernorm(x, ln2_g, ln2_b)
        xt = m.reshape(-1, Dd)
        T = xt.shape[0]
        probs = jax.nn.softmax(xt @ Wg, axis=-1)
        wts, idx = jax.lax.top_k(probs, K)
        wts = wts / jnp.sum(wts, axis=-1, keepdims=True)
        h1 = jax.nn.gelu(jnp.einsum('td,edf->etf', xt, W1) + b1[:, None, :])
        ye = jnp.einsum('etf,efd->etd', h1, W2) + b2[:, None, :]
        sel = ye[idx, jnp.arange(T)[:, None], :]
        moe_out = jnp.sum(wts[..., None] * sel, axis=1).reshape(Bb, Ss, Dd)
        return x + moe_out
    x = L0_attn_x
    x = x + 0.5 * _L0_ffn_ref(_layernorm(x, axis=-1), L0_ffn_weight, L0_ffn_alpha, L0_ffn_bias)
    x = x + _L0_attn_ref(_layernorm(x, axis=-1), L0_attn_pos_phases, L0_attn_Wpv, L0_attn_bpv, L0_attn_Wk, L0_attn_bk, L0_attn_Wkv, L0_attn_bkv, L0_attn_Wg1, L0_attn_bg1, L0_attn_Wg2, L0_attn_bg2, L0_attn_Wb1, L0_attn_bb1, L0_attn_Wb2, L0_attn_bb2, L0_attn_ln_g, L0_attn_ln_b, L0_attn_Wo, L0_attn_bo)
    x = x + 0.5 * _L0_ffn_ref(_layernorm(x, axis=-1), L0_ffn_weight, L0_ffn_alpha, L0_ffn_bias)
    x = x + 0.5 * _L1_ffn_ref(_layernorm(x, axis=-1), L1_ffn_ln1_g, L1_ffn_ln1_b, L1_ffn_ln2_g, L1_ffn_ln2_b, L1_ffn_Wq, L1_ffn_Wk, L1_ffn_Wv, L1_ffn_Wo, L1_ffn_Wg, L1_ffn_W1, L1_ffn_b1, L1_ffn_W2, L1_ffn_b2)
    x = x + _L1_attn_ref(_layernorm(x, axis=-1), L1_attn_Wq, L1_attn_Wv, L1_attn_q_norm_w, L1_attn_v_norm_w)
    x = x + 0.5 * _L1_ffn_ref(_layernorm(x, axis=-1), L1_ffn_ln1_g, L1_ffn_ln1_b, L1_ffn_ln2_g, L1_ffn_ln2_b, L1_ffn_Wq, L1_ffn_Wk, L1_ffn_Wv, L1_ffn_Wo, L1_ffn_Wg, L1_ffn_W1, L1_ffn_b1, L1_ffn_W2, L1_ffn_b2)
    return x

_drawn_inputs = setup_inputs


def setup_inputs(seed=0):
    import zlib

    import numpy as np

    out = dict(_drawn_inputs(seed))
    spreads = {'L0_attn_bpv': (0.0, 0.421),
     'L0_attn_bk': (0.0, 0.8),
     'L0_attn_bkv': (0.0, 0.556),
     'L0_attn_bg1': (0.0, 0.8),
     'L0_attn_bb1': (0.0, 0.8),
     'L0_attn_bb2': (0.0, 0.8),
     'L0_attn_ln_g': (1.0, 0.6),
     'L0_attn_ln_b': (0.0, 0.8),
     'L0_attn_bo': (0.0, 0.409),
     'L1_attn_q_norm_w': (1.0, 0.2),
     'L1_attn_v_norm_w': (1.0, 0.2),
     'L1_ffn_ln1_g': (1.0, 0.6),
     'L1_ffn_ln1_b': (0.0, 0.8),
     'L1_ffn_ln2_g': (1.0, 0.6),
     'L1_ffn_ln2_b': (0.0, 0.8),
     'L1_ffn_b1': (0.0, 0.8),
     'L1_ffn_b2': (0.0, 0.8)}
    factors = {'L0_attn_Wk': 8.0,
     'L0_attn_Wkv': 8.0,
     'L0_attn_Wg1': 8.0,
     'L0_attn_Wg2': 8.0,
     'L0_attn_Wb1': 8.0,
     'L0_attn_Wb2': 8.0,
     'L0_ffn_bias': 3.207,
     'L1_ffn_Wq': 8.0,
     'L1_ffn_Wk': 8.0,
     'L1_ffn_Wv': 8.0,
     'L1_ffn_Wo': 8.0,
     'L1_ffn_Wg': 8.0,
     'L1_ffn_W1': 8.0,
     'L1_ffn_W2': 8.0}
    for name, (base, spread) in spreads.items():
        noise = np.random.default_rng([zlib.crc32(name.encode()), seed]).standard_normal(out[name].shape)
        drawn = base * np.exp(spread * noise) if base else spread * noise
        out[name] = jnp.asarray(drawn.astype(out[name].dtype))
    for name, factor in factors.items():
        out[name] = (out[name] * factor).astype(out[name].dtype)
    return out
```

```python
from contextlib import ExitStack

import numpy as np

import concourse.bass as bass
from concourse import mybir

F32 = mybir.dt.float32
BF16 = mybir.dt.bfloat16
U32 = mybir.dt.uint32
ALU = mybir.AluOpType
ACT = mybir.ActivationFunctionType
AX = mybir.AxisListType

P = 128
B, S, D = 8, 512, 128
NT = S // P
H, DH = 16, 8
GH = 4
NG = H // GH
E, F = 8, 512
NF = F // P
HC = 32
EPS = 1e-5
EPS_RMS = 1e-8
SCORE_SCALE = float(DH) ** -0.5
RSQRT_D = float(D) ** -0.5
PI = 3.1415925
MAGIC = 12582912.0
TWO_PI_HI = 6.28125
TWO_PI_MID = 0.0019350051879882812
TWO_PI_LO = float(2.0 * np.pi - 6.28125 - 0.0019350051879882812)

INS = ["L0_attn_x", "L0_attn_pos_phases", "L0_attn_Wpv", "L0_attn_bpv", "L0_attn_Wk", "L0_attn_bk",
       "L0_attn_Wkv", "L0_attn_bkv", "L0_attn_Wg1", "L0_attn_bg1", "L0_attn_Wg2", "L0_attn_bg2",
       "L0_attn_Wb1", "L0_attn_bb1", "L0_attn_Wb2", "L0_attn_bb2", "L0_attn_ln_g", "L0_attn_ln_b",
       "L0_attn_Wo", "L0_attn_bo", "L0_ffn_weight", "L0_ffn_alpha", "L0_ffn_bias", "L1_attn_Wq",
       "L1_attn_Wv", "L1_attn_q_norm_w", "L1_attn_v_norm_w", "L1_ffn_ln1_g", "L1_ffn_ln1_b",
       "L1_ffn_ln2_g", "L1_ffn_ln2_b", "L1_ffn_Wq", "L1_ffn_Wk", "L1_ffn_Wv", "L1_ffn_Wo",
       "L1_ffn_Wg", "L1_ffn_W1", "L1_ffn_b1", "L1_ffn_W2", "L1_ffn_b2"]


class Signal:

    def __init__(self, sem, each):
        self.sem, self.each, self.before = sem, each, 0

    def at(self, b, n=None):
        n = self.each if n is None else n
        return (b if self.each == 1 else b * self.each) + (self.before + n)


class Turn:

    def __init__(self, step, k):
        self.step, self.sem, self.k = step, step.sem, k

    def at(self, b):
        return self.step.at(b, self.k)


class Signals:

    def __init__(self, nc, ctx, prefix):
        self.nc, self.ctx, self.prefix, self.found, self.runs = nc, ctx, prefix, {}, 0

    def run(self):
        for s in self.found.values():
            s.before = self.runs * B * s.each
        self.runs += 1
        return self

    def __call__(self, name, each=1):
        if name not in self.found:
            self.found[name] = Signal(self.ctx.enter_context(self.nc.semaphore(self.prefix + name)), each)
        return self.found[name]


class Memory:
    pass


def tile3(ap, n=NT):
    return ap.rearrange("p (t f) -> p t f", t=n)


def wide(ap, n):
    return ap.unsqueeze(2).to_broadcast([ap.shape[0], ap.shape[1], n])


def again(ap, n):
    return ap.unsqueeze(1).to_broadcast([ap.shape[0], n, ap.shape[1]])


def fence(dve, m):
    dve.memset(m.fence[:, :], 0.0)


def layer_stats(dve, m, src, st, mv, stats_done, mv_done, b):
    fence(dve, m)
    for i in range(NT):
        nc_stats = dve.bn_stats(st[:, i, :], src[:, i, :])
    nc_stats.then_inc(stats_done.sem, 1)
    dve.wait_ge(stats_done.sem, stats_done.at(b))
    fence(dve, m)
    for i in range(NT):
        agg = dve.bn_aggr(mv[:, i, :], st[:, i, :])
    agg.then_inc(mv_done.sem, 1)


def normalise(dve, dst, src, mv, rstd):
    for i in range(NT):
        last = dve.tensor_scalar(dst[:, i, :], src[:, i, :], mv[:, i, 0:1], rstd[:, i:i + 1],
                                 ALU.subtract, ALU.mult)
    return last


def transpose_tiles(pe, out, src, ident, n=NT):
    for i in range(n):
        last = pe.transpose(out[:, i * P:(i + 1) * P], src[:, i, :], ident)
    return last


def phase_load(nc, a, m, keep_ctx):
    with ExitStack() as ctx:
        def sb(name, shape, dt):
            return ctx.enter_context(nc.sbuf_tensor(name, shape, dt))

        def sem(name):
            return keep_ctx.enter_context(nc.semaphore(name))

        bank = [ctx.enter_context(nc.psum_tensor(f"ld_bank{i}", [P, 512], F32)) for i in range(8)]
        w_raw = sb("w_raw", [P, D], F32)
        w_abs = sb("w_abs", [P, D], F32)
        w_row = sb("w_row", [P, 1], F32)
        w_pos = sb("w_pos", [P, D], F32)
        w_neg = sb("w_neg", [P, D], F32)
        mean_w = sb("mean_w", [P, P], F32)
        delta = sb("delta", [P, 2], F32)
        alpha = sb("alpha", [P, 1], F32)
        phases = sb("phases", [P, NT, D], F32)
        turns = sb("turns", [P, S], F32)
        arg_sin = sb("arg_sin", [P, S], F32)
        arg_cos = sb("arg_cos", [P, S], F32)
        wrap = sb("wrap", [P, S], F32)
        lin_raw = sb("lin_raw", [P, 2, D], F32)
        wg2 = sb("wg2", [P, 1], F32)
        wb2 = sb("wb2", [D // 2, 2], F32)
        wb2_diff = sb("wb2_diff", [D // 2, 1], F32)
        bb2 = sb("bb2", [P, 2], F32)
        b1_raw = sb("b1_raw", [E * NF, P], F32)

        loaded = sem("loaded")
        pool_done = sem("ld_pool_done")
        dve_done = sem("ld_dve_done")
        abs_done = sem("abs_done")
        mean_ps = sem("mean_ps")
        phases_ps = sem("phases_ps")
        weff_ps = sem("weff_ps")
        lin_ps = sem("lin_ps")
        sin_args = sem("sin_args")
        tables = sem("tables")

        loads = []

        def load(dst, src):
            loads.append((dst, src))

        def column(dst, src):
            load(dst, src.unsqueeze(1))

        load(w_raw[:, :], a["L0_ffn_weight"])
        load(phases[:, :, :], a["L0_attn_pos_phases"][0:S, :].rearrange("(t p) d -> p t d", p=P))
        load(alpha[:, :], a["L0_ffn_alpha"].partition_broadcast(P))
        load(lin_raw[:, 0, :], a["L1_attn_Wq"])
        load(lin_raw[:, 1, :], a["L1_attn_Wv"])
        load(wg2[:, :], a["L0_attn_Wg2"])
        load(wb2[:, :], a["L0_attn_Wb2"])
        load(bb2[:, :], a["L0_attn_bb2"].partition_broadcast(P))
        load(m.x[:, :, :], a["L0_attn_x"].rearrange("b (t p) d -> p (b t) d", p=P))
        load(m.w_pv[:, :], a["L0_attn_Wpv"])
        load(m.w_k[:, :], a["L0_attn_Wk"])
        load(m.w_kv[:, :], a["L0_attn_Wkv"])
        load(m.w_g1[:, :, :], a["L0_attn_Wg1"].rearrange("(s d) n -> d s n", s=2))
        load(m.w_b1[:, :], a["L0_attn_Wb1"])
        load(m.w_o[:, :], a["L0_attn_Wo"])
        column(m.b_pv[:, :], a["L0_attn_bpv"])
        column(m.b_k[:, :], a["L0_attn_bk"])
        column(m.b_kv[:, :], a["L0_attn_bkv"])
        column(m.b_g1[:, :], a["L0_attn_bg1"])
        column(m.b_b1[:, :], a["L0_attn_bb1"])
        column(m.ln_g[:, :], a["L0_attn_ln_g"])
        column(m.ln_b[:, :], a["L0_attn_ln_b"])
        column(m.ln1_g[:, :], a["L1_ffn_ln1_g"])
        column(m.ln1_b[:, :], a["L1_ffn_ln1_b"])
        column(m.ln2_g[:, :], a["L1_ffn_ln2_g"])
        column(m.ln2_b[:, :], a["L1_ffn_ln2_b"])
        load(m.half_bg2[:, :], a["L0_attn_bg2"].partition_broadcast(P))
        load(m.ffn_bias[:, :], a["L0_ffn_bias"].partition_broadcast(P))
        load(m.bo[:, :], a["L0_attn_bo"].partition_broadcast(P))
        load(m.norm_w[:, 0:D], a["L1_attn_q_norm_w"].rearrange("h d -> (h d)").partition_broadcast(P))
        load(m.norm_w[:, D:2 * D], a["L1_attn_v_norm_w"].rearrange("h d -> (h d)").partition_broadcast(P))
        load(m.w_qkv[:, 0:D], a["L1_ffn_Wq"])
        load(m.w_qkv[:, D:2 * D], a["L1_ffn_Wk"])
        load(m.w_qkv[:, 2 * D:3 * D], a["L1_ffn_Wv"])
        load(m.w_out[:, :], a["L1_ffn_Wo"])
        load(m.w_gate[:, :], a["L1_ffn_Wg"])
        load(m.w1[:, :, :], a["L1_ffn_W1"].rearrange("e d f -> d e f"))
        load(m.w2[:, :, :, :], a["L1_ffn_W2"].rearrange("e (c p) d -> p e c d", p=P))
        load(b1_raw[:, :], a["L1_ffn_b1"].rearrange("e (c p) -> (e c) p", p=P))
        load(m.b2[:, :], a["L1_ffn_b2"])

        block = ctx.enter_context(nc.Block())

        @block.sync
        def _(sp):
            for dst, src in loads:
                sp.dma_start(dst, src).then_inc(loaded, 16)
            sp.wait_ge(loaded, 16 * len(loads))

        @block.gpsimd
        def _(pool):
            pool.memset(m.ident[:, :], 0.0).then_inc(pool_done, 1)
            pool.wait_ge(pool_done, 1)
            pool.affine_select(out=m.ident[:, :], in_=m.ident[:, :], compare_op=ALU.not_equal, fill=1.0,
                               base=0, pattern=[[-1, P]], channel_multiplier=1).then_inc(pool_done, 1)
            pool.wait_ge(pool_done, 2)
            pool.tensor_copy(m.ident_bf[:, :], m.ident[:, :]).then_inc(pool_done, 1)
            pool.memset(m.causal[:, :], 1.0).then_inc(pool_done, 1)
            pool.wait_ge(pool_done, 4)
            pool.affine_select(out=m.causal[:, :], in_=m.causal[:, :], compare_op=ALU.is_ge, fill=0.0,
                               base=0, pattern=[[1, P]], channel_multiplier=-1).then_inc(pool_done, 1)
            pool.iota(m.expert_id[:, :], pattern=[[1, E]], base=0, channel_multiplier=0,
                      allow_small_or_imprecise_dtypes=True).then_inc(pool_done, 1)
            pool.memset(mean_w[:, :], 0.7 / (D * D)).then_inc(pool_done, 1)
            pool.memset(m.half_pow[:, :], -0.5).then_inc(pool_done, 1)
            pool.memset(m.eps[:, :], EPS).then_inc(pool_done, 1)
            pool.memset(m.u_t[:, 0:1], 0.0).then_inc(pool_done, 1)
            pool.memset(m.key_cos[:, 0:1], 0.0).then_inc(pool_done, 1)
            pool.memset(m.key_sin[:, 0:1], 0.0).then_inc(pool_done, 1)
            pool.memset(m.half_pi[:, :], float(np.pi / 2)).then_inc(pool_done, 1)

        @block.vector
        def _(dve):
            count = [0]

            def then(ins):
                count[0] += 1
                ins.then_inc(dve_done, 1)
                dve.wait_ge(dve_done, count[0])

            then(dve.memset(m.zeros[:, :], 0.0))
            then(dve.memset(m.ones[:, :], 1.0))
            then(dve.memset(m.kz[:, :, :, :], 0.0))
            then(dve.memset(m.q_split[:, :, :, :], 0.0))
            then(dve.memset(m.k_split[:, :, :, :], 0.0))
            then(dve.memset(m.k_split[:, :, :, 24:26], 1.0))
            then(dve.memset(m.v_wide[:, :, :, :], 0.0))
            then(dve.memset(m.v_wide[:, :, :, DH:DH + 1], 1.0))
            dve.wait_ge(loaded, 16 * len(loads))
            dve.wait_ge(mean_ps, 1)
            then(dve.tensor_copy(delta[:, 0:1], bank[0][:, 0:1]))
            then(dve.tensor_scalar(delta[:, 1:2], delta[:, 0:1], -1.0, None, ALU.mult))
            then(dve.tensor_scalar(w_pos[:, :], w_raw[:, :], delta[:, 0:1], None, ALU.is_gt))
            then(dve.tensor_scalar(w_neg[:, :], w_raw[:, :], delta[:, 1:2], None, ALU.is_lt))
            then(dve.tensor_tensor(w_pos[:, :], w_pos[:, :], w_neg[:, :], ALU.subtract))
            then(dve.tensor_scalar(w_raw[:, :], w_pos[:, :], alpha[:, 0:1], None, ALU.mult))
            dve.wait_ge(weff_ps, 1)
            then(dve.tensor_copy(m.w_eff[:, :], bank[1][:, 0:P]))
            dve.wait_ge(lin_ps, 1)
            then(dve.tensor_copy(m.w_lin[:, :], bank[2][:, 0:2 * D]))
            then(dve.tensor_copy(m.b1[:, :, :], bank[2][:, 2 * P:2 * P + E * NF].rearrange("p (e c) -> p e c", e=E)))
            then(dve.tensor_scalar(m.w_g2[:, :], m.ones[:, 0:P], wg2[:, 0:1], None, ALU.mult))
            then(dve.tensor_tensor(wb2_diff[:, :], wb2[:, 0:1], wb2[:, 1:2], ALU.subtract))
            then(dve.tensor_scalar(m.w_b2[:, :], m.ones[0:D // 2, 0:P], wb2_diff[:, 0:1], None, ALU.mult))
            then(dve.tensor_tensor(m.half_bb2[:, :], bb2[:, 0:1], bb2[:, 1:2], ALU.subtract))
            then(dve.tensor_scalar(m.half_bb2[:, :], m.half_bb2[:, :], 0.5, None, ALU.mult))
            then(dve.tensor_scalar(m.half_bg2[:, :], m.half_bg2[:, :], 0.5, None, ALU.mult))
            then(dve.tensor_scalar(m.half_bias[:, :], m.ffn_bias[:, :], 0.5, None, ALU.mult))
            dve.wait_ge(phases_ps, 1)
            for arg, quarter in ((arg_sin, 0.0), (arg_cos, float(np.pi / 2))):
                then(dve.tensor_scalar(turns[:, :], bank[3][:, :], float(1 / (2 * np.pi)), MAGIC,
                                       ALU.mult, ALU.add))
                then(dve.tensor_scalar(turns[:, :], turns[:, :], MAGIC, None, ALU.subtract))
                then(dve.scalar_tensor_tensor(out=arg[:, :], in0=turns[:, :], scalar=-TWO_PI_HI,
                                              in1=bank[3][:, :], op0=ALU.mult, op1=ALU.add))
                then(dve.scalar_tensor_tensor(out=arg[:, :], in0=turns[:, :], scalar=-TWO_PI_MID,
                                              in1=arg[:, :], op0=ALU.mult, op1=ALU.add))
                then(dve.scalar_tensor_tensor(out=arg[:, :], in0=turns[:, :], scalar=-TWO_PI_LO,
                                              in1=arg[:, :], op0=ALU.mult, op1=ALU.add))
                if quarter:
                    then(dve.tensor_scalar(arg[:, :], arg[:, :], quarter, None, ALU.add))
                    then(dve.tensor_scalar(wrap[:, :], arg[:, :], PI, -2 * float(np.pi), ALU.is_gt, ALU.mult))
                    then(dve.tensor_tensor(arg[:, :], arg[:, :], wrap[:, :], ALU.add))
                then(dve.tensor_scalar(arg[:, :], arg[:, :], PI, -PI, ALU.min, ALU.max))
            dve.nop().then_inc(sin_args, 1)

        @block.scalar
        def _(act):
            act.wait_ge(loaded, 16 * len(loads))
            act.activation(w_abs[:, :], w_raw[:, :], ACT.Abs, accum_out=w_row[:, 0:1]).then_inc(abs_done, 1)
            act.wait_ge(sin_args, 1)
            act.activation(m.pos_sin[:, :], arg_sin[:, :], ACT.Sin).then_inc(tables, 1)
            act.activation(m.pos_cos[:, :], arg_cos[:, :], ACT.Sin).then_inc(tables, 1)

        @block.tensor
        def _(pe):
            pe.wait_ge(pool_done, 13)
            pe.wait_ge(abs_done, 1)
            pe.matmul(bank[0][:, 0:1], mean_w[:, :], w_row[:, :], start=True, stop=True).then_inc(mean_ps, 1)
            pe.wait_ge(loaded, 16 * len(loads))
            for i in range(NT):
                last = pe.transpose(bank[3][:, i * P:(i + 1) * P], phases[:, i, :], m.ident[:, :])
            last.then_inc(phases_ps, 1)
            for i in range(2):
                last = pe.transpose(bank[2][:, i * P:(i + 1) * P], lin_raw[:, i, :], m.ident[:, :])
            pe.transpose(bank[2][:, 2 * P:2 * P + E * NF], b1_raw[:, :], m.ident[0:E * NF, 0:E * NF])\
                .then_inc(lin_ps, 1)
            pe.wait_ge(dve_done, 14)
            pe.transpose(bank[1][:, 0:P], w_raw[:, :], m.ident[:, :]).then_inc(weff_ps, 1)


def phase_mixer(nc, m, signal):
    with ExitStack() as ctx:
        def sb(name, shape, dt=F32):
            return ctx.enter_context(nc.sbuf_tensor("mx_" + name, shape, dt))

        bank = [ctx.enter_context(nc.psum_tensor(f"mx_bank{i}", [P, 512], F32)) for i in range(8)]
        st = sb("st", [P, NT, 6])
        mv = sb("mv", [P, NT, 2])
        rstd = sb("rstd", [P, NT])
        var = sb("var", [P, NT])
        z = sb("z", [P, NT, D])
        z_t = sb("z_t", [P, S])
        x0 = sb("x0", [P, NT, D])
        x1 = sb("x1", [P, NT, D])
        x2 = sb("x2", [P, NT, D])
        u = sb("u", [P, NT, D])
        xu = sb("xu", [P, NT, D])
        pv = sb("pv", [P, S])
        kt = sb("kt", [P, S])
        kv = sb("kv", [P, S])
        kabs = sb("kabs", [P, S])
        gh = sb("gh", [P, S])
        bh = sb("bh", [D // 2, S])
        gt = sb("gt", [P, S])
        wt = sb("wt", [P, S])
        vg = sb("vg", [P, S])
        gcum = sb("gcum", [1, S])
        c_in = sb("c_in", [P, S])
        s_in = sb("s_in", [P, S])
        c_mem = sb("c_mem", [P, S])
        s_mem = sb("s_mem", [P, S])
        kc_in = sb("kc_in", [P, S])
        ks_in = sb("ks_in", [P, S])
        kc_mem = sb("kc_mem", [P, S])
        ks_mem = sb("ks_mem", [P, S])
        pos = sb("pos", [P, S])
        kvr = sb("kvr", [P, S])
        gm = sb("gm", [P, NT])
        gp = sb("gp", [P, NT])
        w0 = sb("w0", [P, NT])
        w1 = sb("w1", [P, NT])
        w1g = sb("w1g", [P, NT])
        pw = sb("pw", [P, NT, D])
        bl = sb("bl", [P, NT, D])

        LN = ("a", "u", "bl", "c")

        def turns(name, keys):
            return {k: Turn(signal(name, len(keys)), i + 1) for i, k in enumerate(keys)}

        stats = turns("stats", LN)
        mv_done = turns("mv", LN)
        var_done = turns("var", LN)
        rstd_done = turns("rstd", LN)
        z_done = turns("z", LN)
        zt_ps = turns("zt_ps", LN)
        zt_done = turns("zt", LN)
        biased = turns("biased", ("a", "c"))
        ffn_ps = turns("ffn_ps", ("a", "c"))
        x1_done = signal("x1")
        x3_done = signal("x3")
        proj_ps = signal("proj_ps", 5)
        gh_done = signal("gh", 2)
        gate_ps = signal("gate_ps", 2)
        gt_done = signal("gt", 2)
        kt_done = signal("kt")
        pv_done = signal("pv")
        kv_done = signal("kv")
        kabs_done = signal("kabs")
        key_done = signal("key", 2)
        vg_done = signal("vg")
        pos_in = signal("pos_in", 2)
        pos_mem = signal("pos_mem", 2)
        pos_mul = signal("pos_mul", 2)
        pos_done = signal("pos")
        gcum_done = signal("gcum")
        kvg_done = signal("kvg")
        key_in = signal("key_in", 2)
        key_mem = signal("key_mem", 2)
        key_mul = signal("key_mul", 2)
        kvr_done = signal("kvr")
        scal_ps = signal("scal_ps")
        scal_done = signal("scal", 3)
        gp_done = signal("gp")
        w1g_done = signal("w1g")
        ret_ps = signal("ret_ps", 2)
        pw_done = signal("pw")
        bl_done = signal("bl_sum")
        out_ps = signal("out_ps")
        xu_done = signal("xu")
        xub_done = signal("xub")
        x2_done = signal("x2")
        block = ctx.enter_context(nc.Block())

        def ln_pool(pool, k, b):
            pool.wait_ge(mv_done[k].sem, mv_done[k].at(b))
            pool.tensor_tensor(var[:, :], mv[:, :, 1], m.eps[:, :], ALU.add).then_inc(var_done[k].sem, 1)
            pool.wait_ge(var_done[k].sem, var_done[k].at(b))
            pool.tensor_tensor(rstd[:, :], var[:, :], m.half_pow[:, 0:NT], ALU.pow).then_inc(rstd_done[k].sem, 1)

        @block.gpsimd
        def _(pool):
            with pool.Fori(0, B) as b:
                x_b = m.x[:, bass.ds(b * NT, NT), :]
                ln_pool(pool, "a", b)
                pool.tensor_tensor(x0[:, :, :], x_b, again(m.half_bias[:, :], NT), ALU.add)\
                    .then_inc(biased["a"].sem, 1)
                ln_pool(pool, "u", b)
                pool.wait_ge(z_done["u"].sem, z_done["u"].at(b))
                pool.tensor_tensor(xu[:, :, :], x1[:, :, :], u[:, :, :], ALU.add).then_inc(xu_done.sem, 1)
                pool.wait_ge(xu_done.sem, xu_done.at(b))
                pool.tensor_tensor(xu[:, :, :], xu[:, :, :], again(m.bo[:, :], NT), ALU.add)\
                    .then_inc(xub_done.sem, 1)
                pool.wait_ge(scal_done.sem, scal_done.at(b))
                pool.tensor_tensor(gp[:, :], gm[:, :], m.half_pow[:, 0:NT], ALU.pow).then_inc(gp_done.sem, 1)
                pool.wait_ge(gp_done.sem, gp_done.at(b))
                pool.tensor_tensor(w1g[:, :], w1[:, :], gp[:, :], ALU.mult).then_inc(w1g_done.sem, 1)
                ln_pool(pool, "bl", b)
                ln_pool(pool, "c", b)
                pool.wait_ge(x2_done.sem, x2_done.at(b))
                pool.tensor_tensor(x0[:, :, :], x2[:, :, :], again(m.half_bias[:, :], NT), ALU.add)\
                    .then_inc(biased["c"].sem, 1)

        @block.vector
        def _(dve):
            with dve.Fori(0, B) as b:
                x_b = m.x[:, bass.ds(b * NT, NT), :]

                def ln(k, src, dst):
                    layer_stats(dve, m, src, st, mv, stats[k], mv_done[k], b)
                    dve.wait_ge(rstd_done[k].sem, rstd_done[k].at(b))
                    normalise(dve, dst, src, mv, rstd).then_inc(z_done[k].sem, 1)

                ln("a", x_b, z)
                dve.wait_ge(ffn_ps["a"].sem, ffn_ps["a"].at(b))
                dve.wait_ge(biased["a"].sem, biased["a"].at(b))
                dve.scalar_tensor_tensor(out=x1[:, :, :], in0=tile3(bank[1][:, :]), scalar=0.5,
                                         in1=x0[:, :, :], op0=ALU.mult, op1=ALU.add).then_inc(x1_done.sem, 1)
                dve.wait_ge(x1_done.sem, x1_done.at(b))
                ln("u", x1, u)
                dve.wait_ge(pv_done.sem, pv_done.at(b))
                dve.tensor_tensor(c_in[:, :], pv[:, :], m.pos_cos[:, :], ALU.mult).then_inc(pos_in.sem, 1)
                dve.tensor_tensor(s_in[:, :], pv[:, :], m.pos_sin[:, :], ALU.mult).then_inc(pos_in.sem, 1)
                dve.wait_ge(pos_in.sem, pos_in.at(b))
                dve.tensor_tensor_scan(c_mem[:, :], m.zeros[:, :], c_in[:, :], 0.0, ALU.add, ALU.add)\
                    .then_inc(pos_mem.sem, 1)
                dve.tensor_tensor_scan(s_mem[:, :], m.zeros[:, :], s_in[:, :], 0.0, ALU.add, ALU.add)\
                    .then_inc(pos_mem.sem, 1)
                dve.wait_ge(pos_mem.sem, pos_mem.at(b))
                dve.tensor_tensor(c_in[:, :], c_mem[:, :], m.pos_cos[:, :], ALU.mult).then_inc(pos_mul.sem, 1)
                dve.tensor_tensor(s_in[:, :], s_mem[:, :], m.pos_sin[:, :], ALU.mult).then_inc(pos_mul.sem, 1)
                dve.wait_ge(pos_mul.sem, pos_mul.at(b))
                dve.tensor_tensor(pos[:, :], c_in[:, :], s_in[:, :], ALU.add).then_inc(pos_done.sem, 1)
                dve.wait_ge(gt_done.sem, gt_done.at(b))
                dve.tensor_scalar(vg[:, :], gt[:, :], 0.5, 0.5, ALU.mult, ALU.add).then_inc(vg_done.sem, 1)
                dve.wait_ge(vg_done.sem, vg_done.at(b))
                dve.tensor_tensor_scan(gcum[:, :], m.zeros[0:1, :], vg[0:1, :], 0.0, ALU.add, ALU.add)\
                    .then_inc(gcum_done.sem, 1)
                dve.wait_ge(kv_done.sem, kv_done.at(b))
                dve.tensor_tensor(kv[:, :], kv[:, :], vg[:, :], ALU.mult).then_inc(kvg_done.sem, 1)
                dve.wait_ge(kvg_done.sem, kvg_done.at(b))
                dve.wait_ge(key_done.sem, key_done.at(b))
                dve.tensor_tensor(kc_in[:, :], kv[:, :], m.key_cos[:, 0:S], ALU.mult).then_inc(key_in.sem, 1)
                dve.tensor_tensor(ks_in[:, :], kv[:, :], m.key_sin[:, 0:S], ALU.mult).then_inc(key_in.sem, 1)
                dve.wait_ge(key_in.sem, key_in.at(b))
                dve.tensor_tensor_scan(kc_mem[:, :], m.zeros[:, :], kc_in[:, :], 0.0, ALU.add, ALU.add)\
                    .then_inc(key_mem.sem, 1)
                dve.tensor_tensor_scan(ks_mem[:, :], m.zeros[:, :], ks_in[:, :], 0.0, ALU.add, ALU.add)\
                    .then_inc(key_mem.sem, 1)
                dve.wait_ge(key_mem.sem, key_mem.at(b))
                dve.tensor_tensor(kc_in[:, :], kc_mem[:, :], m.key_cos[:, 1:S + 1], ALU.mult)\
                    .then_inc(key_mul.sem, 1)
                dve.tensor_tensor(ks_in[:, :], ks_mem[:, :], m.key_sin[:, 1:S + 1], ALU.mult)\
                    .then_inc(key_mul.sem, 1)
                dve.wait_ge(key_mul.sem, key_mul.at(b))
                dve.tensor_tensor(kvr[:, :], kc_in[:, :], ks_in[:, :], ALU.add).then_inc(kvr_done.sem, 1)
                dve.wait_ge(scal_ps.sem, scal_ps.at(b))
                dve.tensor_scalar(gm[:, :], bank[0][:, 0:NT], 1.0, None, ALU.max).then_inc(scal_done.sem, 1)
                dve.tensor_scalar(w0[:, :], bank[0][:, NT:2 * NT], 0.5 * RSQRT_D, 0.5 * RSQRT_D,
                                  ALU.mult, ALU.add).then_inc(scal_done.sem, 1)
                dve.tensor_scalar(w1[:, :], bank[0][:, NT:2 * NT], -0.5 * RSQRT_D, 0.5 * RSQRT_D,
                                  ALU.mult, ALU.add).then_inc(scal_done.sem, 1)
                dve.wait_ge(pw_done.sem, pw_done.at(b))
                dve.wait_ge(w1g_done.sem, w1g_done.at(b))
                dve.wait_ge(ret_ps.sem, ret_ps.at(b))
                for i in range(NT):
                    last = dve.scalar_tensor_tensor(out=bl[:, i, :], in0=bank[3][:, i * P:(i + 1) * P],
                                                    scalar=w1g[:, i:i + 1], in1=pw[:, i, :],
                                                    op0=ALU.mult, op1=ALU.add)
                last.then_inc(bl_done.sem, 1)
                dve.wait_ge(bl_done.sem, bl_done.at(b))
                ln("bl", bl, z)
                dve.wait_ge(out_ps.sem, out_ps.at(b))
                dve.wait_ge(xub_done.sem, xub_done.at(b))
                dve.tensor_tensor(x2[:, :, :], tile3(bank[5][:, :]), xu[:, :, :], ALU.add).then_inc(x2_done.sem, 1)
                dve.wait_ge(x2_done.sem, x2_done.at(b))
                ln("c", x2, z)
                dve.wait_ge(ffn_ps["c"].sem, ffn_ps["c"].at(b))
                dve.wait_ge(biased["c"].sem, biased["c"].at(b))
                dve.scalar_tensor_tensor(out=x_b, in0=tile3(bank[7][:, :]), scalar=0.5, in1=x0[:, :, :],
                                         op0=ALU.mult, op1=ALU.add).then_inc(x3_done.sem, 1)

        @block.scalar
        def _(act):
            with act.Fori(0, B) as b:
                act.wait_ge(zt_ps["a"].sem, zt_ps["a"].at(b))
                act.activation(z_t[:, :], bank[0][:, :], ACT.Copy).then_inc(zt_done["a"].sem, 1)
                act.wait_ge(zt_ps["u"].sem, zt_ps["u"].at(b))
                act.activation(m.u_t[:, 1:S + 1], bank[0][:, :], ACT.Copy).then_inc(zt_done["u"].sem, 1)
                act.wait_ge(proj_ps.sem, proj_ps.at(b, 1))
                act.activation(gh[:, :], bank[5][:, :], ACT.Gelu, bias=m.b_g1[:, 0:1]).then_inc(gh_done.sem, 1)
                act.wait_ge(proj_ps.sem, proj_ps.at(b, 2))
                act.activation(bh[:, :], bank[6][0:D // 2, :], ACT.Gelu, bias=m.b_b1[:, 0:1])\
                    .then_inc(gh_done.sem, 1)
                act.wait_ge(proj_ps.sem, proj_ps.at(b, 4))
                act.activation(pv[:, :], bank[2][:, :], ACT.Identity, bias=m.b_pv[:, 0:1]).then_inc(pv_done.sem, 1)
                act.wait_ge(proj_ps.sem, proj_ps.at(b, 5))
                act.activation(kv[:, :], bank[4][:, :], ACT.Identity, bias=m.b_kv[:, 0:1]).then_inc(kv_done.sem, 1)
                act.wait_ge(gate_ps.sem, gate_ps.at(b, 1))
                act.activation(gt[:, :], bank[7][:, :], ACT.Tanh, bias=m.half_bg2[:, 0:1], scale=0.5)\
                    .then_inc(gt_done.sem, 1)
                act.wait_ge(gate_ps.sem, gate_ps.at(b, 2))
                act.activation(wt[:, :], bank[1][:, :], ACT.Tanh, bias=m.half_bb2[:, 0:1], scale=0.5)\
                    .then_inc(gt_done.sem, 1)
                act.activation(kt[:, :], bank[3][:, :], ACT.Tanh, bias=m.b_k[:, 0:1]).then_inc(kt_done.sem, 1)
                act.wait_ge(kt_done.sem, kt_done.at(b))
                act.activation(kabs[:, :], kt[:, :], ACT.Abs).then_inc(kabs_done.sem, 1)
                act.activation(m.key_sin[:, 1:S + 1], kt[:, :], ACT.Sin, scale=PI).then_inc(key_done.sem, 1)
                act.wait_ge(kabs_done.sem, kabs_done.at(b))
                act.activation(m.key_cos[:, 1:S + 1], kabs[:, :], ACT.Sin, bias=m.half_pi[:, 0:1], scale=-PI)\
                    .then_inc(key_done.sem, 1)
                act.wait_ge(ret_ps.sem, ret_ps.at(b, 1))
                act.wait_ge(scal_done.sem, scal_done.at(b))
                for i in range(NT):
                    last = act.activation(pw[:, i, :], bank[2][:, i * P:(i + 1) * P], ACT.Copy, scale=w0[:, i:i + 1])
                last.then_inc(pw_done.sem, 1)
                act.wait_ge(zt_ps["bl"].sem, zt_ps["bl"].at(b))
                act.activation(z_t[:, :], bank[4][:, :], ACT.Identity, bias=m.ln_b[:, 0:1],
                               scale=m.ln_g[:, 0:1]).then_inc(zt_done["bl"].sem, 1)
                act.wait_ge(zt_ps["c"].sem, zt_ps["c"].at(b))
                act.activation(z_t[:, :], bank[6][:, :], ACT.Copy).then_inc(zt_done["c"].sem, 1)

        @block.tensor
        def _(pe):
            def ffn(k, out, b):
                pe.wait_ge(zt_done[k].sem, zt_done[k].at(b))
                for i in range(NT):
                    last = pe.matmul(out[:, i * P:(i + 1) * P], z_t[:, i * P:(i + 1) * P], m.w_eff[:, :],
                                     start=True, stop=True)
                last.then_inc(ffn_ps[k].sem, 1)

            with pe.Fori(0, B) as b:
                pe.wait_ge(z_done["a"].sem, z_done["a"].at(b))
                transpose_tiles(pe, bank[0], z, m.ident[:, :]).then_inc(zt_ps["a"].sem, 1)
                ffn("a", bank[1], b)
                pe.wait_ge(z_done["u"].sem, z_done["u"].at(b))
                transpose_tiles(pe, bank[0], u, m.ident[:, :]).then_inc(zt_ps["u"].sem, 1)
                pe.wait_ge(zt_done["u"].sem, zt_done["u"].at(b))
                cur, shifted = m.u_t[:, 1:S + 1], m.u_t[:, 0:S]
                pe.matmul(bank[5][:, :], m.w_g1[:, 0, :], cur, start=True, stop=False)
                pe.matmul(bank[5][:, :], m.w_g1[:, 1, :], shifted, start=False, stop=True).then_inc(proj_ps.sem, 1)
                pe.matmul(bank[6][0:D // 2, :], m.w_b1[:, :], cur, start=True, stop=True).then_inc(proj_ps.sem, 1)
                pe.matmul(bank[3][:, :], m.w_k[:, :], cur, start=True, stop=True).then_inc(proj_ps.sem, 1)
                pe.matmul(bank[2][:, :], m.w_pv[:, :], cur, start=True, stop=True).then_inc(proj_ps.sem, 1)
                pe.matmul(bank[4][:, :], m.w_kv[:, :], cur, start=True, stop=True).then_inc(proj_ps.sem, 1)
                pe.wait_ge(gh_done.sem, gh_done.at(b, 1))
                pe.matmul(bank[7][:, :], m.w_g2[:, :], gh[:, :], start=True, stop=True).then_inc(gate_ps.sem, 1)
                pe.wait_ge(gh_done.sem, gh_done.at(b, 2))
                pe.wait_ge(x1_done.sem, x1_done.at(b))
                pe.matmul(bank[1][:, :], m.w_b2[:, :], bh[:, :], start=True, stop=True).then_inc(gate_ps.sem, 1)
                pe.wait_ge(pos_done.sem, pos_done.at(b))
                transpose_tiles(pe, bank[2], tile3(pos[:, :]), m.ident[:, :]).then_inc(ret_ps.sem, 1)
                pe.wait_ge(gcum_done.sem, gcum_done.at(b))
                pe.wait_ge(gt_done.sem, gt_done.at(b))
                for i in range(NT):
                    pe.matmul(bank[0][:, i:i + 1], gcum[0:1, i * P:(i + 1) * P], m.ones[0:1, 0:1],
                              start=True, stop=True)
                for i in range(NT):
                    last = pe.matmul(bank[0][:, NT + i:NT + i + 1], wt[0:1, i * P:(i + 1) * P],
                                     m.ones[0:1, 0:1], start=True, stop=True)
                last.then_inc(scal_ps.sem, 1)
                pe.wait_ge(kvr_done.sem, kvr_done.at(b))
                transpose_tiles(pe, bank[3], tile3(kvr[:, :]), m.ident[:, :]).then_inc(ret_ps.sem, 1)
                pe.wait_ge(z_done["bl"].sem, z_done["bl"].at(b))
                transpose_tiles(pe, bank[4], z, m.ident[:, :]).then_inc(zt_ps["bl"].sem, 1)
                pe.wait_ge(zt_done["bl"].sem, zt_done["bl"].at(b))
                for i in range(NT):
                    last = pe.matmul(bank[5][:, i * P:(i + 1) * P], z_t[:, i * P:(i + 1) * P], m.w_o[:, :],
                                     start=True, stop=True)
                last.then_inc(out_ps.sem, 1)
                pe.wait_ge(z_done["c"].sem, z_done["c"].at(b))
                transpose_tiles(pe, bank[6], z, m.ident[:, :]).then_inc(zt_ps["c"].sem, 1)
                ffn("c", bank[7], b)


def phase_softmax(nc, m, signal, tag):
    with ExitStack() as ctx:
        def sb(name, shape, dt=F32):
            return ctx.enter_context(nc.sbuf_tensor(tag + name, shape, dt))

        bank = [ctx.enter_context(nc.psum_tensor(f"{tag}bank{i}", [P, 512], F32)) for i in range(2)]
        pair = [ctx.enter_context(nc.psum_tensor(f"{tag}pair{i}", [P, 2, 512], F32)) for i in range(2)]
        av = ctx.enter_context(nc.psum_tensor(tag + "av", [P, 512], F32))
        misc = ctx.enter_context(nc.psum_tensor(tag + "misc", [P, 512], F32))
        misc_bf = misc[:, :].bitcast(BF16)
        turn_bf = [pair[g // 2][:, g % 2, :].bitcast(BF16) for g in range(NG)]
        st = sb("st", [P, NT, 6])
        mv = sb("mv", [P, NT, 2])
        var = sb("var", [P, NT])
        rstd = sb("rstd", [P, NT])
        r_sq = sb("r_sq", [P, NT])
        v_y = sb("v_y", [P, NT])
        r_y = sb("r_y", [P, NT])
        rstd2 = sb("rstd2", [P, NT])
        z = sb("z", [P, NT, D])
        z2 = sb("z2", [P, NT, D])
        h_t = sb("h_t", [P, S])
        k_t = sb("k_t", [P, NG, S], BF16)
        q1 = sb("q1", [P, NG, S], BF16)
        q2 = sb("q2", [P, S], BF16)
        mx = sb("mx", [P, NT, H])
        prob = sb("prob", [P, 8, S])
        av_s = sb("av_s", [P, S])
        rec = sb("rec", [P, NT, GH])
        ctx_s = sb("ctx_s", [P, NT, D])
        ctx_t = sb("ctx_t", [P, S])

        stats = signal("stats")
        mv_done = signal("mv_done")
        var_done = signal("var_done")
        rstd_done = signal("rstd_done")
        rsq_done = signal("rsq_done")
        vy_done = signal("vy_done")
        vye_done = signal("vye_done")
        ry_done = signal("ry_done")
        rstd2_done = signal("rstd2_done")
        y_done = signal("y_done")
        z_done = signal("z_done")
        ht_ps = signal("ht_ps")
        ht_done = signal("ht_done")
        qkv_ps = signal("qkv_ps", NT)
        hi_done = signal("hi_done", NT)
        m_zero = signal("m_zero")
        lo_done = signal("lo_done", NT)
        v_done = signal("v_done", NT)
        kt_ps = signal("kt_ps", NG)
        kt_done = signal("kt_done", NG)
        q1_ps = signal("q1_ps", NG)
        q1_done = signal("q1_done", NG)
        kz_done = signal("kz_done", 16 * GH)
        s1_ps = signal("s1_ps", NG * 16)
        max_done = signal("max_done", NG * 16)
        mh_done = signal("mh_done", NG)
        ml_done = signal("ml_done", NG)
        q2_ps = signal("q2_ps", NG)
        q2_done = signal("q2_done", NG)
        s2_ps = signal("s2_ps", NG * 8)
        exp_done = signal("exp_done", NG * 8)
        av_part = signal("av_part", NG * 4)
        avs_done = signal("avs_done", NG)
        avt_ps = signal("avt_ps", NG)
        rec_done = signal("rec_done", NG)
        ctx_done = signal("ctx_done", NG)
        ct_ps = signal("ct_ps")
        ct_done = signal("ct_done")
        wo_ps = signal("wo_ps")
        y2_done = signal("y2_done")
        stats2 = signal("stats2")
        mv2_done = signal("mv2_done")
        var2_done = signal("var2_done")
        rstdb_done = signal("rstdb_done")
        z2_done = signal("z2_done")
        mt_ps = signal("mt_ps")
        mt_done = signal("mt_done")
        block = ctx.enter_context(nc.Block())

        @block.sync
        def _(sp):
            with sp.Fori(0, B) as b:
                sp.wait_ge(kt_done.sem, kt_done.at(b))
                for j in range(GH):
                    rows = slice(HC * j, HC * (j + 1))
                    sp.dma_start(m.kz[rows, j, :, :], k_t[rows, :, :]).then_inc(kz_done.sem, 16)
            sp.wait_ge(kz_done.sem, kz_done.at(B - 1))

        @block.gpsimd
        def _(pool):
            with pool.Fori(0, B) as b:
                pool.wait_ge(mv_done.sem, mv_done.at(b))
                pool.tensor_tensor(var[:, :], mv[:, :, 1], m.eps[:, :], ALU.add).then_inc(var_done.sem, 1)
                pool.wait_ge(var_done.sem, var_done.at(b))
                pool.tensor_tensor(rstd[:, :], var[:, :], m.half_pow[:, 0:NT], ALU.pow).then_inc(rstd_done.sem, 1)
                pool.wait_ge(rstd_done.sem, rstd_done.at(b))
                pool.tensor_tensor(r_sq[:, :], rstd[:, :], rstd[:, :], ALU.mult).then_inc(rsq_done.sem, 1)
                pool.wait_ge(rsq_done.sem, rsq_done.at(b))
                pool.tensor_tensor(v_y[:, :], r_sq[:, :], mv[:, :, 1], ALU.mult).then_inc(vy_done.sem, 1)
                pool.wait_ge(vy_done.sem, vy_done.at(b))
                pool.tensor_tensor(var[:, :], v_y[:, :], m.eps[:, :], ALU.add).then_inc(vye_done.sem, 1)
                pool.wait_ge(vye_done.sem, vye_done.at(b))
                pool.tensor_tensor(r_y[:, :], var[:, :], m.half_pow[:, 0:NT], ALU.pow).then_inc(ry_done.sem, 1)
                pool.wait_ge(ry_done.sem, ry_done.at(b))
                pool.tensor_tensor(rstd2[:, :], r_y[:, :], rstd[:, :], ALU.mult).then_inc(rstd2_done.sem, 1)
                pool.wait_ge(mv2_done.sem, mv2_done.at(b))
                pool.tensor_tensor(var[:, :], mv[:, :, 1], m.eps[:, :], ALU.add).then_inc(var2_done.sem, 1)
                pool.wait_ge(var2_done.sem, var2_done.at(b))
                pool.tensor_tensor(rstd[:, :], var[:, :], m.half_pow[:, 0:NT], ALU.pow).then_inc(rstdb_done.sem, 1)

        @block.vector
        def _(dve):
            with dve.Fori(0, B) as b:
                x_b = m.x[:, bass.ds(b * NT, NT), :]
                y_b = m.y[:, bass.ds(b * NT, NT), :]
                layer_stats(dve, m, x_b, st, mv, stats, mv_done, b)
                dve.wait_ge(rstd_done.sem, rstd_done.at(b))
                normalise(dve, y_b, x_b, mv, rstd).then_inc(y_done.sem, 1)
                dve.wait_ge(rstd2_done.sem, rstd2_done.at(b))
                normalise(dve, z, x_b, mv, rstd2).then_inc(z_done.sem, 1)
                dve.memset(m.q_split[:, :, :, 24:26], 0.0).then_inc(m_zero.sem, 1)
                for i in range(NT):
                    src = bank[i % 2]
                    dve.wait_ge(qkv_ps.sem, qkv_ps.at(b, i + 1))
                    dve.wait_ge(hi_done.sem, hi_done.at(b, i + 1))
                    heads = lambda lo: src[:, lo:lo + D].rearrange("p (h d) -> p h d", d=DH)
                    dve.scalar_tensor_tensor(out=m.q_split[:, i, :, 8:16], in0=heads(0), scalar=SCORE_SCALE,
                                             in1=m.q_split[:, i, :, 0:8], op0=ALU.mult, op1=ALU.subtract)
                    dve.tensor_tensor(m.k_split[:, i, :, 16:24], heads(D), m.k_split[:, i, :, 0:8],
                                      ALU.subtract).then_inc(lo_done.sem, 1)
                    dve.tensor_copy(m.v_wide[:, i, :, 0:DH], heads(2 * D)).then_inc(v_done.sem, 1)

                def row_max(g, n):
                    dve.wait_ge(s1_ps.sem, s1_ps.at(b, 16 * g + n + 1))
                    dve.tensor_reduce(mx[:, n // GH, GH * g + n % GH:GH * g + n % GH + 1], bank[n % 2][:, :],
                                      AX.X, ALU.max).then_inc(max_done.sem, 1)

                def write_max(g):
                    dve.wait_ge(max_done.sem, max_done.at(b, 16 * (g + 1)))
                    dve.wait_ge(q1_ps.sem, q1_ps.at(b))
                    heads = slice(GH * g, GH * (g + 1))
                    dve.tensor_scalar(m.q_split[:, :, heads, 24], mx[:, :, heads], -1.0, None, ALU.mult)\
                        .then_inc(mh_done.sem, 1)
                    dve.wait_ge(mh_done.sem, mh_done.at(b, g + 1))
                    dve.scalar_tensor_tensor(out=m.q_split[:, :, heads, 25], in0=mx[:, :, heads], scalar=-1.0,
                                             in1=m.q_split[:, :, heads, 24], op0=ALU.mult, op1=ALU.subtract)\
                        .then_inc(ml_done.sem, 1)

                def finish_group(g):
                    dve.wait_ge(av_part.sem, av_part.at(b, 4 * (g + 1)))
                    dve.tensor_copy(av_s[:, :], av[:, :]).then_inc(avs_done.sem, 1)
                    dve.wait_ge(avt_ps.sem, avt_ps.at(b, g + 1))
                    t = misc[:, :].rearrange("p (t h c) -> p t h c", t=NT, c=HC)
                    dve.reciprocal(rec[:, :, :], t[:, :, :, DH]).then_inc(rec_done.sem, 1)
                    dve.wait_ge(rec_done.sem, rec_done.at(b, g + 1))
                    for i in range(NT):
                        last = dve.tensor_tensor(
                            ctx_s[:, i, 32 * g:32 * (g + 1)].rearrange("p (h d) -> p h d", d=DH),
                            t[:, i, :, 0:DH], wide(rec[:, i, :], DH), ALU.mult)
                    last.then_inc(ctx_done.sem, 1)

                for n in range(16):
                    row_max(0, n)
                write_max(0)
                for g in range(NG):
                    if g + 1 < NG:
                        for n in range(16):
                            row_max(g + 1, n)
                        write_max(g + 1)
                    finish_group(g)
                dve.wait_ge(wo_ps.sem, wo_ps.at(b))
                dve.tensor_tensor(y_b, tile3(misc[:, :]), y_b, ALU.add).then_inc(y2_done.sem, 1)
                dve.wait_ge(y2_done.sem, y2_done.at(b))
                layer_stats(dve, m, y_b, st, mv, stats2, mv2_done, b)
                dve.wait_ge(rstdb_done.sem, rstdb_done.at(b))
                normalise(dve, z2, y_b, mv, rstd).then_inc(z2_done.sem, 1)

        @block.scalar
        def _(act):
            with act.Fori(0, B) as b:
                act.wait_ge(ht_ps.sem, ht_ps.at(b))
                act.activation(h_t[:, :], misc[:, :], ACT.Identity, bias=m.ln1_b[:, 0:1],
                               scale=m.ln1_g[:, 0:1]).then_inc(ht_done.sem, 1)
                for i in range(NT):
                    act.wait_ge(qkv_ps.sem, qkv_ps.at(b, i + 1))
                    src = bank[i % 2]
                    for q, lo, to, scale in ((m.q_split, 0, (0, 16), SCORE_SCALE), (m.k_split, D, (0, 8), 1.0)):
                        heads = src[:, lo:lo + D].rearrange("p (h d) -> p h d", d=DH)
                        for c in to:
                            last = act.activation(q[:, i, :, c:c + DH], heads, ACT.Copy, scale=scale)
                    last.then_inc(hi_done.sem, 1)
                for g in range(NG):
                    act.wait_ge(kt_ps.sem, kt_ps.at(b, g + 1))
                    act.activation(k_t[:, g, :], turn_bf[g][:, 0:512], ACT.Copy)\
                        .then_inc(kt_done.sem, 1)
                for g in range(NG):
                    act.wait_ge(q1_ps.sem, q1_ps.at(b, g + 1))
                    act.activation(q1[:, g, :], turn_bf[g][:, 0:512], ACT.Copy)\
                        .then_inc(q1_done.sem, 1)
                for g in range(NG):
                    act.wait_ge(q2_ps.sem, q2_ps.at(b, g + 1))
                    act.activation(q2[:, :], misc_bf[:, 0:512], ACT.Copy).then_inc(q2_done.sem, 1)
                    for n in range(8):
                        act.wait_ge(s2_ps.sem, s2_ps.at(b, 8 * g + n + 1))
                        if g or n >= 4:
                            act.wait_ge(av_part.sem, av_part.at(b, 4 * g + (n - 4) // 2 + 1))
                        act.activation(prob[:, 2 * (n % 4):2 * (n % 4) + 2, :], pair[n % 2][:, :, :], ACT.Exp)\
                            .then_inc(exp_done.sem, 1)
                act.wait_ge(ct_ps.sem, ct_ps.at(b))
                act.activation(ctx_t[:, :], misc[:, :], ACT.Copy).then_inc(ct_done.sem, 1)
                act.wait_ge(mt_ps.sem, mt_ps.at(b))
                act.activation(m.m_t[:, bass.ds(b * S, S)], misc[:, :], ACT.Identity, bias=m.ln2_b[:, 0:1],
                               scale=m.ln2_g[:, 0:1]).then_inc(mt_done.sem, 1)

        @block.tensor
        def _(pe):
            with pe.Fori(0, B) as b:
                pe.wait_ge(z_done.sem, z_done.at(b))
                transpose_tiles(pe, misc, z, m.ident[:, :]).then_inc(ht_ps.sem, 1)
                pe.wait_ge(ht_done.sem, ht_done.at(b))
                for i in range(NT):
                    if i >= 2:
                        pe.wait_ge(hi_done.sem, hi_done.at(b, i - 1))
                        pe.wait_ge(v_done.sem, v_done.at(b, i - 1))
                    pe.matmul(bank[i % 2][:, 0:3 * D], h_t[:, i * P:(i + 1) * P], m.w_qkv[:, :],
                              start=True, stop=True).then_inc(qkv_ps.sem, 1)
                pe.wait_ge(lo_done.sem, lo_done.at(b))
                for g in range(NG):
                    for i in range(NT):
                        last = pe.transpose(turn_bf[g][:, i * P:(i + 1) * P],
                                            m.k_split[:, i, GH * g:GH * (g + 1), :].rearrange("p h c -> p (h c)"),
                                            m.ident_bf[:, :])
                    last.then_inc(kt_ps.sem, 1)
                pe.wait_ge(m_zero.sem, m_zero.at(b))
                for g in range(NG):
                    pe.wait_ge(kt_done.sem, kt_done.at(b, g + 1))
                    for i in range(NT):
                        last = pe.transpose(turn_bf[g][:, i * P:(i + 1) * P],
                                            m.q_split[:, i, GH * g:GH * (g + 1), :].rearrange("p h c -> p (h c)"),
                                            m.ident_bf[:, :])
                    last.then_inc(q1_ps.sem, 1)
                pe.wait_ge(kz_done.sem, kz_done.at(b))

                def scores_for_max(g, n):
                    i, j = n // GH, n % GH
                    pe.wait_ge(q1_done.sem, q1_done.at(b, g + 1))
                    if g or n >= 2:
                        pe.wait_ge(max_done.sem, max_done.at(b, 16 * g + n - 1))
                    pe.matmul(bank[n % 2][:, :], q1[:, g, i * P:(i + 1) * P], m.kz[:, j, g, :],
                              start=True, stop=True).then_inc(s1_ps.sem, 1)

                def scores_shifted(g, n):
                    i, j = n // GH, n % GH
                    c = n // 2
                    if n % 2 == 0 and (g or c >= 2):
                        pe.wait_ge(exp_done.sem, exp_done.at(b, 8 * g + c - 1))
                    last = pe.matmul(pair[c % 2][:, n % 2, :], m.kz[:, j, g, i * P:(i + 1) * P], q2[:, :],
                                     start=True, stop=True)
                    if n % 2:
                        last.then_inc(s2_ps.sem, 1)

                def values(g, i):
                    pe.wait_ge(exp_done.sem, exp_done.at(b, 8 * g + 2 * i + 2))
                    if g and i == 0:
                        pe.wait_ge(avs_done.sem, avs_done.at(b, g))
                    for j in range(GH):
                        last = pe.matmul(av[HC * j:HC * (j + 1), :], m.v_wide[:, i, GH * g + j, :],
                                         prob[:, GH * (i % 2) + j, :], start=(i == 0), stop=(i == NT - 1))
                    last.then_inc(av_part.sem, 1)

                pe.wait_ge(v_done.sem, v_done.at(b))
                for n in range(16):
                    scores_for_max(0, n)
                for g in range(NG):
                    pe.wait_ge(ml_done.sem, ml_done.at(b, g + 1))
                    if g:
                        pe.wait_ge(ctx_done.sem, ctx_done.at(b, g))
                    else:
                        pe.wait_ge(q1_done.sem, q1_done.at(b))
                    for i in range(NT):
                        last = pe.transpose(misc_bf[:, i * P:(i + 1) * P],
                                            m.q_split[:, i, GH * g:GH * (g + 1), :].rearrange("p h c -> p (h c)"),
                                            m.ident_bf[:, :])
                    last.then_inc(q2_ps.sem, 1)
                    pe.wait_ge(q2_done.sem, q2_done.at(b, g + 1))
                    for n in range(16):
                        if g + 1 < NG:
                            scores_for_max(g + 1, n)
                        scores_shifted(g, n)
                        if n % 4 == 3 and n >= 7:
                            values(g, n // 4 - 1)
                    values(g, NT - 1)
                    pe.wait_ge(avs_done.sem, avs_done.at(b, g + 1))
                    transpose_tiles(pe, misc, tile3(av_s[:, :]), m.ident[:, :]).then_inc(avt_ps.sem, 1)
                pe.wait_ge(ctx_done.sem, ctx_done.at(b))
                transpose_tiles(pe, misc, ctx_s, m.ident[:, :]).then_inc(ct_ps.sem, 1)
                pe.wait_ge(ct_done.sem, ct_done.at(b))
                for i in range(NT):
                    last = pe.matmul(misc[:, i * P:(i + 1) * P], ctx_t[:, i * P:(i + 1) * P], m.w_out[:, :],
                                     start=True, stop=True)
                last.then_inc(wo_ps.sem, 1)
                pe.wait_ge(z2_done.sem, z2_done.at(b))
                transpose_tiles(pe, misc, z2, m.ident[:, :]).then_inc(mt_ps.sem, 1)
                pe.wait_ge(mt_done.sem, mt_done.at(b))


def phase_experts(nc, m, signal, tag, out=None):
    with ExitStack() as ctx:
        def sb(name, shape, dt=F32):
            return ctx.enter_context(nc.sbuf_tensor(tag + name, shape, dt))

        hid = [ctx.enter_context(nc.psum_tensor(f"{tag}hid{i}", [P, 512], F32)) for i in range(4)]
        yps = [ctx.enter_context(nc.psum_tensor(f"{tag}yps{i}", [P, 512], F32)) for i in range(2)]
        misc = [ctx.enter_context(nc.psum_tensor(f"{tag}misc{i}", [P, 512], F32)) for i in range(2)]
        h1 = sb("h1", [P, 2, NF, S])
        logit = sb("logit", [P, NT, E])
        top = sb("top", [P, NT, 8])
        top_i = sb("top_i", [P, NT, 8], U32)
        top_f = sb("top_f", [P, NT, 2])
        gap = sb("gap", [P, NT])
        gap_t = sb("gap_t", [P, NT])
        wts = sb("wts", [P, NT, 2])
        one1 = sb("one1", [P, NT, E])
        one2 = sb("one2", [P, NT, E])
        gates = sb("gates", [P, NT, E])
        gates_t = sb("gates_t", [E, S])
        acc = sb("acc", [P, NT, D])
        m_b = sb("m_b", [P, S])

        copied = signal("copied")
        lg_ps = signal("lg_ps")
        lg_done = signal("lg_done")
        top_done = signal("top_done")
        idx_done = signal("idx_done")
        idxf_done = signal("idxf_done")
        gap_done = signal("gap_done")
        gapt_done = signal("gapt_done")
        wts_done = signal("wts_done")
        one_done = signal("one_done")
        gates_done = signal("gates_done")
        gt_ps = signal("gt_ps")
        gt_done = signal("gt_done")
        b2_ps = signal("b2_ps")
        hid_ps = signal("hid_ps", E * NF)
        h1_done = signal("h1_done", E * NF)
        y_ps = signal("y_ps", E)
        acc_done = signal("acc_done", E + 1)
        x_done = signal("x_done")
        stored = signal("stored", 16)
        stored.before = 0
        block = ctx.enter_context(nc.Block())

        @block.sync
        def _(sp):
            if out is not None:
                with sp.Fori(0, B) as b:
                    sp.wait_ge(x_done.sem, x_done.at(b))
                    sp.dma_start(out[bass.ds(b, 1), :, :].rearrange("b (t p) d -> p (b t) d", p=P),
                                 m.x[:, bass.ds(b * NT, NT), :]).then_inc(stored.sem, 16)
                sp.wait_ge(stored.sem, stored.at(B - 1))

        @block.vector
        def _(dve):
            with dve.Fori(0, B) as b:
                x_b = m.x[:, bass.ds(b * NT, NT), :]
                y_b = m.y[:, bass.ds(b * NT, NT), :]
                dve.wait_ge(lg_ps.sem, lg_ps.at(b))
                dve.tensor_copy(logit[:, :, :], tile3(misc[0][:, 0:NT * E])).then_inc(lg_done.sem, 1)
                dve.wait_ge(lg_done.sem, lg_done.at(b))
                fence(dve, m)
                for i in range(NT):
                    last = dve.max(top[:, i, :], logit[:, i, :])
                last.then_inc(top_done.sem, 1)
                dve.wait_ge(top_done.sem, top_done.at(b))
                fence(dve, m)
                for i in range(NT):
                    last = dve.max_index(top_i[:, i, :], top[:, i, :], logit[:, i, :])
                last.then_inc(idx_done.sem, 1)
                dve.tensor_tensor(gap[:, :], top[:, :, 0], top[:, :, 1], ALU.subtract).then_inc(gap_done.sem, 1)
                dve.wait_ge(idx_done.sem, idx_done.at(b))
                dve.tensor_copy(top_f[:, :, :], top_i[:, :, 0:2]).then_inc(idxf_done.sem, 1)
                dve.wait_ge(gapt_done.sem, gapt_done.at(b))
                dve.tensor_scalar(wts[:, :, 0], gap_t[:, :], 0.5, 0.5, ALU.mult, ALU.add)
                dve.tensor_scalar(wts[:, :, 1], gap_t[:, :], -0.5, 0.5, ALU.mult, ALU.add).then_inc(wts_done.sem, 1)
                dve.wait_ge(wts_done.sem, wts_done.at(b))
                dve.wait_ge(idxf_done.sem, idxf_done.at(b))
                for i in range(NT):
                    dve.tensor_scalar(one1[:, i, :], m.expert_id[:, :], top_f[:, i, 0:1], wts[:, i, 0:1],
                                      ALU.is_equal, ALU.mult)
                    last = dve.tensor_scalar(one2[:, i, :], m.expert_id[:, :], top_f[:, i, 1:2], wts[:, i, 1:2],
                                             ALU.is_equal, ALU.mult)
                last.then_inc(one_done.sem, 1)
                dve.wait_ge(one_done.sem, one_done.at(b))
                dve.tensor_tensor(gates[:, :, :], one1[:, :, :], one2[:, :, :], ALU.add).then_inc(gates_done.sem, 1)
                dve.wait_ge(gt_ps.sem, gt_ps.at(b))
                dve.tensor_copy(gates_t[:, :], misc[1][0:E, :]).then_inc(gt_done.sem, 1)
                dve.wait_ge(b2_ps.sem, b2_ps.at(b))
                dve.tensor_tensor(acc[:, :, :], tile3(misc[0][:, :]), y_b, ALU.add).then_inc(acc_done.sem, 1)
                for e in range(E):
                    dve.wait_ge(y_ps.sem, y_ps.at(b, e + 1))
                    dve.wait_ge(acc_done.sem, acc_done.at(b, e + 1))
                    for i in range(NT):
                        last = dve.scalar_tensor_tensor(out=acc[:, i, :], in0=yps[e % 2][:, i * P:(i + 1) * P],
                                                        scalar=gates[:, i, e:e + 1], in1=acc[:, i, :],
                                                        op0=ALU.mult, op1=ALU.add)
                    last.then_inc(acc_done.sem, 1)
                dve.wait_ge(acc_done.sem, acc_done.at(b))
                dve.scalar_tensor_tensor(out=x_b, in0=acc[:, :, :], scalar=0.5, in1=x_b, op0=ALU.mult,
                                         op1=ALU.add).then_inc(x_done.sem, 1)

        @block.scalar
        def _(act):
            with act.Fori(0, B) as b:
                act.wait_ge(gap_done.sem, gap_done.at(b))
                act.activation(gap_t[:, :], gap[:, :], ACT.Tanh, scale=0.5).then_inc(gapt_done.sem, 1)
                for e in range(E):
                    for c in range(NF):
                        n = e * NF + c
                        act.wait_ge(hid_ps.sem, hid_ps.at(b, n + 1))
                        if e >= 2 and c == 0:
                            act.wait_ge(y_ps.sem, y_ps.at(b, e - 1))
                        act.activation(h1[:, e % 2, c, :], hid[n % 4][:, :], ACT.Gelu_apprx_tanh,
                                       bias=m.b1[:, e, c:c + 1]).then_inc(h1_done.sem, 1)

        @block.tensor
        def _(pe):
            with pe.Fori(0, B) as b:
                pe.wait_ge(copied.sem, copied.at(b))
                for i in range(NT):
                    last = pe.matmul(misc[0][:, i * E:(i + 1) * E], m_b[:, i * P:(i + 1) * P],
                                     m.w_gate[:, :], start=True, stop=True)
                last.then_inc(lg_ps.sem, 1)

                def hidden(e):
                    for c in range(NF):
                        n = e * NF + c
                        if n >= 4:
                            pe.wait_ge(h1_done.sem, h1_done.at(b, n - 3))
                        pe.matmul(hid[n % 4][:, :], m.w1[:, e, c * P:(c + 1) * P], m.m_t[:, bass.ds(b * S, S)],
                                  start=True, stop=True).then_inc(hid_ps.sem, 1)

                def outputs(e):
                    if e >= 2:
                        pe.wait_ge(acc_done.sem, acc_done.at(b, e))
                    pe.wait_ge(h1_done.sem, h1_done.at(b, NF * (e + 1)))
                    for i in range(NT):
                        for c in range(NF):
                            last = pe.matmul(yps[e % 2][:, i * P:(i + 1) * P],
                                             h1[:, e % 2, c, i * P:(i + 1) * P], m.w2[:, e, c, :],
                                             start=(c == 0), stop=(c == NF - 1))
                    last.then_inc(y_ps.sem, 1)

                hidden(0)
                pe.wait_ge(gates_done.sem, gates_done.at(b))
                for i in range(NT):
                    last = pe.transpose(misc[1][0:E, i * P:(i + 1) * P], gates[:, i, :], m.ident[:, :])
                last.then_inc(gt_ps.sem, 1)
                pe.wait_ge(gt_done.sem, gt_done.at(b))
                for i in range(NT):
                    last = pe.matmul(misc[0][:, i * P:(i + 1) * P], gates_t[:, i * P:(i + 1) * P], m.b2[:, :],
                                     start=True, stop=True)
                last.then_inc(b2_ps.sem, 1)
                for e in range(E):
                    if e + 1 < E:
                        hidden(e + 1)
                    outputs(e)

        @block.gpsimd
        def _(pool):
            pool.tensor_copy(m_b[:, :], m.m_t[:, 0:S]).then_inc(copied.sem, 1)
            with pool.Fori(1, B) as b:
                pool.wait_ge(lg_ps.sem, lg_ps.at(b, 0))
                pool.tensor_copy(m_b[:, :], m.m_t[:, bass.ds(b * S, S)]).then_inc(copied.sem, 1)


def phase_linear(nc, m, signal):
    with ExitStack() as ctx:
        def sb(name, shape, dt=F32):
            return ctx.enter_context(nc.sbuf_tensor("li_" + name, shape, dt))

        bank = [ctx.enter_context(nc.psum_tensor(f"li_bank{i}", [P, 512], F32)) for i in range(6)]
        av = ctx.enter_context(nc.psum_tensor("li_av", [P, 512], F32))
        misc = ctx.enter_context(nc.psum_tensor("li_misc", [P, 512], F32))
        turn_bf = [bank[2 + g][:, :].bitcast(BF16) for g in range(NG)]
        st = sb("st", [P, NT, 6])
        mv = sb("mv", [P, NT, 2])
        var = sb("var", [P, NT])
        rstd = sb("rstd", [P, NT])
        y = sb("y", [P, NT, D])
        y_t = sb("y_t", [P, S])
        sq = sb("sq", [P, NT, 2 * D])
        ss = sb("ss", [P, NT, 2 * H])
        ms = sb("ms", [P, NT, 2 * H])
        rr = sb("rr", [P, NT, 2 * H])
        pw = sb("pw", [P, NT, 2 * H])
        qv = sb("qv", [P, NT, 2 * D])
        k_t = sb("k_t", [P, NG, S], BF16)
        q1 = sb("q1", [P, NG, S], BF16)
        prob = sb("prob", [P, 8, S])
        av_s = sb("av_s", [P, S])
        ctx_s = sb("ctx_s", [P, NT, D])

        stats = signal("stats")
        mv_done = signal("mv")
        var_done = signal("var")
        rstd_done = signal("rstd")
        y_done = signal("y")
        yt_ps = signal("yt_ps")
        yt_done = signal("yt")
        qv_ps = signal("qv_ps", 2)
        sq_done = signal("sq", 2)
        ss_done = signal("ss")
        ms_done = signal("ms")
        rr_done = signal("rr")
        qr_done = signal("qr", 2)
        qw_done = signal("qw")
        hi_done = signal("hi", 2)
        lo_done = signal("lo", 2)
        v_done = signal("v")
        kt_ps = signal("kt_ps", NG)
        kt_done = signal("kt", NG)
        q1_ps = signal("q1_ps", NG)
        q1_done = signal("q1", NG)
        kz_done = signal("kz", 16 * GH)
        s_ps = signal("s_ps", NG * 16)
        mask_done = signal("mask", NG * 16)
        rest_done = signal("rest", NG * 12)
        av_part = signal("av_part", NG * 4)
        avs_done = signal("avs", NG)
        avt_ps = signal("avt_ps", NG)
        ctx_done = signal("ctx", NG)
        x_done = signal("x")
        pow_init = signal("pow_init").sem
        block = ctx.enter_context(nc.Block())

        @block.sync
        def _(sp):
            with sp.Fori(0, B) as b:
                sp.wait_ge(kt_done.sem, kt_done.at(b))
                for j in range(GH):
                    rows = slice(HC * j, HC * (j + 1))
                    sp.dma_start(m.kz[rows, j, :, :], k_t[rows, :, :]).then_inc(kz_done.sem, 16)
            sp.wait_ge(kz_done.sem, kz_done.at(B - 1))

        @block.gpsimd
        def _(pool):
            pool.memset(pw[:, :, :], -0.5).then_inc(pow_init, 1)
            pool.wait_ge(pow_init, 1)
            with pool.Fori(0, B) as b:
                pool.wait_ge(mv_done.sem, mv_done.at(b))
                pool.tensor_tensor(var[:, :], mv[:, :, 1], m.eps[:, :], ALU.add).then_inc(var_done.sem, 1)
                pool.wait_ge(var_done.sem, var_done.at(b))
                pool.tensor_tensor(rstd[:, :], var[:, :], m.half_pow[:, 0:NT], ALU.pow).then_inc(rstd_done.sem, 1)
                pool.wait_ge(ms_done.sem, ms_done.at(b))
                pool.tensor_tensor(rr[:, :, :], ms[:, :, :], pw[:, :, :], ALU.pow).then_inc(rr_done.sem, 1)

        def per_head(ap):
            return ap.rearrange("p t (h d) -> p t h d", d=DH)

        @block.vector
        def _(dve):
            dve.memset(m.q_split[:, :, :, 24:26], 0.0)
            with dve.Fori(0, B) as b:
                x_b = m.x[:, bass.ds(b * NT, NT), :]
                layer_stats(dve, m, x_b, st, mv, stats, mv_done, b)
                dve.wait_ge(rstd_done.sem, rstd_done.at(b))
                normalise(dve, y, x_b, mv, rstd).then_inc(y_done.sem, 1)
                dve.wait_ge(sq_done.sem, sq_done.at(b))
                dve.tensor_reduce(ss[:, :, :], per_head(sq[:, :, :]), AX.X, ALU.add).then_inc(ss_done.sem, 1)
                dve.wait_ge(ss_done.sem, ss_done.at(b))
                dve.tensor_scalar(ms[:, :, :], ss[:, :, :], 1.0 / DH, EPS_RMS, ALU.mult, ALU.add)\
                    .then_inc(ms_done.sem, 1)
                dve.wait_ge(hi_done.sem, hi_done.at(b, 1))
                dve.tensor_tensor(m.k_split[:, :, :, 16:24], per_head(y[:, :, :]), m.k_split[:, :, :, 0:8],
                                  ALU.subtract).then_inc(lo_done.sem, 1)
                dve.wait_ge(rr_done.sem, rr_done.at(b))
                for c in range(2):
                    for i in (2 * c, 2 * c + 1):
                        o = (i % 2) * 2 * D
                        last = dve.tensor_tensor(
                            qv[:, i, :].rearrange("p (h d) -> p h d", d=DH),
                            bank[c][:, o:o + 2 * D].rearrange("p (h d) -> p h d", d=DH),
                            wide(rr[:, i, :], DH), ALU.mult)
                    last.then_inc(qr_done.sem, 1)
                dve.wait_ge(qr_done.sem, qr_done.at(b))
                dve.tensor_tensor(qv[:, :, :], qv[:, :, :], again(m.norm_w[:, :], NT), ALU.mult)\
                    .then_inc(qw_done.sem, 1)
                dve.wait_ge(qw_done.sem, qw_done.at(b))
                dve.tensor_copy(m.v_wide[:, :, :, 0:DH], per_head(qv[:, :, D:2 * D])).then_inc(v_done.sem, 1)
                dve.wait_ge(hi_done.sem, hi_done.at(b, 2))
                dve.tensor_tensor(m.q_split[:, :, :, 8:16], per_head(qv[:, :, 0:D]), m.q_split[:, :, :, 0:8],
                                  ALU.subtract).then_inc(lo_done.sem, 1)
                for g in range(NG):
                    for n in range(16):
                        i, s = n // GH, (16 * g + n) % 6
                        dve.wait_ge(s_ps.sem, s_ps.at(b, 16 * g + n + 1))
                        if g or n >= 8:
                            dve.wait_ge(av_part.sem, av_part.at(b, 4 * g + n // 4 - 1))
                        if n < 12:
                            dve.wait_ge(rest_done.sem, rest_done.at(b, 12 * g + n + 1))
                        dve.tensor_tensor(prob[:, n % 8, i * P:(i + 1) * P], bank[s][:, i * P:(i + 1) * P],
                                          m.causal[:, :], ALU.mult).then_inc(mask_done.sem, 1)
                    dve.wait_ge(av_part.sem, av_part.at(b, 4 * (g + 1)))
                    dve.tensor_copy(av_s[:, :], av[:, :]).then_inc(avs_done.sem, 1)
                    dve.wait_ge(avt_ps.sem, avt_ps.at(b, g + 1))
                    t = misc[:, :].rearrange("p (t h c) -> p t h c", t=NT, c=HC)
                    for i in range(NT):
                        last = dve.tensor_copy(
                            ctx_s[:, i, 32 * g:32 * (g + 1)].rearrange("p (h d) -> p h d", d=DH), t[:, i, :, 0:DH])
                    last.then_inc(ctx_done.sem, 1)
                dve.wait_ge(ctx_done.sem, ctx_done.at(b))
                dve.tensor_tensor(x_b, x_b, ctx_s[:, :, :], ALU.add).then_inc(x_done.sem, 1)

        @block.scalar
        def _(act):
            with act.Fori(0, B) as b:
                act.wait_ge(yt_ps.sem, yt_ps.at(b))
                act.activation(y_t[:, :], misc[:, :], ACT.Copy).then_inc(yt_done.sem, 1)
                for c in (0, 8):
                    last = act.activation(m.k_split[:, :, :, c:c + DH], per_head(y[:, :, :]), ACT.Copy)
                last.then_inc(hi_done.sem, 1)
                for c in range(2):
                    act.wait_ge(qv_ps.sem, qv_ps.at(b, c + 1))
                    act.activation(sq[:, 2 * c:2 * c + 2, :], tile3(bank[c][:, :], 2), ACT.Square)\
                        .then_inc(sq_done.sem, 1)
                act.wait_ge(qw_done.sem, qw_done.at(b))
                for c in (0, 16):
                    last = act.activation(m.q_split[:, :, :, c:c + DH], per_head(qv[:, :, 0:D]), ACT.Copy)
                last.then_inc(hi_done.sem, 1)
                for g in range(NG):
                    act.wait_ge(kt_ps.sem, kt_ps.at(b, g + 1))
                    act.activation(k_t[:, g, :], turn_bf[g][:, 0:512], ACT.Copy)\
                        .then_inc(kt_done.sem, 1)
                for g in range(NG):
                    act.wait_ge(q1_ps.sem, q1_ps.at(b, g + 1))
                    act.activation(q1[:, g, :], turn_bf[g][:, 0:512], ACT.Copy)\
                        .then_inc(q1_done.sem, 1)
                for g in range(NG):
                    for n in range(12):
                        i, s = n // GH, (16 * g + n) % 6
                        act.wait_ge(s_ps.sem, s_ps.at(b, 16 * g + n + 1))
                        if g or n >= 8:
                            act.wait_ge(av_part.sem, av_part.at(b, 4 * g + n // 4 - 1))
                        act.activation(prob[:, n % 8, (i + 1) * P:], bank[s][:, (i + 1) * P:], ACT.Copy)\
                            .then_inc(rest_done.sem, 1)

        @block.tensor
        def _(pe):
            with pe.Fori(0, B) as b:
                pe.wait_ge(y_done.sem, y_done.at(b))
                transpose_tiles(pe, misc, y, m.ident[:, :]).then_inc(yt_ps.sem, 1)
                pe.wait_ge(yt_done.sem, yt_done.at(b))
                for i in range(NT):
                    o = (i % 2) * 2 * D
                    last = pe.matmul(bank[i // 2][:, o:o + 2 * D], y_t[:, i * P:(i + 1) * P], m.w_lin[:, :],
                                     start=True, stop=True)
                    if i % 2:
                        last.then_inc(qv_ps.sem, 1)
                pe.wait_ge(lo_done.sem, lo_done.at(b, 1))
                for g in range(NG):
                    for i in range(NT):
                        last = pe.transpose(turn_bf[g][:, i * P:(i + 1) * P],
                                            m.k_split[:, i, GH * g:GH * (g + 1), :].rearrange("p h c -> p (h c)"),
                                            m.ident_bf[:, :])
                    last.then_inc(kt_ps.sem, 1)
                pe.wait_ge(lo_done.sem, lo_done.at(b, 2))
                for g in range(NG):
                    pe.wait_ge(kt_done.sem, kt_done.at(b, g + 1))
                    for i in range(NT):
                        last = pe.transpose(turn_bf[g][:, i * P:(i + 1) * P],
                                            m.q_split[:, i, GH * g:GH * (g + 1), :].rearrange("p h c -> p (h c)"),
                                            m.ident_bf[:, :])
                    last.then_inc(q1_ps.sem, 1)
                pe.wait_ge(kz_done.sem, kz_done.at(b))
                pe.wait_ge(q1_done.sem, q1_done.at(b))
                pe.wait_ge(v_done.sem, v_done.at(b))

                def scores(g, n):
                    i, j, s = n // GH, n % GH, 16 * g + n
                    if s >= 6:
                        p = s - 6
                        pe.wait_ge(mask_done.sem, mask_done.at(b, p + 1))
                        pe.wait_ge(rest_done.sem, rest_done.at(b, 12 * (p // 16) + min(p % 16 + 1, 12)))
                    pe.matmul(bank[s % 6][:, i * P:], m.kz[:, j, g, i * P:(i + 1) * P], q1[:, g, i * P:],
                              start=True, stop=True).then_inc(s_ps.sem, 1)

                def values(g, i):
                    pe.wait_ge(mask_done.sem, mask_done.at(b, 16 * g + 4 * (i + 1)))
                    pe.wait_ge(rest_done.sem, rest_done.at(b, 12 * g + min(4 * (i + 1), 12)))
                    if g and i == 0:
                        pe.wait_ge(avs_done.sem, avs_done.at(b, g))
                    for j in range(GH):
                        last = pe.matmul(av[HC * j:HC * (j + 1), i * P:], m.v_wide[:, i, GH * g + j, :],
                                         prob[:, GH * (i % 2) + j, i * P:], start=(i == 0), stop=(i == NT - 1))
                    last.then_inc(av_part.sem, 1)

                for g in range(NG):
                    for n in range(16):
                        scores(g, n)
                        if n % 4 == 3 and n >= 7:
                            values(g, n // 4 - 1)
                    values(g, NT - 1)
                    pe.wait_ge(avs_done.sem, avs_done.at(b, g + 1))
                    if g:
                        pe.wait_ge(ctx_done.sem, ctx_done.at(b, g))
                    transpose_tiles(pe, misc, tile3(av_s[:, :]), m.ident[:, :]).then_inc(avt_ps.sem, 1)
                pe.wait_ge(ctx_done.sem, ctx_done.at(b))


def macaron_kernel(nc, a, out):
    with ExitStack() as ctx:
        m = Memory()

        def keep(name, shape, dt=F32):
            return ctx.enter_context(nc.sbuf_tensor("m_" + name, shape, dt))

        m.x = keep("x", [P, B * NT, D])
        m.y = keep("y", [P, B * NT, D])
        m.m_t = keep("m_t", [P, B * S])
        m.ident = keep("ident", [P, P])
        m.ident_bf = keep("ident_bf", [P, P], BF16)
        m.causal = keep("causal", [P, P])
        m.expert_id = keep("expert_id", [P, E])
        m.half_pow = keep("half_pow", [P, NT])
        m.eps = keep("eps", [P, NT])
        m.fence = keep("fence", [1, 1])
        m.half_pi = keep("half_pi", [P, 1])
        m.zeros = keep("zeros", [P, S])
        m.ones = keep("ones", [P, P])
        m.pos_cos = keep("pos_cos", [P, S])
        m.pos_sin = keep("pos_sin", [P, S])
        m.key_cos = keep("key_cos", [P, S + 1])
        m.key_sin = keep("key_sin", [P, S + 1])
        m.u_t = keep("u_t", [P, S + 1])
        m.w_pv = keep("w_pv", [P, D])
        m.w_k = keep("w_k", [P, D])
        m.w_kv = keep("w_kv", [P, D])
        m.w_o = keep("w_o", [P, D])
        m.w_eff = keep("w_eff", [P, D])
        m.w_g2 = keep("w_g2", [P, D])
        m.w_out = keep("w_out", [P, D])
        m.w_g1 = keep("w_g1", [P, 2, D])
        m.w_b1 = keep("w_b1", [P, D // 2])
        m.w_b2 = keep("w_b2", [D // 2, P])
        m.w_lin = keep("w_lin", [P, 2 * D])
        m.w_qkv = keep("w_qkv", [P, 3 * D])
        m.w_gate = keep("w_gate", [P, E])
        m.w1 = keep("w1", [P, E, F])
        m.w2 = keep("w2", [P, E, NF, D])
        m.b1 = keep("b1", [P, E, NF])
        m.b2 = keep("b2", [E, D])
        m.b_pv = keep("b_pv", [P, 1])
        m.b_k = keep("b_k", [P, 1])
        m.b_kv = keep("b_kv", [P, 1])
        m.b_g1 = keep("b_g1", [P, 1])
        m.b_b1 = keep("b_b1", [D // 2, 1])
        m.ln_g = keep("ln_g", [P, 1])
        m.ln_b = keep("ln_b", [P, 1])
        m.ln1_g = keep("ln1_g", [P, 1])
        m.ln1_b = keep("ln1_b", [P, 1])
        m.ln2_g = keep("ln2_g", [P, 1])
        m.ln2_b = keep("ln2_b", [P, 1])
        m.half_bg2 = keep("half_bg2", [P, 1])
        m.half_bb2 = keep("half_bb2", [P, 1])
        m.ffn_bias = keep("ffn_bias", [P, D])
        m.half_bias = keep("half_bias", [P, D])
        m.bo = keep("bo", [P, D])
        m.norm_w = keep("norm_w", [P, 2 * D])
        m.kz = keep("kz", [P, GH, NG, S], BF16)
        m.q_split = keep("q_split", [P, NT, H, HC], BF16)
        m.k_split = keep("k_split", [P, NT, H, HC], BF16)
        m.v_wide = keep("v_wide", [P, NT, H, HC])

        mixer = Signals(nc, ctx, "mx_")
        softmax = Signals(nc, ctx, "sm_")
        experts = Signals(nc, ctx, "ex_")
        linear = Signals(nc, ctx, "li_")
        phase_load(nc, a, m, ctx)
        phase_mixer(nc, m, mixer.run())
        phase_softmax(nc, m, softmax.run(), "s1_")
        phase_experts(nc, m, experts.run(), "e1_")
        phase_linear(nc, m, linear.run())
        phase_softmax(nc, m, softmax.run(), "s2_")
        phase_experts(nc, m, experts.run(), "e2_", out)


def kernel(**inputs):
    import concourse.bacc as bacc
    from concourse.bass_utils import run_bass_kernel_spmd

    nc = bacc.Bacc("TRN2", target_bir_lowering=False, num_devices=1)
    arrays, args = {}, {}
    for name in INS:
        a = np.ascontiguousarray(inputs[name])
        arrays[f"in_{name}"] = a
        args[name] = nc.dram_tensor(f"in_{name}", a.shape, mybir.dt.from_np(a.dtype), kind="ExternalInput").ap()
    out = nc.dram_tensor("out_x", (B, S, D), F32, kind="ExternalOutput").ap()
    macaron_kernel(nc, args, out)
    r = run_bass_kernel_spmd(nc, [arrays], core_ids=[0])
    return r.results[0]["out_x"]
```

```python
from contextlib import ExitStack

import numpy as np

import concourse.bass as bass
from concourse import mybir

F32 = mybir.dt.float32
BF16 = mybir.dt.bfloat16
U32 = mybir.dt.uint32
ALU = mybir.AluOpType
ACT = mybir.ActivationFunctionType
AX = mybir.AxisListType

P = 128
B, S, D = 8, 512, 128
NT = S // P
H, DH = 16, 8
GH = 4
NG = H // GH
E, F = 8, 512
NF = F // P
assert E == B and NF == NT
HC = 32
EPS = 1e-5
EPS_RMS = 1e-8
SCORE_SCALE = float(DH) ** -0.5
RSQRT_D = float(D) ** -0.5
PI = 3.1415925
MAGIC = 12582912.0
TWO_PI_HI = 6.28125
TWO_PI_MID = 0.0019350051879882812
TWO_PI_LO = float(2.0 * np.pi - 6.28125 - 0.0019350051879882812)

INS = ["L0_attn_x", "L0_attn_pos_phases", "L0_attn_Wpv", "L0_attn_bpv", "L0_attn_Wk", "L0_attn_bk",
       "L0_attn_Wkv", "L0_attn_bkv", "L0_attn_Wg1", "L0_attn_bg1", "L0_attn_Wg2", "L0_attn_bg2",
       "L0_attn_Wb1", "L0_attn_bb1", "L0_attn_Wb2", "L0_attn_bb2", "L0_attn_ln_g", "L0_attn_ln_b",
       "L0_attn_Wo", "L0_attn_bo", "L0_ffn_weight", "L0_ffn_alpha", "L0_ffn_bias", "L1_attn_Wq",
       "L1_attn_Wv", "L1_attn_q_norm_w", "L1_attn_v_norm_w", "L1_ffn_ln1_g", "L1_ffn_ln1_b",
       "L1_ffn_ln2_g", "L1_ffn_ln2_b", "L1_ffn_Wq", "L1_ffn_Wk", "L1_ffn_Wv", "L1_ffn_Wo",
       "L1_ffn_Wg", "L1_ffn_W1", "L1_ffn_b1", "L1_ffn_W2", "L1_ffn_b2"]


class Signal:

    def __init__(self, sem, each):
        self.sem, self.each, self.before = sem, each, 0

    def at(self, b, n=None):
        n = self.each if n is None else n
        return (b if self.each == 1 else b * self.each) + (self.before + n)


class Turn:

    def __init__(self, step, k):
        self.step, self.sem, self.k = step, step.sem, k

    def at(self, b):
        return self.step.at(b, self.k)


class Signals:

    def __init__(self, nc, ctx, prefix):
        self.nc, self.ctx, self.prefix, self.found, self.runs = nc, ctx, prefix, {}, 0

    def run(self):
        for s in self.found.values():
            s.before = self.runs * B * s.each
        self.runs += 1
        return self

    def __call__(self, name, each=1):
        if name not in self.found:
            self.found[name] = Signal(self.ctx.enter_context(self.nc.semaphore(self.prefix + name)), each)
        return self.found[name]


class Memory:
    pass


def tile3(ap, n=NT):
    return ap.rearrange("p (t f) -> p t f", t=n)


def wide(ap, n):
    return ap.unsqueeze(2).to_broadcast([ap.shape[0], ap.shape[1], n])


def again(ap, n):
    return ap.unsqueeze(1).to_broadcast([ap.shape[0], n, ap.shape[1]])


def fence(dve, m):
    dve.memset(m.fence[:, :], 0.0)


def layer_stats(dve, m, src, st, mv, stats_done, mv_done, b):
    fence(dve, m)
    for i in range(NT):
        nc_stats = dve.bn_stats(st[:, i, :], src[:, i, :])
    nc_stats.then_inc(stats_done.sem, 1)
    dve.wait_ge(stats_done.sem, stats_done.at(b))
    fence(dve, m)
    for i in range(NT):
        agg = dve.bn_aggr(mv[:, i, :], st[:, i, :])
    agg.then_inc(mv_done.sem, 1)


def normalise(dve, dst, src, mv, rstd):
    for i in range(NT):
        last = dve.tensor_scalar(dst[:, i, :], src[:, i, :], mv[:, i, 0:1], rstd[:, i:i + 1],
                                 ALU.subtract, ALU.mult)
    return last


def transpose_tiles(pe, out, src, ident, n=NT):
    for i in range(n):
        last = pe.transpose(out[:, i * P:(i + 1) * P], src[:, i, :], ident)
    return last


def phase_load(nc, a, m, keep_ctx):
    with ExitStack() as ctx:
        def sb(name, shape, dt):
            return ctx.enter_context(nc.sbuf_tensor(name, shape, dt))

        def sem(name):
            return keep_ctx.enter_context(nc.semaphore(name))

        bank = [ctx.enter_context(nc.psum_tensor(f"ld_bank{i}", [P, 512], F32)) for i in range(8)]
        w_raw = sb("w_raw", [P, D], F32)
        w_abs = sb("w_abs", [P, D], F32)
        w_row = sb("w_row", [P, 1], F32)
        w_pos = sb("w_pos", [P, D], F32)
        w_neg = sb("w_neg", [P, D], F32)
        mean_w = sb("mean_w", [P, P], F32)
        delta = sb("delta", [P, 2], F32)
        alpha = sb("alpha", [P, 1], F32)
        phases = sb("phases", [P, NT, D], F32)
        turns = sb("turns", [P, S], F32)
        arg_sin = sb("arg_sin", [P, S], F32)
        arg_cos = sb("arg_cos", [P, S], F32)
        wrap = sb("wrap", [P, S], F32)
        lin_raw = sb("lin_raw", [P, 2, D], F32)
        wg2 = sb("wg2", [P, 1], F32)
        wb2 = sb("wb2", [D // 2, 2], F32)
        wb2_diff = sb("wb2_diff", [D // 2, 1], F32)
        bb2 = sb("bb2", [P, 2], F32)
        b1_raw = sb("b1_raw", [E * NF, P], F32)

        loaded = sem("loaded")
        pool_done = sem("ld_pool_done")
        dve_done = sem("ld_dve_done")
        abs_done = sem("abs_done")
        mean_ps = sem("mean_ps")
        phases_ps = sem("phases_ps")
        weff_ps = sem("weff_ps")
        lin_ps = sem("lin_ps")
        sin_args = sem("sin_args")
        tables = sem("tables")

        loads = []

        def load(dst, src):
            loads.append((dst, src))

        def column(dst, src):
            load(dst, src.unsqueeze(1))

        load(w_raw[:, :], a["L0_ffn_weight"])
        load(phases[:, :, :], a["L0_attn_pos_phases"][0:S, :].rearrange("(t p) d -> p t d", p=P))
        load(alpha[:, :], a["L0_ffn_alpha"].partition_broadcast(P))
        load(lin_raw[:, 0, :], a["L1_attn_Wq"])
        load(lin_raw[:, 1, :], a["L1_attn_Wv"])
        load(wg2[:, :], a["L0_attn_Wg2"])
        load(wb2[:, :], a["L0_attn_Wb2"])
        load(bb2[:, :], a["L0_attn_bb2"].partition_broadcast(P))
        load(m.x[:, :, :], a["L0_attn_x"].rearrange("b (t p) d -> p (b t) d", p=P))
        load(m.w_pv[:, :], a["L0_attn_Wpv"])
        load(m.w_k[:, :], a["L0_attn_Wk"])
        load(m.w_kv[:, :], a["L0_attn_Wkv"])
        load(m.w_g1[:, :, :], a["L0_attn_Wg1"].rearrange("(s d) n -> d s n", s=2))
        load(m.w_b1[:, :], a["L0_attn_Wb1"])
        load(m.w_o[:, :], a["L0_attn_Wo"])
        column(m.b_pv[:, :], a["L0_attn_bpv"])
        column(m.b_k[:, :], a["L0_attn_bk"])
        column(m.b_kv[:, :], a["L0_attn_bkv"])
        column(m.b_g1[:, :], a["L0_attn_bg1"])
        column(m.b_b1[:, :], a["L0_attn_bb1"])
        column(m.ln_g[:, :], a["L0_attn_ln_g"])
        column(m.ln_b[:, :], a["L0_attn_ln_b"])
        column(m.ln1_g[:, :], a["L1_ffn_ln1_g"])
        column(m.ln1_b[:, :], a["L1_ffn_ln1_b"])
        column(m.ln2_g[:, :], a["L1_ffn_ln2_g"])
        column(m.ln2_b[:, :], a["L1_ffn_ln2_b"])
        load(m.half_bg2[:, :], a["L0_attn_bg2"].partition_broadcast(P))
        load(m.ffn_bias[:, :], a["L0_ffn_bias"].partition_broadcast(P))
        load(m.bo[:, :], a["L0_attn_bo"].partition_broadcast(P))
        load(m.norm_w[:, 0:D], a["L1_attn_q_norm_w"].rearrange("h d -> (h d)").partition_broadcast(P))
        load(m.norm_w[:, D:2 * D], a["L1_attn_v_norm_w"].rearrange("h d -> (h d)").partition_broadcast(P))
        load(m.w_qkv[:, 0:D], a["L1_ffn_Wq"])
        load(m.w_qkv[:, D:2 * D], a["L1_ffn_Wk"])
        load(m.w_qkv[:, 2 * D:3 * D], a["L1_ffn_Wv"])
        load(m.w_out[:, :], a["L1_ffn_Wo"])
        load(m.w_gate[:, :], a["L1_ffn_Wg"])
        load(b1_raw[:, :], a["L1_ffn_b1"].rearrange("e (c p) -> (e c) p", p=P))
        load(m.b2[:, :], a["L1_ffn_b2"])

        block = ctx.enter_context(nc.Block())

        @block.sync
        def _(sp):
            for dst, src in loads:
                sp.dma_start(dst, src).then_inc(loaded, 16)
            sp.wait_ge(loaded, 16 * len(loads))

        @block.gpsimd
        def _(pool):
            pool.memset(m.ident[:, :], 0.0).then_inc(pool_done, 1)
            pool.wait_ge(pool_done, 1)
            pool.affine_select(out=m.ident[:, :], in_=m.ident[:, :], compare_op=ALU.not_equal, fill=1.0,
                               base=0, pattern=[[-1, P]], channel_multiplier=1).then_inc(pool_done, 1)
            pool.wait_ge(pool_done, 2)
            pool.tensor_copy(m.ident_bf[:, :], m.ident[:, :]).then_inc(pool_done, 1)
            pool.memset(m.causal[:, :], 1.0).then_inc(pool_done, 1)
            pool.wait_ge(pool_done, 4)
            pool.affine_select(out=m.causal[:, :], in_=m.causal[:, :], compare_op=ALU.is_ge, fill=0.0,
                               base=0, pattern=[[1, P]], channel_multiplier=-1).then_inc(pool_done, 1)
            pool.iota(m.expert_id[:, :], pattern=[[1, E]], base=0, channel_multiplier=0,
                      allow_small_or_imprecise_dtypes=True).then_inc(pool_done, 1)
            pool.memset(mean_w[:, :], 0.7 / (D * D)).then_inc(pool_done, 1)
            pool.memset(m.half_pow[:, :, :], -0.5).then_inc(pool_done, 1)
            pool.memset(m.eps[:, :], EPS).then_inc(pool_done, 1)
            pool.memset(m.zero_bf[:, :], 0.0).then_inc(pool_done, 1)
            pool.memset(m.u_t[:, 0:1], 0.0).then_inc(pool_done, 1)
            pool.memset(m.key_cos[:, 0:1], 0.0).then_inc(pool_done, 1)
            pool.memset(m.key_sin[:, 0:1], 0.0).then_inc(pool_done, 1)
            pool.memset(m.half_pi[:, :], float(np.pi / 2)).then_inc(pool_done, 1)

        @block.vector
        def _(dve):
            count = [0]

            def then(ins):
                count[0] += 1
                ins.then_inc(dve_done, 1)
                dve.wait_ge(dve_done, count[0])

            then(dve.memset(m.zeros[:, :], 0.0))
            then(dve.memset(m.ones[:, :], 1.0))
            for p in range(2):
                dve.memset(m.kz[:, p, :, :, :], 0.0)
                dve.memset(m.q_split[:, p, :, :, :], 0.0)
                dve.memset(m.v_wide[:, p, :, :, :], 0.0)
            then(dve.memset(m.k_split[:, :, :, :], 0.0))
            then(dve.memset(m.k_split[:, :, :, 24:26], 1.0))
            for p in range(2):
                then(dve.memset(m.v_wide[:, p, :, :, DH:DH + 1], 1.0))
            dve.wait_ge(loaded, 16 * len(loads))
            dve.wait_ge(mean_ps, 1)
            then(dve.tensor_copy(delta[:, 0:1], bank[0][:, 0:1]))
            then(dve.tensor_scalar(delta[:, 1:2], delta[:, 0:1], -1.0, None, ALU.mult))
            then(dve.tensor_scalar(w_pos[:, :], w_raw[:, :], delta[:, 0:1], None, ALU.is_gt))
            then(dve.tensor_scalar(w_neg[:, :], w_raw[:, :], delta[:, 1:2], None, ALU.is_lt))
            then(dve.tensor_tensor(w_pos[:, :], w_pos[:, :], w_neg[:, :], ALU.subtract))
            then(dve.tensor_scalar(w_raw[:, :], w_pos[:, :], alpha[:, 0:1], None, ALU.mult))
            dve.wait_ge(weff_ps, 1)
            then(dve.tensor_copy(m.w_eff[:, :], bank[1][:, 0:P]))
            dve.wait_ge(lin_ps, 1)
            then(dve.tensor_copy(m.w_lin[:, :], bank[2][:, 0:2 * D]))
            then(dve.tensor_copy(m.b1[:, :, :], bank[2][:, 2 * P:2 * P + E * NF].rearrange("p (e c) -> p e c", e=E)))
            then(dve.tensor_scalar(m.w_g2[:, :], m.ones[:, 0:P], wg2[:, 0:1], None, ALU.mult))
            then(dve.tensor_tensor(wb2_diff[:, :], wb2[:, 0:1], wb2[:, 1:2], ALU.subtract))
            then(dve.tensor_scalar(m.w_b2[:, :], m.ones[0:D // 2, 0:P], wb2_diff[:, 0:1], None, ALU.mult))
            then(dve.tensor_tensor(m.half_bb2[:, :], bb2[:, 0:1], bb2[:, 1:2], ALU.subtract))
            then(dve.tensor_scalar(m.half_bb2[:, :], m.half_bb2[:, :], 0.5, None, ALU.mult))
            then(dve.tensor_scalar(m.half_bg2[:, :], m.half_bg2[:, :], 0.5, None, ALU.mult))
            then(dve.tensor_scalar(m.half_bias[:, :], m.ffn_bias[:, :], 0.5, None, ALU.mult))
            dve.wait_ge(phases_ps, 1)
            for arg, quarter in ((arg_sin, 0.0), (arg_cos, float(np.pi / 2))):
                then(dve.tensor_scalar(turns[:, :], bank[3][:, :], float(1 / (2 * np.pi)), MAGIC,
                                       ALU.mult, ALU.add))
                then(dve.tensor_scalar(turns[:, :], turns[:, :], MAGIC, None, ALU.subtract))
                then(dve.scalar_tensor_tensor(out=arg[:, :], in0=turns[:, :], scalar=-TWO_PI_HI,
                                              in1=bank[3][:, :], op0=ALU.mult, op1=ALU.add))
                then(dve.scalar_tensor_tensor(out=arg[:, :], in0=turns[:, :], scalar=-TWO_PI_MID,
                                              in1=arg[:, :], op0=ALU.mult, op1=ALU.add))
                then(dve.scalar_tensor_tensor(out=arg[:, :], in0=turns[:, :], scalar=-TWO_PI_LO,
                                              in1=arg[:, :], op0=ALU.mult, op1=ALU.add))
                if quarter:
                    then(dve.tensor_scalar(arg[:, :], arg[:, :], quarter, None, ALU.add))
                    then(dve.tensor_scalar(wrap[:, :], arg[:, :], PI, -2 * float(np.pi), ALU.is_gt, ALU.mult))
                    then(dve.tensor_tensor(arg[:, :], arg[:, :], wrap[:, :], ALU.add))
                then(dve.tensor_scalar(arg[:, :], arg[:, :], PI, -PI, ALU.min, ALU.max))
            dve.nop().then_inc(sin_args, 1)

        @block.scalar
        def _(act):
            act.wait_ge(loaded, 16 * len(loads))
            act.activation(w_abs[:, :], w_raw[:, :], ACT.Abs, accum_out=w_row[:, 0:1]).then_inc(abs_done, 1)
            act.wait_ge(sin_args, 1)
            act.activation(m.pos_sin[:, :], arg_sin[:, :], ACT.Sin).then_inc(tables, 1)
            act.activation(m.pos_cos[:, :], arg_cos[:, :], ACT.Sin).then_inc(tables, 1)

        @block.tensor
        def _(pe):
            pe.wait_ge(pool_done, 14)
            pe.wait_ge(abs_done, 1)
            pe.matmul(bank[0][:, 0:1], mean_w[:, :], w_row[:, :], start=True, stop=True).then_inc(mean_ps, 1)
            pe.wait_ge(loaded, 16 * len(loads))
            for i in range(NT):
                last = pe.transpose(bank[3][:, i * P:(i + 1) * P], phases[:, i, :], m.ident[:, :])
            last.then_inc(phases_ps, 1)
            for i in range(2):
                last = pe.transpose(bank[2][:, i * P:(i + 1) * P], lin_raw[:, i, :], m.ident[:, :])
            pe.transpose(bank[2][:, 2 * P:2 * P + E * NF], b1_raw[:, :], m.ident[0:E * NF, 0:E * NF])\
                .then_inc(lin_ps, 1)
            pe.wait_ge(dve_done, 12)
            pe.transpose(bank[1][:, 0:P], w_raw[:, :], m.ident[:, :]).then_inc(weff_ps, 1)


def phase_mixer(nc, a, m, signal):
    with ExitStack() as ctx:
        def sb(name, shape, dt=F32):
            return ctx.enter_context(nc.sbuf_tensor("mx_" + name, shape, dt))

        bank = [ctx.enter_context(nc.psum_tensor(f"mx_bank{i}", [P, 512], F32)) for i in range(8)]
        st = sb("st", [P, NT, 6])
        mv = sb("mv", [P, NT, 2])
        rstd = sb("rstd", [P, NT])
        var = sb("var", [P, NT])
        z = sb("z", [P, NT, D])
        z_t = sb("z_t", [P, S])
        x0 = sb("x0", [P, NT, D])
        x1 = sb("x1", [P, NT, D])
        x2 = sb("x2", [P, NT, D])
        u = sb("u", [P, NT, D])
        xu = sb("xu", [P, NT, D])
        pv = sb("pv", [P, S])
        kt = sb("kt", [P, S])
        kv = sb("kv", [P, S])
        kabs = sb("kabs", [P, S])
        gh = sb("gh", [P, S])
        bh = sb("bh", [D // 2, S])
        gt = sb("gt", [P, S])
        wt = sb("wt", [P, S])
        vg = sb("vg", [P, S])
        gcum = sb("gcum", [1, S])
        c_in = sb("c_in", [P, S])
        s_in = sb("s_in", [P, S])
        c_mem = sb("c_mem", [P, S])
        s_mem = sb("s_mem", [P, S])
        kc_in = sb("kc_in", [P, S])
        ks_in = sb("ks_in", [P, S])
        kc_mem = sb("kc_mem", [P, S])
        ks_mem = sb("ks_mem", [P, S])
        pos = sb("pos", [P, S])
        kvr = sb("kvr", [P, S])
        gm = sb("gm", [P, NT])
        gp = sb("gp", [P, NT])
        w0 = sb("w0", [P, NT])
        w1 = sb("w1", [P, NT])
        w1g = sb("w1g", [P, NT])
        pw = sb("pw", [P, NT, D])
        bl = sb("bl", [P, NT, D])
        w1_raw = sb("w1_raw", [P, 1, F])
        w2_raw = sb("w2_raw", [P, 1, NF, D])

        LN = ("a", "u", "bl", "c")

        def turns(name, keys):
            return {k: Turn(signal(name, len(keys)), i + 1) for i, k in enumerate(keys)}

        stats = turns("stats", LN)
        mv_done = turns("mv", LN)
        var_done = turns("var", LN)
        rstd_done = turns("rstd", LN)
        z_done = turns("z", LN)
        zt_ps = turns("zt_ps", LN)
        zt_done = turns("zt", LN)
        biased = turns("biased", ("a", "c"))
        ffn_ps = turns("ffn_ps", ("a", "c"))
        x1_done = signal("x1")
        x3_done = signal("x3")
        proj_ps = signal("proj_ps", 5)
        gh_done = signal("gh", 2)
        gate_ps = signal("gate_ps", 2)
        gt_done = signal("gt", 2)
        kt_done = signal("kt")
        pv_done = signal("pv")
        kv_done = signal("kv")
        kabs_done = signal("kabs")
        key_done = signal("key", 2)
        vg_done = signal("vg")
        pos_in = signal("pos_in", 2)
        pos_mem = signal("pos_mem", 2)
        pos_mul = signal("pos_mul", 2)
        pos_done = signal("pos")
        gcum_done = signal("gcum")
        kvg_done = signal("kvg")
        key_in = signal("key_in", 2)
        key_mem = signal("key_mem", 2)
        key_mul = signal("key_mul", 2)
        kvr_done = signal("kvr")
        scal_ps = signal("scal_ps")
        scal_done = signal("scal", 3)
        gp_done = signal("gp")
        w1g_done = signal("w1g")
        ret_ps = signal("ret_ps", 2)
        pw_done = signal("pw")
        bl_done = signal("bl_sum")
        out_ps = signal("out_ps")
        xu_done = signal("xu")
        xub_done = signal("xub")
        x2_done = signal("x2")
        w_loaded = signal("w_loaded", 32)
        w_hi_done = signal("w_hi", 2)
        w_lo_done = signal("w_lo", 2)
        block = ctx.enter_context(nc.Block())

        def ln_pool(pool, k, b):
            pool.wait_ge(mv_done[k].sem, mv_done[k].at(b))
            pool.tensor_tensor(var[:, :], mv[:, :, 1], m.eps[:, :], ALU.add).then_inc(var_done[k].sem, 1)
            pool.wait_ge(var_done[k].sem, var_done[k].at(b))
            pool.tensor_tensor(rstd[:, :], var[:, :], m.half_pow[:, 0, :], ALU.pow).then_inc(rstd_done[k].sem, 1)

        @block.sync
        def _(sp):
            def load_expert(b):
                sp.dma_start(w1_raw[:, :, :], a["L1_ffn_W1"][bass.ds(b, 1), :, :].rearrange("e d f -> d e f"))\
                    .then_inc(w_loaded.sem, 16)
                sp.dma_start(w2_raw[:, :, :, :],
                             a["L1_ffn_W2"][bass.ds(b, 1), :, :].rearrange("e (c p) d -> p e c d", p=P))\
                    .then_inc(w_loaded.sem, 16)

            load_expert(0)
            with sp.Fori(1, E) as b:
                sp.wait_ge(w_lo_done.sem, w_lo_done.at(b, 0))
                load_expert(b)

        @block.gpsimd
        def _(pool):
            with pool.Fori(0, B) as b:
                x_b = m.x[:, bass.ds(b * NT, NT), :]
                ln_pool(pool, "a", b)
                pool.tensor_tensor(x0[:, :, :], x_b, again(m.half_bias[:, :], NT), ALU.add)\
                    .then_inc(biased["a"].sem, 1)
                ln_pool(pool, "u", b)
                pool.wait_ge(z_done["u"].sem, z_done["u"].at(b))
                pool.tensor_tensor(xu[:, :, :], x1[:, :, :], u[:, :, :], ALU.add).then_inc(xu_done.sem, 1)
                pool.wait_ge(xu_done.sem, xu_done.at(b))
                pool.tensor_tensor(xu[:, :, :], xu[:, :, :], again(m.bo[:, :], NT), ALU.add)\
                    .then_inc(xub_done.sem, 1)
                pool.wait_ge(scal_done.sem, scal_done.at(b))
                pool.tensor_tensor(gp[:, :], gm[:, :], m.half_pow[:, 0, :], ALU.pow).then_inc(gp_done.sem, 1)
                pool.wait_ge(gp_done.sem, gp_done.at(b))
                pool.tensor_tensor(w1g[:, :], w1[:, :], gp[:, :], ALU.mult).then_inc(w1g_done.sem, 1)
                ln_pool(pool, "bl", b)
                ln_pool(pool, "c", b)
                pool.wait_ge(x2_done.sem, x2_done.at(b))
                pool.tensor_tensor(x0[:, :, :], x2[:, :, :], again(m.half_bias[:, :], NT), ALU.add)\
                    .then_inc(biased["c"].sem, 1)
                w1_full = w1_raw[:, :, :].rearrange("p e (c d) -> p (e c) d", d=D)
                w2_full = w2_raw[:, :, :, :].rearrange("p e c d -> p (e c) d")
                parts = [w[:, bass.ds(b, 1), :].rearrange("p e (c d) -> p (e c) d", d=D)
                         for w in (m.w1_hi, m.w1_lo, m.w2_hi, m.w2_lo)]
                pool.wait_ge(w_loaded.sem, w_loaded.at(b))
                pool.tensor_tensor(parts[0], w1_full, again(m.zero_bf[:, :], NF), ALU.add).then_inc(w_hi_done.sem, 1)
                pool.tensor_tensor(parts[2], w2_full, again(m.zero_bf[:, :], NF), ALU.add).then_inc(w_hi_done.sem, 1)
                pool.wait_ge(w_hi_done.sem, w_hi_done.at(b))
                pool.tensor_tensor(parts[1], w1_full, parts[0], ALU.subtract).then_inc(w_lo_done.sem, 1)
                pool.tensor_tensor(parts[3], w2_full, parts[2], ALU.subtract).then_inc(w_lo_done.sem, 1)

        @block.vector
        def _(dve):
            with dve.Fori(0, B) as b:
                x_b = m.x[:, bass.ds(b * NT, NT), :]

                def ln(k, src, dst):
                    layer_stats(dve, m, src, st, mv, stats[k], mv_done[k], b)
                    dve.wait_ge(rstd_done[k].sem, rstd_done[k].at(b))
                    normalise(dve, dst, src, mv, rstd).then_inc(z_done[k].sem, 1)

                ln("a", x_b, z)
                dve.wait_ge(ffn_ps["a"].sem, ffn_ps["a"].at(b))
                dve.wait_ge(biased["a"].sem, biased["a"].at(b))
                dve.scalar_tensor_tensor(out=x1[:, :, :], in0=tile3(bank[1][:, :]), scalar=0.5,
                                         in1=x0[:, :, :], op0=ALU.mult, op1=ALU.add).then_inc(x1_done.sem, 1)
                dve.wait_ge(x1_done.sem, x1_done.at(b))
                ln("u", x1, u)
                dve.wait_ge(pv_done.sem, pv_done.at(b))
                dve.tensor_tensor(c_in[:, :], pv[:, :], m.pos_cos[:, :], ALU.mult).then_inc(pos_in.sem, 1)
                dve.tensor_tensor(s_in[:, :], pv[:, :], m.pos_sin[:, :], ALU.mult).then_inc(pos_in.sem, 1)
                dve.wait_ge(pos_in.sem, pos_in.at(b))
                dve.tensor_tensor_scan(c_mem[:, :], m.zeros[:, :], c_in[:, :], 0.0, ALU.add, ALU.add)\
                    .then_inc(pos_mem.sem, 1)
                dve.tensor_tensor_scan(s_mem[:, :], m.zeros[:, :], s_in[:, :], 0.0, ALU.add, ALU.add)\
                    .then_inc(pos_mem.sem, 1)
                dve.wait_ge(pos_mem.sem, pos_mem.at(b))
                dve.tensor_tensor(c_in[:, :], c_mem[:, :], m.pos_cos[:, :], ALU.mult).then_inc(pos_mul.sem, 1)
                dve.tensor_tensor(s_in[:, :], s_mem[:, :], m.pos_sin[:, :], ALU.mult).then_inc(pos_mul.sem, 1)
                dve.wait_ge(pos_mul.sem, pos_mul.at(b))
                dve.tensor_tensor(pos[:, :], c_in[:, :], s_in[:, :], ALU.add).then_inc(pos_done.sem, 1)
                dve.wait_ge(gt_done.sem, gt_done.at(b))
                dve.tensor_scalar(vg[:, :], gt[:, :], 0.5, 0.5, ALU.mult, ALU.add).then_inc(vg_done.sem, 1)
                dve.wait_ge(vg_done.sem, vg_done.at(b))
                dve.tensor_tensor_scan(gcum[:, :], m.zeros[0:1, :], vg[0:1, :], 0.0, ALU.add, ALU.add)\
                    .then_inc(gcum_done.sem, 1)
                dve.wait_ge(kv_done.sem, kv_done.at(b))
                dve.tensor_tensor(kv[:, :], kv[:, :], vg[:, :], ALU.mult).then_inc(kvg_done.sem, 1)
                dve.wait_ge(kvg_done.sem, kvg_done.at(b))
                dve.wait_ge(key_done.sem, key_done.at(b))
                dve.tensor_tensor(kc_in[:, :], kv[:, :], m.key_cos[:, 0:S], ALU.mult).then_inc(key_in.sem, 1)
                dve.tensor_tensor(ks_in[:, :], kv[:, :], m.key_sin[:, 0:S], ALU.mult).then_inc(key_in.sem, 1)
                dve.wait_ge(key_in.sem, key_in.at(b))
                dve.tensor_tensor_scan(kc_mem[:, :], m.zeros[:, :], kc_in[:, :], 0.0, ALU.add, ALU.add)\
                    .then_inc(key_mem.sem, 1)
                dve.tensor_tensor_scan(ks_mem[:, :], m.zeros[:, :], ks_in[:, :], 0.0, ALU.add, ALU.add)\
                    .then_inc(key_mem.sem, 1)
                dve.wait_ge(key_mem.sem, key_mem.at(b))
                dve.tensor_tensor(kc_in[:, :], kc_mem[:, :], m.key_cos[:, 1:S + 1], ALU.mult)\
                    .then_inc(key_mul.sem, 1)
                dve.tensor_tensor(ks_in[:, :], ks_mem[:, :], m.key_sin[:, 1:S + 1], ALU.mult)\
                    .then_inc(key_mul.sem, 1)
                dve.wait_ge(key_mul.sem, key_mul.at(b))
                dve.tensor_tensor(kvr[:, :], kc_in[:, :], ks_in[:, :], ALU.add).then_inc(kvr_done.sem, 1)
                dve.wait_ge(scal_ps.sem, scal_ps.at(b))
                dve.tensor_scalar(gm[:, :], bank[0][:, 0:NT], 1.0, None, ALU.max).then_inc(scal_done.sem, 1)
                dve.tensor_scalar(w0[:, :], bank[0][:, NT:2 * NT], 0.5 * RSQRT_D, 0.5 * RSQRT_D,
                                  ALU.mult, ALU.add).then_inc(scal_done.sem, 1)
                dve.tensor_scalar(w1[:, :], bank[0][:, NT:2 * NT], -0.5 * RSQRT_D, 0.5 * RSQRT_D,
                                  ALU.mult, ALU.add).then_inc(scal_done.sem, 1)
                dve.wait_ge(pw_done.sem, pw_done.at(b))
                dve.wait_ge(w1g_done.sem, w1g_done.at(b))
                dve.wait_ge(ret_ps.sem, ret_ps.at(b))
                for i in range(NT):
                    last = dve.scalar_tensor_tensor(out=bl[:, i, :], in0=bank[3][:, i * P:(i + 1) * P],
                                                    scalar=w1g[:, i:i + 1], in1=pw[:, i, :],
                                                    op0=ALU.mult, op1=ALU.add)
                last.then_inc(bl_done.sem, 1)
                dve.wait_ge(bl_done.sem, bl_done.at(b))
                ln("bl", bl, z)
                dve.wait_ge(out_ps.sem, out_ps.at(b))
                dve.wait_ge(xub_done.sem, xub_done.at(b))
                dve.tensor_tensor(x2[:, :, :], tile3(bank[5][:, :]), xu[:, :, :], ALU.add).then_inc(x2_done.sem, 1)
                dve.wait_ge(x2_done.sem, x2_done.at(b))
                ln("c", x2, z)
                dve.wait_ge(ffn_ps["c"].sem, ffn_ps["c"].at(b))
                dve.wait_ge(biased["c"].sem, biased["c"].at(b))
                dve.scalar_tensor_tensor(out=x_b, in0=tile3(bank[7][:, :]), scalar=0.5, in1=x0[:, :, :],
                                         op0=ALU.mult, op1=ALU.add).then_inc(x3_done.sem, 1)

        @block.scalar
        def _(act):
            with act.Fori(0, B) as b:
                act.wait_ge(zt_ps["a"].sem, zt_ps["a"].at(b))
                act.activation(z_t[:, :], bank[0][:, :], ACT.Copy).then_inc(zt_done["a"].sem, 1)
                act.wait_ge(zt_ps["u"].sem, zt_ps["u"].at(b))
                act.activation(m.u_t[:, 1:S + 1], bank[0][:, :], ACT.Copy).then_inc(zt_done["u"].sem, 1)
                act.wait_ge(proj_ps.sem, proj_ps.at(b, 1))
                act.activation(gh[:, :], bank[5][:, :], ACT.Gelu, bias=m.b_g1[:, 0:1]).then_inc(gh_done.sem, 1)
                act.wait_ge(proj_ps.sem, proj_ps.at(b, 2))
                act.activation(bh[:, :], bank[6][0:D // 2, :], ACT.Gelu, bias=m.b_b1[:, 0:1])\
                    .then_inc(gh_done.sem, 1)
                act.wait_ge(proj_ps.sem, proj_ps.at(b, 4))
                act.activation(pv[:, :], bank[2][:, :], ACT.Identity, bias=m.b_pv[:, 0:1]).then_inc(pv_done.sem, 1)
                act.wait_ge(proj_ps.sem, proj_ps.at(b, 5))
                act.activation(kv[:, :], bank[4][:, :], ACT.Identity, bias=m.b_kv[:, 0:1]).then_inc(kv_done.sem, 1)
                act.wait_ge(gate_ps.sem, gate_ps.at(b, 1))
                act.activation(gt[:, :], bank[7][:, :], ACT.Tanh, bias=m.half_bg2[:, 0:1], scale=0.5)\
                    .then_inc(gt_done.sem, 1)
                act.wait_ge(gate_ps.sem, gate_ps.at(b, 2))
                act.activation(wt[:, :], bank[1][:, :], ACT.Tanh, bias=m.half_bb2[:, 0:1], scale=0.5)\
                    .then_inc(gt_done.sem, 1)
                act.activation(kt[:, :], bank[3][:, :], ACT.Tanh, bias=m.b_k[:, 0:1]).then_inc(kt_done.sem, 1)
                act.wait_ge(kt_done.sem, kt_done.at(b))
                act.activation(kabs[:, :], kt[:, :], ACT.Abs).then_inc(kabs_done.sem, 1)
                act.activation(m.key_sin[:, 1:S + 1], kt[:, :], ACT.Sin, scale=PI).then_inc(key_done.sem, 1)
                act.wait_ge(kabs_done.sem, kabs_done.at(b))
                act.activation(m.key_cos[:, 1:S + 1], kabs[:, :], ACT.Sin, bias=m.half_pi[:, 0:1], scale=-PI)\
                    .then_inc(key_done.sem, 1)
                act.wait_ge(ret_ps.sem, ret_ps.at(b, 1))
                act.wait_ge(scal_done.sem, scal_done.at(b))
                for i in range(NT):
                    last = act.activation(pw[:, i, :], bank[2][:, i * P:(i + 1) * P], ACT.Copy, scale=w0[:, i:i + 1])
                last.then_inc(pw_done.sem, 1)
                act.wait_ge(zt_ps["bl"].sem, zt_ps["bl"].at(b))
                act.activation(z_t[:, :], bank[4][:, :], ACT.Identity, bias=m.ln_b[:, 0:1],
                               scale=m.ln_g[:, 0:1]).then_inc(zt_done["bl"].sem, 1)
                act.wait_ge(zt_ps["c"].sem, zt_ps["c"].at(b))
                act.activation(z_t[:, :], bank[6][:, :], ACT.Copy).then_inc(zt_done["c"].sem, 1)

        @block.tensor
        def _(pe):
            def ffn(k, out, b):
                pe.wait_ge(zt_done[k].sem, zt_done[k].at(b))
                for i in range(NT):
                    last = pe.matmul(out[:, i * P:(i + 1) * P], z_t[:, i * P:(i + 1) * P], m.w_eff[:, :],
                                     start=True, stop=True)
                last.then_inc(ffn_ps[k].sem, 1)

            with pe.Fori(0, B) as b:
                pe.wait_ge(z_done["a"].sem, z_done["a"].at(b))
                transpose_tiles(pe, bank[0], z, m.ident[:, :]).then_inc(zt_ps["a"].sem, 1)
                ffn("a", bank[1], b)
                pe.wait_ge(z_done["u"].sem, z_done["u"].at(b))
                transpose_tiles(pe, bank[0], u, m.ident[:, :]).then_inc(zt_ps["u"].sem, 1)
                pe.wait_ge(zt_done["u"].sem, zt_done["u"].at(b))
                cur, shifted = m.u_t[:, 1:S + 1], m.u_t[:, 0:S]
                pe.matmul(bank[5][:, :], m.w_g1[:, 0, :], cur, start=True, stop=False)
                pe.matmul(bank[5][:, :], m.w_g1[:, 1, :], shifted, start=False, stop=True).then_inc(proj_ps.sem, 1)
                pe.matmul(bank[6][0:D // 2, :], m.w_b1[:, :], cur, start=True, stop=True).then_inc(proj_ps.sem, 1)
                pe.matmul(bank[3][:, :], m.w_k[:, :], cur, start=True, stop=True).then_inc(proj_ps.sem, 1)
                pe.matmul(bank[2][:, :], m.w_pv[:, :], cur, start=True, stop=True).then_inc(proj_ps.sem, 1)
                pe.matmul(bank[4][:, :], m.w_kv[:, :], cur, start=True, stop=True).then_inc(proj_ps.sem, 1)
                pe.wait_ge(gh_done.sem, gh_done.at(b, 1))
                pe.matmul(bank[7][:, :], m.w_g2[:, :], gh[:, :], start=True, stop=True).then_inc(gate_ps.sem, 1)
                pe.wait_ge(gh_done.sem, gh_done.at(b, 2))
                pe.wait_ge(x1_done.sem, x1_done.at(b))
                pe.matmul(bank[1][:, :], m.w_b2[:, :], bh[:, :], start=True, stop=True).then_inc(gate_ps.sem, 1)
                pe.wait_ge(pos_done.sem, pos_done.at(b))
                transpose_tiles(pe, bank[2], tile3(pos[:, :]), m.ident[:, :]).then_inc(ret_ps.sem, 1)
                pe.wait_ge(gcum_done.sem, gcum_done.at(b))
                pe.wait_ge(gt_done.sem, gt_done.at(b))
                for i in range(NT):
                    pe.matmul(bank[0][:, i:i + 1], gcum[0:1, i * P:(i + 1) * P], m.ones[0:1, 0:1],
                              start=True, stop=True)
                for i in range(NT):
                    last = pe.matmul(bank[0][:, NT + i:NT + i + 1], wt[0:1, i * P:(i + 1) * P],
                                     m.ones[0:1, 0:1], start=True, stop=True)
                last.then_inc(scal_ps.sem, 1)
                pe.wait_ge(kvr_done.sem, kvr_done.at(b))
                transpose_tiles(pe, bank[3], tile3(kvr[:, :]), m.ident[:, :]).then_inc(ret_ps.sem, 1)
                pe.wait_ge(z_done["bl"].sem, z_done["bl"].at(b))
                transpose_tiles(pe, bank[4], z, m.ident[:, :]).then_inc(zt_ps["bl"].sem, 1)
                pe.wait_ge(zt_done["bl"].sem, zt_done["bl"].at(b))
                for i in range(NT):
                    last = pe.matmul(bank[5][:, i * P:(i + 1) * P], z_t[:, i * P:(i + 1) * P], m.w_o[:, :],
                                     start=True, stop=True)
                last.then_inc(out_ps.sem, 1)
                pe.wait_ge(z_done["c"].sem, z_done["c"].at(b))
                transpose_tiles(pe, bank[6], z, m.ident[:, :]).then_inc(zt_ps["c"].sem, 1)
                ffn("c", bank[7], b)


def phase_softmax(nc, m, signal, tag):
    STEPS = NG * 16
    SHIFT_LAG = 7
    VALUE_LAG = (14, 17, 21, 24)
    TAKE, TURN, DIVIDE = 25, 26, 28
    with ExitStack() as ctx:
        def sb(name, shape, dt=F32):
            return ctx.enter_context(nc.sbuf_tensor(tag + name, shape, dt))

        raw = [ctx.enter_context(nc.psum_tensor(f"{tag}raw{i}", [P, 512], F32)) for i in range(3)]
        low = [ctx.enter_context(nc.psum_tensor(f"{tag}low{i}", [P, 512], F32)) for i in range(3)]
        av = ctx.enter_context(nc.psum_tensor(tag + "av", [P, 512], F32))
        misc = ctx.enter_context(nc.psum_tensor(tag + "misc", [P, 512], F32))
        misc_bf = misc[:, :].bitcast(BF16)
        st = sb("st", [P, NT, 6])
        mv = sb("mv", [P, NT, 2])
        va = sb("va", [P, 2, NT])
        rs = sb("rs", [P, 2, NT])
        st2 = sb("st2", [P, NT, 6])
        mv2 = sb("mv2", [P, NT, 2])
        va2 = sb("va2", [P, NT])
        rs2 = sb("rs2", [P, NT])
        z = sb("z", [P, NT, D])
        z2 = sb("z2", [P, NT, D])
        h_t = sb("h_t", [P, S])
        k_t = sb("k_t", [P, NG, S], BF16)
        q1 = sb("q1", [P, 2, NG, S], BF16)
        q2 = sb("q2", [P, 2, S], BF16)
        mx = sb("mx", [P, NT, H])
        prob = sb("prob", [P, 8, S])
        av_s = sb("av_s", [P, S])
        rec = sb("rec", [P, NT, GH])
        ctx_s = sb("ctx_s", [P, NT, D])
        ctx_t = sb("ctx_t", [P, S])

        stats = signal("stats")
        mv_done = signal("mv_done")
        var_done = signal("var_done")
        rstd_done = signal("rstd_done")
        y_done = signal("y_done")
        z_done = signal("z_done")
        ht_ps = signal("ht_ps")
        ht_done = signal("ht_done")
        qkv_ps = signal("qkv_ps", NT)
        hi_done = signal("hi_done", NT)
        copy_done = signal("copy_done", NT)
        m_zero = signal("m_zero")
        lo_done = signal("lo_done", NT)
        v_done = signal("v_done", NT)
        kt_ps = signal("kt_ps", 2)
        kt_done = signal("kt_done", 2)
        q1_ps = signal("q1_ps", 2)
        q1_done = signal("q1_done", 2)
        kz_done = signal("kz_done", 16 * GH)
        s1_ps = signal("s1_ps", STEPS)
        max_done = signal("max_done", STEPS)
        mh_done = signal("mh_done", NG)
        ml_done = signal("ml_done", NG)
        q2_ps = signal("q2_ps", NG)
        q2_done = signal("q2_done", NG)
        s2_ps = signal("s2_ps", STEPS)
        exp_done = signal("exp_done", STEPS)
        av_part = signal("av_part", NG * NT)
        avs_done = signal("avs_done", NG)
        avt_ps = signal("avt_ps", NG)
        rec_done = signal("rec_done", NG)
        ctx_done = signal("ctx_done", NG)
        ct_ps = signal("ct_ps")
        ct_done = signal("ct_done")
        wo_ps = signal("wo_ps")
        y2_done = signal("y2_done")
        stats2 = signal("stats2")
        mv2_done = signal("mv2_done")
        var2_done = signal("var2_done")
        rstd2_done = signal("rstd2_done")
        z2_done = signal("z2_done")
        mt_ps = signal("mt_ps")
        mt_done = signal("mt_done")
        block = ctx.enter_context(nc.Block())

        def batches(eng, head, body, last):
            head()
            body(0, 0, False, True)
            with eng.Fori(0, (B - 2) // 2) as i:
                body(i * 2 + 1, 1, True, True)
                body(i * 2 + 2, 0, True, True)
            body(B - 1, 1, True, False)
            last()

        @block.sync
        def _(sp):
            def spread(b, p):
                sp.wait_ge(kt_done.sem, kt_done.at(b))
                for j in range(GH):
                    rows = slice(HC * j, HC * (j + 1))
                    sp.dma_start(m.kz[rows, p, j, :, :], k_t[rows, :, :]).then_inc(kz_done.sem, 16)

            spread(0, 0)
            with sp.Fori(0, (B - 2) // 2) as i:
                spread(i * 2 + 1, 1)
                spread(i * 2 + 2, 0)
            spread(B - 1, 1)
            sp.wait_ge(kz_done.sem, kz_done.at(B - 1))

        @block.gpsimd
        def _(pool):
            def norm(b):
                pool.wait_ge(var_done.sem, var_done.at(b))
                pool.tensor_tensor(rs[:, :, :], va[:, :, :], m.half_pow[:, :, :], ALU.pow)\
                    .then_inc(rstd_done.sem, 1)

            def copies(b, p):
                for i in range(NT):
                    pool.wait_ge(hi_done.sem, hi_done.at(b, i + 1))
                    pool.tensor_tensor(m.q_split[:, p, i, :, 16:24], m.q_split[:, p, i, :, 0:8],
                                       m.zero_bf[:, :].rearrange("p (h d) -> p h d", d=DH), ALU.add)
                    pool.tensor_copy(m.k_split[:, i, :, 8:16], m.k_split[:, i, :, 0:8]).then_inc(copy_done.sem, 1)

            def head():
                norm(0)
                copies(0, 0)

            def norm2(b):
                pool.wait_ge(var2_done.sem, var2_done.at(b))
                pool.tensor_tensor(rs2[:, :], va2[:, :], m.half_pow[:, 0, :], ALU.pow).then_inc(rstd2_done.sem, 1)

            def body(b, p, before, behind):
                if behind:
                    norm(b + 1)
                    copies(b + 1, 1 - p)
                if before:
                    norm2(b - 1)

            batches(pool, head, body, lambda: norm2(B - 1))

        @block.vector
        def _(dve):
            def rows(store, b):
                return store[:, bass.ds(b * NT, NT), :]

            def stats_x(b):
                layer_stats(dve, m, rows(m.x, b), st, mv, stats, mv_done, b)
                dve.wait_ge(mv_done.sem, mv_done.at(b))
                dve.tensor_scalar(va[:, 0, :], mv[:, :, 1], EPS, None, ALU.add)
                dve.tensor_scalar(va[:, 1, :], mv[:, :, 1], 1.0 + EPS, EPS * EPS, ALU.mult, ALU.add)\
                    .then_inc(var_done.sem, 1)

            def norm_x(b):
                dve.wait_ge(rstd_done.sem, rstd_done.at(b))
                normalise(dve, z, rows(m.x, b), mv, rs[:, 1, :]).then_inc(z_done.sem, 1)
                normalise(dve, rows(m.y, b), rows(m.x, b), mv, rs[:, 0, :]).then_inc(y_done.sem, 1)

            def clear_max(b, p):
                dve.memset(m.q_split[:, p, :, :, 24:26], 0.0).then_inc(m_zero.sem, 1)

            def low_parts(b, p, i):
                dve.wait_ge(hi_done.sem, hi_done.at(b, i + 1))
                heads = lambda lo: misc[:, lo:lo + D].rearrange("p (h d) -> p h d", d=DH)
                dve.scalar_tensor_tensor(out=m.q_split[:, p, i, :, 8:16], in0=heads(0), scalar=SCORE_SCALE,
                                         in1=m.q_split[:, p, i, :, 0:8], op0=ALU.mult, op1=ALU.subtract)
                dve.tensor_tensor(m.k_split[:, i, :, 16:24], heads(D), m.k_split[:, i, :, 0:8],
                                  ALU.subtract).then_inc(lo_done.sem, 1)
                dve.tensor_copy(m.v_wide[:, p, i, :, 0:DH], heads(2 * D)).then_inc(v_done.sem, 1)

            def row_max(b, n):
                g, n = n // 16, n % 16
                dve.wait_ge(s1_ps.sem, s1_ps.at(b, 16 * g + n + 1))
                h = GH * g + n % GH
                dve.tensor_reduce(mx[:, n // GH, h:h + 1], raw[(16 * g + n) % 3][:, :], AX.X, ALU.max)\
                    .then_inc(max_done.sem, 1)

            def write_max(b, p, g):
                dve.wait_ge(max_done.sem, max_done.at(b, 16 * (g + 1)))
                dve.wait_ge(q1_ps.sem, q1_ps.at(b))
                heads = slice(GH * g, GH * (g + 1))
                dve.tensor_scalar(m.q_split[:, p, :, heads, 24], mx[:, :, heads], -1.0, None, ALU.mult)\
                    .then_inc(mh_done.sem, 1)
                dve.wait_ge(mh_done.sem, mh_done.at(b, g + 1))
                dve.scalar_tensor_tensor(out=m.q_split[:, p, :, heads, 25], in0=mx[:, :, heads], scalar=-1.0,
                                         in1=m.q_split[:, p, :, heads, 24], op0=ALU.mult, op1=ALU.subtract)\
                    .then_inc(ml_done.sem, 1)

            def divide(b, g, before):
                dve.wait_ge(avt_ps.sem, avt_ps.at(b, g + 1))
                t = av[:, :].rearrange("p (t h c) -> p t h c", t=NT, c=HC)
                dve.reciprocal(rec[:, :, :], t[:, :, :, DH]).then_inc(rec_done.sem, 1)
                dve.wait_ge(rec_done.sem, rec_done.at(b, g + 1))
                if g == 0 and before:
                    dve.wait_ge(ct_ps.sem, ct_ps.at(b - 1))
                dve.tensor_tensor(ctx_s[:, :, 32 * g:32 * (g + 1)].rearrange("p t (h d) -> p t h d", d=DH),
                                  t[:, :, :, 0:DH], rec[:, :, :].unsqueeze(3).to_broadcast([P, NT, GH, DH]),
                                  ALU.mult).then_inc(ctx_done.sem, 1)

            def add_output(b):
                dve.wait_ge(wo_ps.sem, wo_ps.at(b))
                dve.tensor_tensor(rows(m.y, b), tile3(misc[:, :]), rows(m.y, b), ALU.add)\
                    .then_inc(y2_done.sem, 1)

            def stats_y(b):
                dve.wait_ge(y2_done.sem, y2_done.at(b))
                layer_stats(dve, m, rows(m.y, b), st2, mv2, stats2, mv2_done, b)
                dve.wait_ge(mv2_done.sem, mv2_done.at(b))
                dve.tensor_scalar(va2[:, :], mv2[:, :, 1], EPS, None, ALU.add).then_inc(var2_done.sem, 1)

            def norm_y(b):
                dve.wait_ge(rstd2_done.sem, rstd2_done.at(b))
                normalise(dve, z2, rows(m.y, b), mv2, rs2).then_inc(z2_done.sem, 1)

            def head():
                stats_x(0)
                norm_x(0)
                clear_max(0, 0)
                for i in range(NT):
                    low_parts(0, 0, i)
                for n in range(16):
                    row_max(0, n)
                write_max(0, 0, 0)

            def body(b, p, before, behind):
                for t in range(STEPS):
                    if t < STEPS - 16:
                        row_max(b, t + 16)
                    elif behind:
                        row_max(b + 1, t + 16 - STEPS)
                    if behind:
                        if t == 0:
                            stats_x(b + 1)
                        if t == 4:
                            norm_x(b + 1)
                            clear_max(b + 1, 1 - p)
                        if t in (11, 14, 26, 29):
                            low_parts(b + 1, 1 - p, (11, 14, 26, 29).index(t))
                    if t % 16 == 15 and t < STEPS - 1:
                        write_max(b, p, t // 16 + 1)
                    if t == STEPS - 1 and behind:
                        write_max(b + 1, 1 - p, 0)
                    if t % 16 == DIVIDE % 16 and (t > 16 or before):
                        g = t // 16 - 1
                        divide(b if g >= 0 else b - 1, g % NG, before)
                    if before:
                        if t == 23:
                            add_output(b - 1)
                            stats_y(b - 1)
                        if t == 30:
                            norm_y(b - 1)

            def last():
                divide(B - 1, NG - 1, True)
                add_output(B - 1)
                stats_y(B - 1)
                norm_y(B - 1)

            batches(dve, head, body, last)

        @block.scalar
        def _(act):
            def to_h(b):
                act.wait_ge(ht_ps.sem, ht_ps.at(b))
                act.activation(h_t[:, :], misc[:, :], ACT.Identity, bias=m.ln1_b[:, 0:1],
                               scale=m.ln1_g[:, 0:1]).then_inc(ht_done.sem, 1)

            def high_parts(b, p, i):
                act.wait_ge(qkv_ps.sem, qkv_ps.at(b, i + 1))
                heads = lambda lo: misc[:, lo:lo + D].rearrange("p (h d) -> p h d", d=DH)
                act.activation(m.q_split[:, p, i, :, 0:DH], heads(0), ACT.Copy, scale=SCORE_SCALE)
                act.activation(m.k_split[:, i, :, 0:DH], heads(D), ACT.Copy).then_inc(hi_done.sem, 1)

            def to_kt(b, c):
                act.wait_ge(kt_ps.sem, kt_ps.at(b, c + 1))
                act.activation(k_t[:, 2 * c:2 * c + 2, :], tile3(misc_bf, 2), ACT.Copy).then_inc(kt_done.sem, 1)

            def to_q1(b, p, c):
                act.wait_ge(q1_ps.sem, q1_ps.at(b, c + 1))
                act.activation(q1[:, p, 2 * c:2 * c + 2, :], tile3(misc_bf, 2), ACT.Copy).then_inc(q1_done.sem, 1)

            def to_q2(b, g):
                act.wait_ge(q2_ps.sem, q2_ps.at(b, g + 1))
                act.activation(q2[:, g % 2, :], misc_bf[:, 0:S], ACT.Copy).then_inc(q2_done.sem, 1)

            def exponentials(b, n, first):
                act.wait_ge(s2_ps.sem, s2_ps.at(b, n + 1))
                if n % 4 == 0 and not (first and n < 8):
                    act.wait_ge(av_part.sem, av_part.at(b, (n - 8) // 4 + 1))
                act.activation(prob[:, n % 8, :], low[n % 3][:, :], ACT.Exp).then_inc(exp_done.sem, 1)

            def take_values(b, g):
                act.wait_ge(av_part.sem, av_part.at(b, NT * (g + 1)))
                act.activation(av_s[:, :], av[:, :], ACT.Copy).then_inc(avs_done.sem, 1)

            def to_ctx(b):
                act.wait_ge(ct_ps.sem, ct_ps.at(b))
                act.activation(ctx_t[:, :], misc[:, :], ACT.Copy).then_inc(ct_done.sem, 1)

            def to_m(b):
                act.wait_ge(mt_ps.sem, mt_ps.at(b))
                act.activation(m.m_t[:, bass.ds(b * S, S)], misc[:, :], ACT.Identity, bias=m.ln2_b[:, 0:1],
                               scale=m.ln2_g[:, 0:1]).then_inc(mt_done.sem, 1)

            def head():
                to_h(0)
                for i in range(NT):
                    high_parts(0, 0, i)
                for c in range(2):
                    to_kt(0, c)
                for c in range(2):
                    to_q1(0, 0, c)

            def body(b, p, before, behind):
                for t in range(STEPS):
                    n = t - SHIFT_LAG
                    if n >= 0 or before:
                        exponentials(b if n >= 0 else b - 1, n % STEPS, not before)
                    if t % 16 == TAKE % 16 and (t > 16 or before):
                        g = t // 16 - 1
                        take_values(b if g >= 0 else b - 1, g % NG)
                    if t % 16 == 4:
                        to_q2(b, t // 16)
                    if behind:
                        if t == 8:
                            to_h(b + 1)
                        if t in (11, 14, 26, 29):
                            high_parts(b + 1, 1 - p, (11, 14, 26, 29).index(t))
                        if t in (32, 34):
                            to_kt(b + 1, (t - 32) // 2)
                        if t in (39, 42):
                            to_q1(b + 1, 1 - p, (t - 39) // 3)
                    if before:
                        if t == 17:
                            to_ctx(b - 1)
                        if t == 46:
                            to_m(b - 1)

            def last():
                for n in range(STEPS - SHIFT_LAG, STEPS):
                    exponentials(B - 1, n, False)
                take_values(B - 1, NG - 1)
                to_ctx(B - 1)
                to_m(B - 1)

            batches(act, head, body, last)

        @block.tensor
        def _(pe):
            def h_tiles(b):
                pe.wait_ge(z_done.sem, z_done.at(b))
                transpose_tiles(pe, misc, z, m.ident[:, :]).then_inc(ht_ps.sem, 1)

            def project(b, i):
                pe.wait_ge(ht_done.sem, ht_done.at(b))
                pe.matmul(misc[:, 0:3 * D], h_t[:, i * P:(i + 1) * P], m.w_qkv[:, :],
                          start=True, stop=True).then_inc(qkv_ps.sem, 1)

            def turn(dst, src, g):
                for i in range(NT):
                    last = pe.transpose(dst[:, i * P:(i + 1) * P],
                                        src[:, i, GH * g:GH * (g + 1), :].rearrange("p h c -> p (h c)"),
                                        m.ident_bf[:, :])
                return last

            def turn_keys(b, c):
                pe.wait_ge(lo_done.sem, lo_done.at(b))
                pe.wait_ge(copy_done.sem, copy_done.at(b))
                turn(misc_bf[:, 0:S], m.k_split, 2 * c)
                turn(misc_bf[:, S:2 * S], m.k_split, 2 * c + 1).then_inc(kt_ps.sem, 1)

            def turn_queries(b, p, c):
                pe.wait_ge(m_zero.sem, m_zero.at(b))
                turn(misc_bf[:, 0:S], m.q_split[:, p, :, :, :], 2 * c)
                turn(misc_bf[:, S:2 * S], m.q_split[:, p, :, :, :], 2 * c + 1).then_inc(q1_ps.sem, 1)

            def turn_shifted(b, p, g):
                pe.wait_ge(ml_done.sem, ml_done.at(b, g + 1))
                turn(misc_bf[:, 0:S], m.q_split[:, p, :, :, :], g).then_inc(q2_ps.sem, 1)

            def scores_for_max(b, p, n, first):
                g, i, j = n // 16, n % 16 // GH, n % GH
                if n == 0:
                    pe.wait_ge(kz_done.sem, kz_done.at(b))
                pe.wait_ge(q1_done.sem, q1_done.at(b, g // 2 + 1))
                if not (first and n < 3):
                    pe.wait_ge(max_done.sem, max_done.at(b, n - 2 if n >= 3 else (0, -2, -1)[n]))
                pe.matmul(raw[n % 3][:, :], q1[:, p, g, i * P:(i + 1) * P], m.kz[:, p, j, g, :],
                          start=True, stop=True).then_inc(s1_ps.sem, 1)

            def scores_shifted(b, p, n, first):
                g, i, j = n // 16, n % 16 // GH, n % GH
                if n % 16 == 0:
                    pe.wait_ge(q2_done.sem, q2_done.at(b, g + 1))
                if not (first and n < 3):
                    pe.wait_ge(exp_done.sem, exp_done.at(b, n - 2 if n >= 3 else (0, -2, -1)[n]))
                pe.matmul(low[n % 3][:, :], m.kz[:, p, j, g, i * P:(i + 1) * P], q2[:, g % 2, :],
                          start=True, stop=True).then_inc(s2_ps.sem, 1)

            def values(b, p, g, i, first):
                pe.wait_ge(exp_done.sem, exp_done.at(b, 16 * g + 4 * i + 4))
                if i == 0:
                    if g == 0:
                        pe.wait_ge(v_done.sem, v_done.at(b))
                    if not (first and g == 0):
                        pe.wait_ge(ctx_done.sem, ctx_done.at(b, g))
                for j in range(GH):
                    last = pe.matmul(av[HC * j:HC * (j + 1), :], m.v_wide[:, p, i, GH * g + j, :],
                                     prob[:, GH * (i % 2) + j, :], start=(i == 0), stop=(i == NT - 1))
                last.then_inc(av_part.sem, 1)

            def turn_values(b, g):
                pe.wait_ge(avs_done.sem, avs_done.at(b, g + 1))
                transpose_tiles(pe, av, tile3(av_s[:, :]), m.ident[:, :]).then_inc(avt_ps.sem, 1)

            def turn_ctx(b):
                pe.wait_ge(ctx_done.sem, ctx_done.at(b))
                transpose_tiles(pe, misc, ctx_s, m.ident[:, :]).then_inc(ct_ps.sem, 1)

            def output(b):
                pe.wait_ge(ct_done.sem, ct_done.at(b))
                for i in range(NT):
                    last = pe.matmul(misc[:, i * P:(i + 1) * P], ctx_t[:, i * P:(i + 1) * P], m.w_out[:, :],
                                     start=True, stop=True)
                last.then_inc(wo_ps.sem, 1)

            def turn_m(b):
                pe.wait_ge(z2_done.sem, z2_done.at(b))
                transpose_tiles(pe, misc, z2, m.ident[:, :]).then_inc(mt_ps.sem, 1)

            def head():
                h_tiles(0)
                for i in range(NT):
                    if i:
                        pe.wait_ge(v_done.sem, v_done.at(0, i))
                    project(0, i)
                pe.wait_ge(v_done.sem, v_done.at(0))
                turn_keys(0, 0)
                pe.wait_ge(kt_done.sem, kt_done.at(0, 1))
                turn_keys(0, 1)
                pe.wait_ge(kt_done.sem, kt_done.at(0, 2))
                turn_queries(0, 0, 0)
                pe.wait_ge(q1_done.sem, q1_done.at(0, 1))
                turn_queries(0, 0, 1)
                for n in range(16):
                    scores_for_max(0, 0, n, True)

            def body(b, p, before, behind):
                for t in range(STEPS):
                    if t < STEPS - 16:
                        scores_for_max(b, p, t + 16, False)
                    elif behind:
                        scores_for_max(b + 1, 1 - p, t + 16 - STEPS, False)
                    n = t - SHIFT_LAG
                    if n >= 0:
                        scores_shifted(b, p, n, not before)
                    elif before:
                        scores_shifted(b - 1, 1 - p, n + STEPS, False)
                    for i in range(NT):
                        n = t - VALUE_LAG[i]
                        if n % 16 == 0 and n >= 0:
                            values(b, p, n // 16, i, not before)
                        elif n % 16 == 0 and before:
                            values(b - 1, 1 - p, NG - 1, i, False)
                    if t % 16 == TURN % 16 and (t > 16 or before):
                        g = t // 16 - 1
                        turn_values(b if g >= 0 else b - 1, g % NG)
                    if t == 3:
                        if before:
                            pe.wait_ge(q2_done.sem, q2_done.at(b - 1, 4))
                        else:
                            pe.wait_ge(q1_done.sem, q1_done.at(b))
                        turn_shifted(b, p, 0)
                    if t == 7 and behind:
                        pe.wait_ge(q2_done.sem, q2_done.at(b, 1))
                        h_tiles(b + 1)
                    if t == 10 and behind:
                        project(b + 1, 0)
                    if t == 13 and behind:
                        pe.wait_ge(v_done.sem, v_done.at(b + 1, 1))
                        project(b + 1, 1)
                    if t == 16 and before:
                        if behind:
                            pe.wait_ge(v_done.sem, v_done.at(b + 1, 2))
                        else:
                            pe.wait_ge(q2_done.sem, q2_done.at(b, 1))
                        turn_ctx(b - 1)
                    if t == 19:
                        if before:
                            pe.wait_ge(ct_done.sem, ct_done.at(b - 1))
                        else:
                            pe.wait_ge(v_done.sem, v_done.at(b + 1, 2))
                        turn_shifted(b, p, 1)
                    if t == 22 and before:
                        pe.wait_ge(q2_done.sem, q2_done.at(b, 2))
                        output(b - 1)
                    if t == 25 and behind:
                        if before:
                            pe.wait_ge(y2_done.sem, y2_done.at(b - 1))
                        else:
                            pe.wait_ge(q2_done.sem, q2_done.at(b, 2))
                        project(b + 1, 2)
                    if t == 28 and behind:
                        pe.wait_ge(v_done.sem, v_done.at(b + 1, 3))
                        project(b + 1, 3)
                    if t == 31 and behind:
                        pe.wait_ge(v_done.sem, v_done.at(b + 1, 4))
                        turn_keys(b + 1, 0)
                    if t == 33 and behind:
                        pe.wait_ge(kt_done.sem, kt_done.at(b + 1, 1))
                        turn_keys(b + 1, 1)
                    if t == 35:
                        if behind:
                            pe.wait_ge(kt_done.sem, kt_done.at(b + 1, 2))
                        else:
                            pe.wait_ge(y2_done.sem, y2_done.at(b - 1))
                        turn_shifted(b, p, 2)
                    if t == 38 and behind:
                        pe.wait_ge(q2_done.sem, q2_done.at(b, 3))
                        turn_queries(b + 1, 1 - p, 0)
                    if t == 41 and behind:
                        pe.wait_ge(q1_done.sem, q1_done.at(b + 1, 1))
                        turn_queries(b + 1, 1 - p, 1)
                    if t == 45 and before:
                        if behind:
                            pe.wait_ge(q1_done.sem, q1_done.at(b + 1, 2))
                        else:
                            pe.wait_ge(q2_done.sem, q2_done.at(b, 3))
                        turn_m(b - 1)
                    if t == 51:
                        if before:
                            pe.wait_ge(mt_done.sem, mt_done.at(b - 1))
                        else:
                            pe.wait_ge(q1_done.sem, q1_done.at(b + 1, 2))
                        turn_shifted(b, p, 3)

            def last():
                for t in range(STEPS, STEPS + 16):
                    n = t - SHIFT_LAG
                    if n < STEPS:
                        scores_shifted(B - 1, 1, n, False)
                    for i in range(NT):
                        if t - VALUE_LAG[i] == STEPS - 16:
                            values(B - 1, 1, NG - 1, i, False)
                turn_values(B - 1, NG - 1)
                pe.wait_ge(q2_done.sem, q2_done.at(B - 1))
                turn_ctx(B - 1)
                output(B - 1)
                turn_m(B - 1)

            batches(pe, head, body, last)


def phase_experts(nc, m, signal, tag, out=None):
    with ExitStack() as ctx:
        def sb(name, shape, dt=F32):
            return ctx.enter_context(nc.sbuf_tensor(tag + name, shape, dt))

        hid = [ctx.enter_context(nc.psum_tensor(f"{tag}hid{i}", [P, 512], F32)) for i in range(4)]
        yps = [ctx.enter_context(nc.psum_tensor(f"{tag}yps{i}", [P, 512], F32)) for i in range(2)]
        misc = [ctx.enter_context(nc.psum_tensor(f"{tag}misc{i}", [P, 512], F32)) for i in range(2)]
        h_full = sb("h_full", [P, NF, S])
        h_hi = sb("h_hi", [P, 2, NF, S], BF16)
        h_lo = sb("h_lo", [P, 2, NF, S], BF16)
        m_hi = sb("m_hi", [P, B * S], BF16)
        m_lo = sb("m_lo", [P, B * S], BF16)
        logit = sb("logit", [P, NT, E])
        top = sb("top", [P, NT, 8])
        top_i = sb("top_i", [P, NT, 8], U32)
        top_f = sb("top_f", [P, NT, 2])
        gap = sb("gap", [P, NT])
        gap_t = sb("gap_t", [P, NT])
        wts = sb("wts", [P, NT, 2])
        one1 = sb("one1", [P, NT, E])
        one2 = sb("one2", [P, NT, E])
        gates = sb("gates", [P, NT, E])
        gates_t = sb("gates_t", [E, S])
        acc = sb("acc", [P, NT, D])
        m_b = sb("m_b", [P, S])

        high_done = signal("high")
        low_done = signal("low")
        copied = signal("copied")
        lg_ps = signal("lg_ps")
        lg_done = signal("lg_done")
        top_done = signal("top_done")
        idx_done = signal("idx_done")
        idxf_done = signal("idxf_done")
        gap_done = signal("gap_done")
        gapt_done = signal("gapt_done")
        wts_done = signal("wts_done")
        one_done = signal("one_done")
        gates_done = signal("gates_done")
        gt_ps = signal("gt_ps")
        gt_done = signal("gt_done")
        b2_ps = signal("b2_ps")
        hid_ps = signal("hid_ps", E * NF)
        h_done = signal("h_done", E * NF)
        hlo_done = signal("hlo_done", E * (NF - 1))
        hlo_pool = signal("hlo_pool", E)
        y_ps = signal("y_ps", E)
        acc_done = signal("acc_done", E + 1)
        x_done = signal("x_done")
        stored = signal("stored", 16)
        stored.before = 0
        block = ctx.enter_context(nc.Block())

        @block.sync
        def _(sp):
            if out is not None:
                with sp.Fori(0, B) as b:
                    sp.wait_ge(x_done.sem, x_done.at(b))
                    sp.dma_start(out[bass.ds(b, 1), :, :].rearrange("b (t p) d -> p (b t) d", p=P),
                                 m.x[:, bass.ds(b * NT, NT), :]).then_inc(stored.sem, 16)
                sp.wait_ge(stored.sem, stored.at(B - 1))

        @block.vector
        def _(dve):
            def low(b, e):
                for c in range(NF - 1):
                    n = e * NF + c
                    dve.wait_ge(h_done.sem, h_done.at(b, n + 1))
                    dve.tensor_tensor(h_lo[:, e % 2, c, :], h_full[:, c, :], h_hi[:, e % 2, c, :], ALU.subtract)\
                        .then_inc(hlo_done.sem, 1)

            def best_two(b):
                dve.wait_ge(lg_ps.sem, lg_ps.at(b))
                dve.tensor_copy(logit[:, :, :], tile3(misc[1][:, 0:NT * E])).then_inc(lg_done.sem, 1)
                dve.wait_ge(lg_done.sem, lg_done.at(b))
                fence(dve, m)
                for i in range(NT):
                    last = dve.max(top[:, i, :], logit[:, i, :])
                last.then_inc(top_done.sem, 1)
                dve.wait_ge(top_done.sem, top_done.at(b))
                fence(dve, m)
                dve.tensor_tensor(gap[:, :], top[:, :, 0], top[:, :, 1], ALU.subtract).then_inc(gap_done.sem, 1)
                for i in range(NT):
                    last = dve.max_index(top_i[:, i, :], top[:, i, :], logit[:, i, :])
                last.then_inc(idx_done.sem, 1)
                dve.wait_ge(idx_done.sem, idx_done.at(b))
                dve.tensor_copy(top_f[:, :, :], top_i[:, :, 0:2]).then_inc(idxf_done.sem, 1)

            def weights(b):
                dve.wait_ge(gapt_done.sem, gapt_done.at(b))
                dve.tensor_scalar(wts[:, :, 0], gap_t[:, :], 0.5, 0.5, ALU.mult, ALU.add)
                dve.tensor_scalar(wts[:, :, 1], gap_t[:, :], -0.5, 0.5, ALU.mult, ALU.add).then_inc(wts_done.sem, 1)
                dve.wait_ge(wts_done.sem, wts_done.at(b))
                dve.wait_ge(idxf_done.sem, idxf_done.at(b))
                for i in range(NT):
                    dve.tensor_scalar(one1[:, i, :], m.expert_id[:, :], top_f[:, i, 0:1], wts[:, i, 0:1],
                                      ALU.is_equal, ALU.mult)
                    last = dve.tensor_scalar(one2[:, i, :], m.expert_id[:, :], top_f[:, i, 1:2], wts[:, i, 1:2],
                                             ALU.is_equal, ALU.mult)
                last.then_inc(one_done.sem, 1)
                dve.wait_ge(one_done.sem, one_done.at(b))
                dve.tensor_tensor(gates[:, :, :], one1[:, :, :], one2[:, :, :], ALU.add).then_inc(gates_done.sem, 1)
                dve.wait_ge(gates_done.sem, gates_done.at(b))

            def accumulate(b, e):
                dve.wait_ge(y_ps.sem, y_ps.at(b, e + 1))
                if e > 0:
                    dve.wait_ge(acc_done.sem, acc_done.at(b, e))
                for i in range(NT):
                    under = acc[:, i, :] if e > 0 else m.y[:, bass.ds(b * NT + i, 1), :].rearrange("p t d -> p (t d)")
                    last = dve.scalar_tensor_tensor(out=acc[:, i, :], in0=yps[e % 2][:, i * P:(i + 1) * P],
                                                    scalar=gates[:, i, e:e + 1], in1=under,
                                                    op0=ALU.mult, op1=ALU.add)
                last.then_inc(acc_done.sem, 1)

            with dve.Fori(0, B) as b:
                x_b = m.x[:, bass.ds(b * NT, NT), :]
                best_two(b)
                low(b, 0)
                weights(b)
                for e in range(1, E):
                    low(b, e)
                    accumulate(b, e - 1)
                    if e == 2:
                        dve.wait_ge(gt_ps.sem, gt_ps.at(b))
                        dve.tensor_copy(gates_t[:, :], misc[1][0:E, :]).then_inc(gt_done.sem, 1)
                accumulate(b, E - 1)
                dve.wait_ge(b2_ps.sem, b2_ps.at(b))
                dve.wait_ge(acc_done.sem, acc_done.at(b, E))
                dve.tensor_tensor(acc[:, :, :], tile3(misc[0][:, :]), acc[:, :, :], ALU.add).then_inc(acc_done.sem, 1)
                dve.wait_ge(acc_done.sem, acc_done.at(b))
                dve.scalar_tensor_tensor(out=x_b, in0=acc[:, :, :], scalar=0.5, in1=x_b, op0=ALU.mult,
                                         op1=ALU.add).then_inc(x_done.sem, 1)

        @block.scalar
        def _(act):
            def tanh(b):
                act.wait_ge(gap_done.sem, gap_done.at(b))
                act.activation(gap_t[:, :], gap[:, :], ACT.Tanh, scale=0.5).then_inc(gapt_done.sem, 1)

            with act.Fori(0, B) as b:
                for e in range(E):
                    for c in range(NF):
                        n = e * NF + c
                        act.wait_ge(hid_ps.sem, hid_ps.at(b, n + 1))
                        if e >= 2 and c == 0:
                            act.wait_ge(y_ps.sem, y_ps.at(b, e - 1))
                        act.activation(h_hi[:, e % 2, c, :], hid[n % 4][:, :], ACT.Gelu_apprx_tanh,
                                       bias=m.b1[:, e, c:c + 1])
                        if e >= 1 and c < NF - 1:
                            act.wait_ge(hlo_done.sem, hlo_done.at(b, (e - 1) * (NF - 1) + c + 1))
                        elif e >= 1:
                            act.wait_ge(hlo_pool.sem, hlo_pool.at(b, e))
                        act.activation(h_full[:, c, :], hid[n % 4][:, :], ACT.Gelu_apprx_tanh,
                                       bias=m.b1[:, e, c:c + 1]).then_inc(h_done.sem, 1)
                    if e == 0:
                        tanh(b)

        @block.tensor
        def _(pe):
            def hidden(b, e):
                for c in range(NF):
                    n = e * NF + c
                    if n >= 4:
                        pe.wait_ge(h_done.sem, h_done.at(b, n - 3))
                    w_hi = m.w1_hi[:, e, c * P:(c + 1) * P]
                    w_lo = m.w1_lo[:, e, c * P:(c + 1) * P]
                    high, low = m_hi[:, bass.ds(b * S, S)], m_lo[:, bass.ds(b * S, S)]
                    pe.matmul(hid[n % 4][:, :], w_hi, high, start=True, stop=False)
                    pe.matmul(hid[n % 4][:, :], w_hi, low, start=False, stop=False)
                    pe.matmul(hid[n % 4][:, :], w_lo, high, start=False, stop=True).then_inc(hid_ps.sem, 1)

            def outputs(b, e):
                if e >= 2:
                    pe.wait_ge(acc_done.sem, acc_done.at(b, e - 1))
                pe.wait_ge(hlo_done.sem, hlo_done.at(b, (NF - 1) * (e + 1)))
                pe.wait_ge(hlo_pool.sem, hlo_pool.at(b, e + 1))
                for i in range(NT):
                    tok = slice(i * P, (i + 1) * P)
                    for c in range(NF):
                        w_hi = m.w2_hi[:, e, c * P:(c + 1) * P]
                        w_lo = m.w2_lo[:, e, c * P:(c + 1) * P]
                        pe.matmul(yps[e % 2][:, tok], h_hi[:, e % 2, c, tok], w_hi, start=(c == 0), stop=False)
                        pe.matmul(yps[e % 2][:, tok], h_hi[:, e % 2, c, tok], w_lo, start=False, stop=False)
                        last = pe.matmul(yps[e % 2][:, tok], h_lo[:, e % 2, c, tok], w_hi,
                                         start=False, stop=(c == NF - 1))
                last.then_inc(y_ps.sem, 1)

            def turn_gates(b):
                pe.wait_ge(gates_done.sem, gates_done.at(b))
                for i in range(NT):
                    last = pe.transpose(misc[1][0:E, i * P:(i + 1) * P], gates[:, i, :], m.ident[:, :])
                last.then_inc(gt_ps.sem, 1)

            def output_bias(b):
                pe.wait_ge(gt_done.sem, gt_done.at(b))
                for i in range(NT):
                    last = pe.matmul(misc[0][:, i * P:(i + 1) * P], gates_t[:, i * P:(i + 1) * P], m.b2[:, :],
                                     start=True, stop=True)
                last.then_inc(b2_ps.sem, 1)

            with pe.Fori(0, B) as b:
                pe.wait_ge(copied.sem, copied.at(b))
                for i in range(NT):
                    last = pe.matmul(misc[1][:, i * E:(i + 1) * E], m_b[:, i * P:(i + 1) * P],
                                     m.w_gate[:, :], start=True, stop=True)
                last.then_inc(lg_ps.sem, 1)
                pe.wait_ge(low_done.sem, low_done.at(b))
                hidden(b, 0)
                for e in range(E):
                    if e + 1 < E:
                        hidden(b, e + 1)
                    outputs(b, e)
                    if e == 1:
                        turn_gates(b)
                    if e == 3:
                        output_bias(b)

        @block.gpsimd
        def _(pool):
            def parts(b):
                full, high, low = (t[:, bass.ds(b * S, S)].rearrange("p (t d) -> p t d", d=D)
                                   for t in (m.m_t, m_hi, m_lo))
                pool.tensor_tensor(high, full, again(m.zero_bf[:, :], NT), ALU.add).then_inc(high_done.sem, 1)
                pool.wait_ge(high_done.sem, high_done.at(b))
                pool.tensor_tensor(low, full, high, ALU.subtract).then_inc(low_done.sem, 1)

            def gate_copy(b):
                pool.tensor_tensor(tile3(m_b[:, :]), m.m_t[:, bass.ds(b * S, S)].rearrange("p (t d) -> p t d", d=D),
                                   again(m.zero_bf[:, :], NT), ALU.add).then_inc(copied.sem, 1)

            def low(b, e):
                pool.wait_ge(h_done.sem, h_done.at(b, NF * (e + 1)))
                pool.tensor_tensor(h_lo[:, e % 2, NF - 1, :], h_full[:, NF - 1, :], h_hi[:, e % 2, NF - 1, :],
                                   ALU.subtract).then_inc(hlo_pool.sem, 1)

            def one_batch(b, behind):
                low(b, 0)
                if behind:
                    pool.wait_ge(lg_ps.sem, lg_ps.at(b))
                    gate_copy(b + 1)
                low(b, 1)
                if behind:
                    parts(b + 1)
                for e in range(2, E):
                    low(b, e)

            parts(0)
            gate_copy(0)
            with pool.Fori(0, B - 1) as b:
                one_batch(b, True)
            one_batch(B - 1, False)


def phase_linear(nc, m, signal):
    STEPS = NG * 16
    VALUE_LAG = (6, 10, 14, 18)
    TAKE, TURN, STORE = 20, 22, 24
    NS = 4
    with ExitStack() as ctx:
        def sb(name, shape, dt=F32):
            return ctx.enter_context(nc.sbuf_tensor("li_" + name, shape, dt))

        score = [ctx.enter_context(nc.psum_tensor(f"li_score{i}", [P, 512], F32)) for i in range(NS)]
        av = ctx.enter_context(nc.psum_tensor("li_av", [P, 512], F32))
        avt = ctx.enter_context(nc.psum_tensor("li_avt", [P, 512], F32))
        misc = [ctx.enter_context(nc.psum_tensor(f"li_misc{i}", [P, 512], F32)) for i in range(2)]
        misc_bf = [t[:, :].bitcast(BF16) for t in misc]
        st = sb("st", [P, NT, 6])
        mv = sb("mv", [P, NT, 2])
        var = sb("var", [P, NT])
        rstd = sb("rstd", [P, NT])
        y = sb("y", [P, NT, D])
        y_t = sb("y_t", [P, S])
        sq = sb("sq", [P, NT, 2 * D])
        ss = sb("ss", [P, NT, 2 * H])
        ms = sb("ms", [P, NT, 2 * H])
        root = sb("root", [P, NT, 2 * H])
        r0 = sb("r0", [P, NT, 2 * H])
        r1 = sb("r1", [P, NT, 2 * H])
        rr = sb("rr", [P, NT, 2 * H])
        qv = sb("qv", [P, NT, 2 * D])
        k_t = sb("k_t", [P, NG, S], BF16)
        q1 = sb("q1", [P, 2, NG, S], BF16)
        prob = sb("prob", [P, 8, S])
        av_s = sb("av_s", [P, S])
        ctx_s = sb("ctx_s", [P, NT, D])

        stats = signal("stats")
        mv_done = signal("mv")
        var_done = signal("var")
        rstd_done = signal("rstd")
        y_done = signal("y")
        yt_ps = signal("yt_ps")
        yt_done = signal("yt")
        qv_ps = signal("qv_ps", 2)
        sq_done = signal("sq", 2)
        ss_done = signal("ss")
        ms_done = signal("ms")
        root_done = signal("root")
        newton = signal("newton", 4)
        rr_done = signal("rr")
        qr_done = signal("qr", 2)
        qw_done = signal("qw")
        hi_done = signal("hi", 2)
        copy_done = signal("copy", 2)
        lo_done = signal("lo", 2)
        v_done = signal("v")
        kt_ps = signal("kt_ps", 2)
        kt_done = signal("kt", 2)
        q1_ps = signal("q1_ps", 2)
        q1_done = signal("q1", 2)
        kz_done = signal("kz", 16 * GH)
        s_ps = signal("s_ps", STEPS)
        mask_done = signal("mask", STEPS)
        rest_done = signal("rest", NG * 12)
        av_part = signal("av_part", NG * NT)
        avs_done = signal("avs", NG)
        avt_ps = signal("avt_ps", NG)
        ctx_done = signal("ctx", NG)
        x_done = signal("x")
        block = ctx.enter_context(nc.Block())

        def batches(eng, head, body, last):
            head()
            body(0, 0, False, True)
            with eng.Fori(0, (B - 2) // 2) as i:
                body(i * 2 + 1, 1, True, True)
                body(i * 2 + 2, 0, True, True)
            body(B - 1, 1, True, False)
            last()

        def per_head(ap):
            return ap.rearrange("p t (h d) -> p t h d", d=DH)

        @block.sync
        def _(sp):
            def spread(b, p):
                sp.wait_ge(kt_done.sem, kt_done.at(b))
                for j in range(GH):
                    rows = slice(HC * j, HC * (j + 1))
                    sp.dma_start(m.kz[rows, p, j, :, :], k_t[rows, :, :]).then_inc(kz_done.sem, 16)

            spread(0, 0)
            with sp.Fori(0, (B - 2) // 2) as i:
                spread(i * 2 + 1, 1)
                spread(i * 2 + 2, 0)
            spread(B - 1, 1)
            sp.wait_ge(kz_done.sem, kz_done.at(B - 1))

        @block.gpsimd
        def _(pool):
            zero = again(m.zero_bf[:, :], NT).rearrange("p t (h d) -> p t h d", d=DH)

            def operands(b):
                pool.wait_ge(var_done.sem, var_done.at(b))
                pool.tensor_tensor(rstd[:, :], var[:, :], m.half_pow[:, 0, :], ALU.pow).then_inc(rstd_done.sem, 1)
                for c, (q, lo, hi) in enumerate(((m.k_split, 0, 8), (m.q_split[:, 0, :, :, :], 0, 16))):
                    pool.wait_ge(hi_done.sem, hi_done.at(b, c + 1))
                    for i in range(NT):
                        last = pool.tensor_tensor(q[:, i, :, hi:hi + DH], q[:, i, :, lo:lo + DH],
                                                  m.zero_bf[:, :].rearrange("p (h d) -> p h d", d=DH), ALU.add)
                    last.then_inc(copy_done.sem, 1)

            operands(0)
            with pool.Fori(1, B) as b:
                operands(b)

        @block.vector
        def _(dve):
            def rows(b):
                return m.x[:, bass.ds(b * NT, NT), :]

            def stats_x(b):
                layer_stats(dve, m, rows(b), st, mv, stats, mv_done, b)
                dve.wait_ge(mv_done.sem, mv_done.at(b))
                dve.tensor_scalar(var[:, :], mv[:, :, 1], EPS, None, ALU.add).then_inc(var_done.sem, 1)

            def norm_x(b):
                dve.wait_ge(rstd_done.sem, rstd_done.at(b))
                normalise(dve, y, rows(b), mv, rstd).then_inc(y_done.sem, 1)

            def key_low(b):
                dve.wait_ge(hi_done.sem, hi_done.at(b, 1))
                dve.tensor_tensor(m.k_split[:, :, :, 16:24], per_head(y[:, :, :]), m.k_split[:, :, :, 0:8],
                                  ALU.subtract).then_inc(lo_done.sem, 1)

            def mean_square(b):
                dve.wait_ge(sq_done.sem, sq_done.at(b))
                dve.tensor_reduce(ss[:, :, :], per_head(sq[:, :, :]), AX.X, ALU.add).then_inc(ss_done.sem, 1)
                dve.wait_ge(ss_done.sem, ss_done.at(b))
                dve.tensor_scalar(ms[:, :, :], ss[:, :, :], 1.0 / DH, EPS_RMS, ALU.mult, ALU.add)\
                    .then_inc(ms_done.sem, 1)

            def inverse_root(b):
                dve.wait_ge(root_done.sem, root_done.at(b))
                dve.reciprocal(r0[:, :, :], root[:, :, :]).then_inc(newton.sem, 1)
                dve.wait_ge(newton.sem, newton.at(b, 1))
                dve.tensor_tensor(r1[:, :, :], r0[:, :, :], r0[:, :, :], ALU.mult).then_inc(newton.sem, 1)
                dve.wait_ge(newton.sem, newton.at(b, 2))
                dve.tensor_tensor(r1[:, :, :], r1[:, :, :], ms[:, :, :], ALU.mult).then_inc(newton.sem, 1)
                dve.wait_ge(newton.sem, newton.at(b, 3))
                dve.tensor_scalar(r1[:, :, :], r1[:, :, :], -0.5, 1.5, ALU.mult, ALU.add).then_inc(newton.sem, 1)
                dve.wait_ge(newton.sem, newton.at(b, 4))
                dve.tensor_tensor(rr[:, :, :], r0[:, :, :], r1[:, :, :], ALU.mult).then_inc(rr_done.sem, 1)

            def rms_norm(b):
                dve.wait_ge(rr_done.sem, rr_done.at(b))
                for c in range(2):
                    dve.tensor_tensor(
                        qv[:, 2 * c:2 * c + 2, :].rearrange("p t (h d) -> p (t h) d", d=DH),
                        misc[c][:, :].rearrange("p (h d) -> p h d", d=DH),
                        wide(rr[:, 2 * c:2 * c + 2, :].rearrange("p t h -> p (t h)"), DH), ALU.mult)\
                        .then_inc(qr_done.sem, 1)
                dve.wait_ge(qr_done.sem, qr_done.at(b))
                dve.tensor_tensor(qv[:, :, :], qv[:, :, :], again(m.norm_w[:, :], NT), ALU.mult)\
                    .then_inc(qw_done.sem, 1)

            def query_low(b, p):
                dve.wait_ge(qw_done.sem, qw_done.at(b))
                dve.tensor_copy(m.v_wide[:, p, :, :, 0:DH], per_head(qv[:, :, D:2 * D])).then_inc(v_done.sem, 1)
                dve.wait_ge(hi_done.sem, hi_done.at(b, 2))
                dve.tensor_tensor(m.q_split[:, 0, :, :, 8:16], per_head(qv[:, :, 0:D]),
                                  m.q_split[:, 0, :, :, 0:8], ALU.subtract).then_inc(lo_done.sem, 1)

            def mask(b, n, first):
                g, u, i = n // 16, n % 16, n % 16 // GH
                if u < 12:
                    dve.wait_ge(rest_done.sem, rest_done.at(b, 12 * g + u + 1))
                else:
                    dve.wait_ge(s_ps.sem, s_ps.at(b, n + 1))
                if n % 4 == 0 and not (first and n < 8):
                    dve.wait_ge(av_part.sem, av_part.at(b, (n - 8) // 4 + 1))
                dve.tensor_tensor(prob[:, n % 8, i * P:(i + 1) * P], score[n % NS][:, i * P:(i + 1) * P],
                                  m.causal[:, :], ALU.mult).then_inc(mask_done.sem, 1)

            def store(b, g):
                dve.wait_ge(avt_ps.sem, avt_ps.at(b, g + 1))
                t = avt[:, :].rearrange("p (t h c) -> p t h c", t=NT, c=HC)
                dve.tensor_copy(ctx_s[:, :, 32 * g:32 * (g + 1)].rearrange("p t (h d) -> p t h d", d=DH),
                                t[:, :, :, 0:DH]).then_inc(ctx_done.sem, 1)

            def add_x(b):
                dve.wait_ge(ctx_done.sem, ctx_done.at(b))
                dve.tensor_tensor(rows(b), rows(b), ctx_s[:, :, :], ALU.add).then_inc(x_done.sem, 1)

            def head():
                dve.memset(m.q_split[:, 0, :, :, 24:26], 0.0)
                stats_x(0)
                norm_x(0)
                key_low(0)
                mean_square(0)
                inverse_root(0)
                rms_norm(0)
                query_low(0, 0)

            def body(b, p, before, behind):
                for t in range(STEPS):
                    if t >= 1:
                        mask(b, t - 1, not before)
                    elif before:
                        mask(b - 1, STEPS - 1, False)
                    if t % 16 == STORE % 16 and (t > 16 or before):
                        g = t // 16 - 1
                        store(b if g >= 0 else b - 1, g % NG)
                    if t == 12 and before:
                        add_x(b - 1)
                    if behind:
                        if t == 0:
                            stats_x(b + 1)
                        if t == 7:
                            norm_x(b + 1)
                        if t == 13:
                            key_low(b + 1)
                        if t == 20:
                            mean_square(b + 1)
                        if t == 24:
                            inverse_root(b + 1)
                        if t == 26:
                            rms_norm(b + 1)
                        if t == 34:
                            query_low(b + 1, 1 - p)

            def last():
                mask(B - 1, STEPS - 1, False)
                store(B - 1, NG - 1)
                add_x(B - 1)

            batches(dve, head, body, last)

        @block.scalar
        def _(act):
            def key_high(b):
                act.wait_ge(y_done.sem, y_done.at(b))
                act.activation(m.k_split[:, :, :, 0:DH], per_head(y[:, :, :]), ACT.Copy).then_inc(hi_done.sem, 1)

            def to_y(b):
                act.wait_ge(yt_ps.sem, yt_ps.at(b))
                act.activation(y_t[:, :], misc[0][:, :], ACT.Copy).then_inc(yt_done.sem, 1)

            def squares(b, c):
                act.wait_ge(qv_ps.sem, qv_ps.at(b, c + 1))
                act.activation(sq[:, 2 * c:2 * c + 2, :], tile3(misc[c][:, :], 2), ACT.Square)\
                    .then_inc(sq_done.sem, 1)

            def roots(b):
                act.wait_ge(ms_done.sem, ms_done.at(b))
                act.activation(root[:, :, :], ms[:, :, :], ACT.Sqrt).then_inc(root_done.sem, 1)

            def query_high(b):
                act.wait_ge(qw_done.sem, qw_done.at(b))
                act.activation(m.q_split[:, 0, :, :, 0:DH], per_head(qv[:, :, 0:D]), ACT.Copy)\
                    .then_inc(hi_done.sem, 1)

            def to_kt(b, c):
                act.wait_ge(kt_ps.sem, kt_ps.at(b, c + 1))
                act.activation(k_t[:, 2 * c:2 * c + 2, :], tile3(misc_bf[c], 2), ACT.Copy).then_inc(kt_done.sem, 1)

            def to_q1(b, p, c):
                act.wait_ge(q1_ps.sem, q1_ps.at(b, c + 1))
                act.activation(q1[:, p, 2 * c:2 * c + 2, :], tile3(misc_bf[c], 2), ACT.Copy)\
                    .then_inc(q1_done.sem, 1)

            def rest(b, n, first):
                i = n % 16 // GH
                act.wait_ge(s_ps.sem, s_ps.at(b, n + 1))
                if n % 4 == 0 and not (first and n < 8):
                    act.wait_ge(av_part.sem, av_part.at(b, (n - 8) // 4 + 1))
                act.activation(prob[:, n % 8, (i + 1) * P:], score[n % NS][:, (i + 1) * P:], ACT.Copy)\
                    .then_inc(rest_done.sem, 1)

            def take_values(b, g):
                act.wait_ge(av_part.sem, av_part.at(b, NT * (g + 1)))
                act.activation(av_s[:, :], av[:, :], ACT.Copy).then_inc(avs_done.sem, 1)

            def head():
                key_high(0)
                to_y(0)
                for c in range(2):
                    squares(0, c)
                roots(0)
                query_high(0)
                for c in range(2):
                    to_kt(0, c)
                for c in range(2):
                    to_q1(0, 0, c)

            def body(b, p, before, behind):
                for t in range(STEPS):
                    if t % 16 < 12:
                        rest(b, t, not before)
                    if t % 16 == TAKE % 16 and (t > 16 or before):
                        g = t // 16 - 1
                        take_values(b if g >= 0 else b - 1, g % NG)
                    if behind:
                        if t == 9:
                            key_high(b + 1)
                        if t == 11:
                            to_y(b + 1)
                        if t in (15, 17):
                            squares(b + 1, (t - 15) // 2)
                        if t == 22:
                            roots(b + 1)
                        if t == 32:
                            query_high(b + 1)
                        if t in (36, 38):
                            to_kt(b + 1, (t - 36) // 2)
                        if t in (46, 48):
                            to_q1(b + 1, 1 - p, (t - 46) // 2)

            def last():
                take_values(B - 1, NG - 1)

            batches(act, head, body, last)

        @block.tensor
        def _(pe):
            def y_tiles(b):
                pe.wait_ge(y_done.sem, y_done.at(b))
                transpose_tiles(pe, misc[0], y, m.ident[:, :]).then_inc(yt_ps.sem, 1)

            def project(b, c):
                pe.wait_ge(yt_done.sem, yt_done.at(b))
                for i in (2 * c, 2 * c + 1):
                    o = (i % 2) * 2 * D
                    last = pe.matmul(misc[c][:, o:o + 2 * D], y_t[:, i * P:(i + 1) * P], m.w_lin[:, :],
                                     start=True, stop=True)
                last.then_inc(qv_ps.sem, 1)

            def turn(dst, src, g):
                for i in range(NT):
                    last = pe.transpose(dst[:, i * P:(i + 1) * P],
                                        src[:, i, GH * g:GH * (g + 1), :].rearrange("p h c -> p (h c)"),
                                        m.ident_bf[:, :])
                return last

            def turn_keys(b, c):
                pe.wait_ge(qr_done.sem, qr_done.at(b, c + 1))
                pe.wait_ge(lo_done.sem, lo_done.at(b, 1))
                pe.wait_ge(copy_done.sem, copy_done.at(b, 1))
                turn(misc_bf[c][:, 0:S], m.k_split, 2 * c)
                turn(misc_bf[c][:, S:2 * S], m.k_split, 2 * c + 1).then_inc(kt_ps.sem, 1)

            def turn_queries(b, c):
                pe.wait_ge(kt_done.sem, kt_done.at(b, c + 1))
                pe.wait_ge(lo_done.sem, lo_done.at(b, 2))
                pe.wait_ge(copy_done.sem, copy_done.at(b, 2))
                turn(misc_bf[c][:, 0:S], m.q_split[:, 0, :, :, :], 2 * c)
                turn(misc_bf[c][:, S:2 * S], m.q_split[:, 0, :, :, :], 2 * c + 1).then_inc(q1_ps.sem, 1)

            def scores(b, p, n, first):
                g, i, j = n // 16, n % 16 // GH, n % GH
                if n == 0:
                    pe.wait_ge(kz_done.sem, kz_done.at(b))
                    pe.wait_ge(q1_done.sem, q1_done.at(b))
                if not (first and n < NS):
                    pe.wait_ge(mask_done.sem, mask_done.at(b, n - NS + 1))
                pe.matmul(score[n % NS][:, i * P:], m.kz[:, p, j, g, i * P:(i + 1) * P], q1[:, p, g, i * P:],
                          start=True, stop=True).then_inc(s_ps.sem, 1)

            def values(b, p, g, i, first):
                pe.wait_ge(mask_done.sem, mask_done.at(b, 16 * g + 4 * (i + 1)))
                if i == 0:
                    if g == 0:
                        pe.wait_ge(v_done.sem, v_done.at(b))
                    if not (first and g == 0):
                        pe.wait_ge(avs_done.sem, avs_done.at(b, g))
                for j in range(GH):
                    last = pe.matmul(av[HC * j:HC * (j + 1), i * P:], m.v_wide[:, p, i, GH * g + j, :],
                                     prob[:, GH * (i % 2) + j, i * P:], start=(i == 0), stop=(i == NT - 1))
                last.then_inc(av_part.sem, 1)

            def turn_values(b, g, first):
                pe.wait_ge(avs_done.sem, avs_done.at(b, g + 1))
                if not (first and g == 0):
                    pe.wait_ge(ctx_done.sem, ctx_done.at(b, g))
                transpose_tiles(pe, avt, tile3(av_s[:, :]), m.ident[:, :]).then_inc(avt_ps.sem, 1)

            def head():
                y_tiles(0)
                for c in range(2):
                    project(0, c)
                for c in range(2):
                    turn_keys(0, c)
                for c in range(2):
                    turn_queries(0, c)

            def body(b, p, before, behind):
                for t in range(STEPS):
                    scores(b, p, t, not before)
                    for i in range(NT):
                        n = t - VALUE_LAG[i]
                        if n % 16 == 0 and n >= 0:
                            values(b, p, n // 16, i, not before)
                        elif n % 16 == 0 and before:
                            values(b - 1, 1 - p, NG - 1, i, False)
                    if t % 16 == TURN % 16 and (t > 16 or before):
                        g = t // 16 - 1
                        turn_values(b if g >= 0 else b - 1, g % NG, not before)
                    if behind:
                        if t == 10:
                            y_tiles(b + 1)
                        if t in (14, 16):
                            project(b + 1, (t - 14) // 2)
                        if t in (35, 37):
                            turn_keys(b + 1, (t - 35) // 2)
                        if t in (45, 47):
                            turn_queries(b + 1, (t - 45) // 2)

            def last():
                for i in range(NT):
                    if VALUE_LAG[i] >= 16:
                        values(B - 1, 1, NG - 1, i, False)
                turn_values(B - 1, NG - 1, False)

            batches(pe, head, body, last)


def macaron_kernel(nc, a, out):
    with ExitStack() as ctx:
        m = Memory()

        def keep_in(where, name, shape, dt=F32):
            return where.enter_context(nc.sbuf_tensor("m_" + name, shape, dt))

        def keep(name, shape, dt=F32):
            return keep_in(ctx, name, shape, dt)

        m.x = keep("x", [P, B * NT, D])
        m.ident = keep("ident", [P, P])
        m.ident_bf = keep("ident_bf", [P, P], BF16)
        m.causal = keep("causal", [P, P])
        m.expert_id = keep("expert_id", [P, E])
        m.half_pow = keep("half_pow", [P, 2, NT])
        m.eps = keep("eps", [P, NT])
        m.zero_bf = keep("zero_bf", [P, D], BF16)
        m.fence = keep("fence", [1, 1])
        m.half_pi = keep("half_pi", [P, 1])
        m.ones = keep("ones", [P, P])
        m.w_pv = keep("w_pv", [P, D])
        m.w_k = keep("w_k", [P, D])
        m.w_kv = keep("w_kv", [P, D])
        m.w_o = keep("w_o", [P, D])
        m.w_eff = keep("w_eff", [P, D])
        m.w_g2 = keep("w_g2", [P, D])
        m.w_out = keep("w_out", [P, D])
        m.w_g1 = keep("w_g1", [P, 2, D])
        m.w_b1 = keep("w_b1", [P, D // 2])
        m.w_b2 = keep("w_b2", [D // 2, P])
        m.w_lin = keep("w_lin", [P, 2 * D])
        m.w_qkv = keep("w_qkv", [P, 3 * D])
        m.w_gate = keep("w_gate", [P, E])
        m.w1_hi = keep("w1_hi", [P, E, F], BF16)
        m.w1_lo = keep("w1_lo", [P, E, F], BF16)
        m.w2_hi = keep("w2_hi", [P, E, F], BF16)
        m.w2_lo = keep("w2_lo", [P, E, F], BF16)
        m.b1 = keep("b1", [P, E, NF])
        m.b2 = keep("b2", [E, D])
        m.b_pv = keep("b_pv", [P, 1])
        m.b_k = keep("b_k", [P, 1])
        m.b_kv = keep("b_kv", [P, 1])
        m.b_g1 = keep("b_g1", [P, 1])
        m.b_b1 = keep("b_b1", [D // 2, 1])
        m.ln_g = keep("ln_g", [P, 1])
        m.ln_b = keep("ln_b", [P, 1])
        m.ln1_g = keep("ln1_g", [P, 1])
        m.ln1_b = keep("ln1_b", [P, 1])
        m.ln2_g = keep("ln2_g", [P, 1])
        m.ln2_b = keep("ln2_b", [P, 1])
        m.half_bg2 = keep("half_bg2", [P, 1])
        m.half_bb2 = keep("half_bb2", [P, 1])
        m.ffn_bias = keep("ffn_bias", [P, D])
        m.half_bias = keep("half_bias", [P, D])
        m.bo = keep("bo", [P, D])
        m.norm_w = keep("norm_w", [P, 2 * D])
        m.kz = keep("kz", [P, 2, GH, NG, S], BF16)
        m.q_split = keep("q_split", [P, 2, NT, H, HC], BF16)
        m.k_split = keep("k_split", [P, NT, H, HC], BF16)
        m.v_wide = keep("v_wide", [P, 2, NT, H, HC])

        mixer = Signals(nc, ctx, "mx_")
        softmax = Signals(nc, ctx, "sm_")
        experts = Signals(nc, ctx, "ex_")
        linear = Signals(nc, ctx, "li_")
        with ExitStack() as early:
            m.zeros = keep_in(early, "zeros", [P, S])
            m.pos_cos = keep_in(early, "pos_cos", [P, S])
            m.pos_sin = keep_in(early, "pos_sin", [P, S])
            m.key_cos = keep_in(early, "key_cos", [P, S + 1])
            m.key_sin = keep_in(early, "key_sin", [P, S + 1])
            m.u_t = keep_in(early, "u_t", [P, S + 1])
            phase_load(nc, a, m, ctx)
            phase_mixer(nc, a, m, mixer.run())
        m.y = keep("y", [P, B * NT, D])
        m.m_t = keep("m_t", [P, B * S])
        phase_softmax(nc, m, softmax.run(), "s1_")
        phase_experts(nc, m, experts.run(), "e1_")
        phase_linear(nc, m, linear.run())
        phase_softmax(nc, m, softmax.run(), "s2_")
        phase_experts(nc, m, experts.run(), "e2_", out)


def kernel(**inputs):
    import concourse.bacc as bacc
    from concourse.bass_utils import run_bass_kernel_spmd

    nc = bacc.Bacc("TRN2", target_bir_lowering=False, num_devices=1)
    arrays, args = {}, {}
    for name in INS:
        a = np.ascontiguousarray(inputs[name])
        arrays[f"in_{name}"] = a
        args[name] = nc.dram_tensor(f"in_{name}", a.shape, mybir.dt.from_np(a.dtype), kind="ExternalInput").ap()
    out = nc.dram_tensor("out_x", (B, S, D), F32, kind="ExternalOutput").ap()
    macaron_kernel(nc, args, out)
    r = run_bass_kernel_spmd(nc, [arrays], core_ids=[0])
    return r.results[0]["out_x"]
```

```python
from contextlib import ExitStack

import numpy as np

import concourse.bass as bass
from concourse import mybir

F32 = mybir.dt.float32
BF16 = mybir.dt.bfloat16
U32 = mybir.dt.uint32
ALU = mybir.AluOpType
ACT = mybir.ActivationFunctionType
AX = mybir.AxisListType

P = 128
B, S, D = 8, 512, 128
NT = S // P
H, DH = 16, 8
GH = 4
NG = H // GH
E, F = 8, 512
NF = F // P
assert E == B and B % 2 == 0
HC = 32
EPS = 1e-5
EPS_RMS = 1e-8
SCORE_SCALE = float(DH) ** -0.5
RSQRT_D = float(D) ** -0.5
PI = 3.1415925
MAGIC = 12582912.0
TWO_PI_HI = 6.28125
TWO_PI_MID = 0.0019350051879882812
TWO_PI_LO = float(2.0 * np.pi - 6.28125 - 0.0019350051879882812)

INS = ["L0_attn_x", "L0_attn_pos_phases", "L0_attn_Wpv", "L0_attn_bpv", "L0_attn_Wk", "L0_attn_bk",
       "L0_attn_Wkv", "L0_attn_bkv", "L0_attn_Wg1", "L0_attn_bg1", "L0_attn_Wg2", "L0_attn_bg2",
       "L0_attn_Wb1", "L0_attn_bb1", "L0_attn_Wb2", "L0_attn_bb2", "L0_attn_ln_g", "L0_attn_ln_b",
       "L0_attn_Wo", "L0_attn_bo", "L0_ffn_weight", "L0_ffn_alpha", "L0_ffn_bias", "L1_attn_Wq",
       "L1_attn_Wv", "L1_attn_q_norm_w", "L1_attn_v_norm_w", "L1_ffn_ln1_g", "L1_ffn_ln1_b",
       "L1_ffn_ln2_g", "L1_ffn_ln2_b", "L1_ffn_Wq", "L1_ffn_Wk", "L1_ffn_Wv", "L1_ffn_Wo",
       "L1_ffn_Wg", "L1_ffn_W1", "L1_ffn_b1", "L1_ffn_W2", "L1_ffn_b2"]


class Signal:

    def __init__(self, sem, each, stands_at=0):
        self.sem, self.each, self.stands_at, self.before = sem, each, stands_at, stands_at

    def at(self, b, n=None):
        n = self.each if n is None else n
        return (b if self.each == 1 else b * self.each) + (self.before + n)


class Turn:

    def __init__(self, step, k):
        self.step, self.sem, self.k = step, step.sem, k

    def at(self, b):
        return self.step.at(b, self.k)


class Signals:

    def __init__(self, nc, ctx, prefix, spare=()):
        self.nc, self.ctx, self.prefix, self.found, self.runs = nc, ctx, prefix, {}, 0
        self.spare = list(spare)

    def run(self):
        for s in self.found.values():
            s.before = s.stands_at + self.runs * B * s.each
        self.runs += 1
        return self

    def __call__(self, name, each=1):
        if name not in self.found:
            if self.spare:
                sem, stands_at = self.spare.pop(0)
            else:
                sem, stands_at = self.ctx.enter_context(self.nc.semaphore(self.prefix + name)), 0
            self.found[name] = Signal(sem, each, stands_at)
        return self.found[name]


class Memory:
    pass


def tile3(ap, n=NT):
    return ap.rearrange("p (t f) -> p t f", t=n)


def wide(ap, n):
    return ap.unsqueeze(2).to_broadcast([ap.shape[0], ap.shape[1], n])


def again(ap, n):
    return ap.unsqueeze(1).to_broadcast([ap.shape[0], n, ap.shape[1]])


def fence(dve, m, cell=0):
    dve.memset(m.fence[:, cell:cell + 1], 0.0)


def pool_fence(pool, m, cell):
    pool.tensor_tensor(m.pool_fence[:, cell:cell + 1], m.eps[0:1, 0:1], m.eps[0:1, 0:1], ALU.add)


def layer_stats(dve, m, src, st, mv, stats_done, mv_done, b, cell=0):
    fence(dve, m, cell)
    for i in range(NT):
        nc_stats = dve.bn_stats(st[:, i, :], src[:, i, :])
    nc_stats.then_inc(stats_done.sem, 1)
    dve.wait_ge(stats_done.sem, stats_done.at(b))
    fence(dve, m, cell + 1)
    for i in range(NT):
        agg = dve.bn_aggr(mv[:, i, :], st[:, i, :])
    agg.then_inc(mv_done.sem, 1)


def normalise(dve, dst, src, mv, rstd):
    for i in range(NT):
        last = dve.tensor_scalar(dst[:, i, :], src[:, i, :], mv[:, i, 0:1], rstd[:, i:i + 1],
                                 ALU.subtract, ALU.mult)
    return last


def transpose_tiles(pe, out, src, ident, n=NT):
    for i in range(n):
        last = pe.transpose(out[:, i * P:(i + 1) * P], src[:, i, :], ident)
    return last


def phase_load(nc, a, m, keep_ctx):
    with ExitStack() as ctx:
        def sb(name, shape, dt):
            return ctx.enter_context(nc.sbuf_tensor(name, shape, dt))

        def sem(name):
            return keep_ctx.enter_context(nc.semaphore(name))

        bank = [ctx.enter_context(nc.psum_tensor(f"ld_bank{i}", [P, 512], F32)) for i in range(8)]
        w_raw = sb("w_raw", [P, D], F32)
        w_abs = sb("w_abs", [P, D], F32)
        w_row = sb("w_row", [P, 1], F32)
        w_pos = sb("w_pos", [P, D], F32)
        w_neg = sb("w_neg", [P, D], F32)
        mean_w = sb("mean_w", [P, P], F32)
        delta = sb("delta", [P, 2], F32)
        alpha = sb("alpha", [P, 1], F32)
        phases = sb("phases", [P, NT, D], F32)
        turns = sb("turns", [P, S], F32)
        arg_sin = sb("arg_sin", [P, S], F32)
        arg_cos = sb("arg_cos", [P, S], F32)
        wrap = sb("wrap", [P, S], F32)
        lin_raw = sb("lin_raw", [P, 2, D], F32)
        wg2 = sb("wg2", [P, 1], F32)
        wb2 = sb("wb2", [D // 2, 2], F32)
        wb2_diff = sb("wb2_diff", [D // 2, 1], F32)
        bb2 = sb("bb2", [P, 2], F32)
        b1_raw = sb("b1_raw", [E * NF, P], F32)

        loaded = sem("loaded")
        pool_done = sem("ld_pool_done")
        dve_done = sem("ld_dve_done")
        abs_done = sem("abs_done")
        mean_ps = sem("mean_ps")
        phases_ps = sem("phases_ps")
        weff_ps = sem("weff_ps")
        lin_ps = sem("lin_ps")
        sin_args = sem("sin_args")
        tables = sem("tables")

        loads, late_loads = [], []

        def load(dst, src):
            loads.append((dst, src))

        def load_late(dst, src):
            late_loads.append((dst, src))

        def column(dst, src):
            load_late(dst, src.unsqueeze(1))

        load(w_raw[:, :], a["L0_ffn_weight"])
        load(phases[:, :, :], a["L0_attn_pos_phases"][0:S, :].rearrange("(t p) d -> p t d", p=P))
        load(alpha[:, :], a["L0_ffn_alpha"].partition_broadcast(P))
        load(m.x[:, :, :], a["L0_attn_x"].rearrange("b (t p) d -> p (b t) d", p=P))
        load(lin_raw[:, 0, :], a["L1_attn_Wq"])
        load(lin_raw[:, 1, :], a["L1_attn_Wv"])
        load(wg2[:, :], a["L0_attn_Wg2"])
        load(wb2[:, :], a["L0_attn_Wb2"])
        load(bb2[:, :], a["L0_attn_bb2"].partition_broadcast(P))
        load_late(m.w_pv[:, :], a["L0_attn_Wpv"])
        load_late(m.w_k[:, :], a["L0_attn_Wk"])
        load_late(m.w_kv[:, :], a["L0_attn_Wkv"])
        load_late(m.w_g1[:, :, :], a["L0_attn_Wg1"].rearrange("(s d) n -> d s n", s=2))
        load_late(m.w_b1[:, :], a["L0_attn_Wb1"])
        load_late(m.w_o[:, :], a["L0_attn_Wo"])
        column(m.b_pv[:, :], a["L0_attn_bpv"])
        column(m.b_k[:, :], a["L0_attn_bk"])
        column(m.b_kv[:, :], a["L0_attn_bkv"])
        column(m.b_g1[:, :], a["L0_attn_bg1"])
        column(m.b_b1[:, :], a["L0_attn_bb1"])
        column(m.ln_g[:, :], a["L0_attn_ln_g"])
        column(m.ln_b[:, :], a["L0_attn_ln_b"])
        column(m.ln1_g[:, :], a["L1_ffn_ln1_g"])
        column(m.ln1_b[:, :], a["L1_ffn_ln1_b"])
        column(m.ln2_g[:, :], a["L1_ffn_ln2_g"])
        column(m.ln2_b[:, :], a["L1_ffn_ln2_b"])
        load(m.half_bg2[:, :], a["L0_attn_bg2"].partition_broadcast(P))
        load(m.ffn_bias[:, :], a["L0_ffn_bias"].partition_broadcast(P))
        load_late(m.bo[:, :], a["L0_attn_bo"].partition_broadcast(P))
        load_late(m.norm_w[:, 0:D], a["L1_attn_q_norm_w"].rearrange("h d -> (h d)").partition_broadcast(P))
        load_late(m.norm_w[:, D:2 * D], a["L1_attn_v_norm_w"].rearrange("h d -> (h d)").partition_broadcast(P))
        load_late(m.w_qkv[:, 0:D], a["L1_ffn_Wq"])
        load_late(m.w_qkv[:, D:2 * D], a["L1_ffn_Wk"])
        load_late(m.w_qkv[:, 2 * D:3 * D], a["L1_ffn_Wv"])
        load_late(m.w_out[:, :], a["L1_ffn_Wo"])
        load_late(m.w_gate[:, :], a["L1_ffn_Wg"])
        load(b1_raw[:, :], a["L1_ffn_b1"].rearrange("e (c p) -> (e c) p", p=P))
        load_late(m.b2[:, :], a["L1_ffn_b2"])

        m.late_count = 16 * len(late_loads)
        block = ctx.enter_context(nc.Block())

        @block.sync
        def _(sp):
            for dst, src in loads:
                sp.dma_start(dst, src).then_inc(loaded, 16)
            for dst, src in late_loads:
                sp.dma_start(dst, src).then_inc(m.late_loaded, 16)
            sp.wait_ge(loaded, 16 * len(loads))

        @block.gpsimd
        def _(pool):
            pool.memset(m.ident[:, :], 0.0).then_inc(pool_done, 1)
            pool.wait_ge(pool_done, 1)
            pool.affine_select(out=m.ident[:, :], in_=m.ident[:, :], compare_op=ALU.not_equal, fill=1.0,
                               base=0, pattern=[[-1, P]], channel_multiplier=1).then_inc(pool_done, 1)
            pool.wait_ge(pool_done, 2)
            pool.tensor_copy(m.ident_bf[:, :], m.ident[:, :]).then_inc(pool_done, 1)
            pool.memset(m.causal[:, :], 1.0).then_inc(pool_done, 1)
            pool.wait_ge(pool_done, 4)
            pool.affine_select(out=m.causal[:, :], in_=m.causal[:, :], compare_op=ALU.is_ge, fill=0.0,
                               base=0, pattern=[[1, P]], channel_multiplier=-1).then_inc(pool_done, 1)
            pool.iota(m.expert_id[:, :], pattern=[[1, E]], base=0, channel_multiplier=0,
                      allow_small_or_imprecise_dtypes=True).then_inc(pool_done, 1)
            pool.memset(mean_w[:, :], 0.7 / (D * D)).then_inc(pool_done, 1)
            pool.memset(m.half_pow[:, :, :], -0.5).then_inc(pool_done, 1)
            pool.memset(m.eps[:, :], EPS).then_inc(pool_done, 1)
            pool.memset(m.zero_bf[:, :], 0.0).then_inc(pool_done, 1)
            pool.memset(m.u_t[:, :, 0:1], 0.0).then_inc(pool_done, 1)
            pool.memset(m.key_cos[:, :, 0:1], 0.0).then_inc(pool_done, 1)
            pool.memset(m.key_sin[:, :, 0:1], 0.0).then_inc(pool_done, 1)
            pool.memset(m.half_pi[:, :], float(np.pi / 2)).then_inc(pool_done, 1)
            for p in range(2):
                pool.memset(m.v_wide[:, p, :, :, :], 0.0).then_inc(pool_done, 1)
            pool.wait_ge(pool_done, 16)
            for p in range(2):
                pool.memset(m.v_wide[:, p, :, :, DH:DH + 1], 1.0).then_inc(pool_done, 1)
            pool.memset(m.kz[:, 1, :, :, :], 0.0).then_inc(pool_done, 1)
            pool.wait_ge(pool_done, 19)

        @block.vector
        def _(dve):
            count = [0]

            def then(ins):
                count[0] += 1
                ins.then_inc(dve_done, 1)
                dve.wait_ge(dve_done, count[0])

            then(dve.memset(m.zeros[:, :], 0.0))
            then(dve.memset(m.ones[:, :], 1.0))
            for p in range(2):
                dve.memset(m.q_split[:, p, :, :, :], 0.0)
            dve.memset(m.kz[:, 0, :, :, :], 0.0)
            then(dve.memset(m.k_split[:, :, :, :], 0.0))
            then(dve.memset(m.k_split[:, :, :, 24:26], 1.0))
            dve.wait_ge(loaded, 16 * len(loads))
            dve.wait_ge(mean_ps, 1)
            then(dve.tensor_copy(delta[:, 0:1], bank[0][:, 0:1]))
            then(dve.tensor_scalar(delta[:, 1:2], delta[:, 0:1], -1.0, None, ALU.mult))
            then(dve.tensor_scalar(w_pos[:, :], w_raw[:, :], delta[:, 0:1], None, ALU.is_gt))
            then(dve.tensor_scalar(w_neg[:, :], w_raw[:, :], delta[:, 1:2], None, ALU.is_lt))
            then(dve.tensor_tensor(w_pos[:, :], w_pos[:, :], w_neg[:, :], ALU.subtract))
            then(dve.tensor_scalar(w_raw[:, :], w_pos[:, :], alpha[:, 0:1], None, ALU.mult))
            dve.wait_ge(weff_ps, 1)
            then(dve.tensor_copy(m.w_eff[:, :], bank[1][:, 0:P]))
            dve.wait_ge(lin_ps, 1)
            then(dve.tensor_copy(m.w_lin[:, :], bank[2][:, 0:2 * D]))
            then(dve.tensor_copy(m.b1[:, :, :], bank[2][:, 2 * P:2 * P + E * NF].rearrange("p (e c) -> p e c", e=E)))
            then(dve.tensor_scalar(m.w_g2[:, :], m.ones[:, 0:P], wg2[:, 0:1], None, ALU.mult))
            then(dve.tensor_tensor(wb2_diff[:, :], wb2[:, 0:1], wb2[:, 1:2], ALU.subtract))
            then(dve.tensor_scalar(m.w_b2[:, :], m.ones[0:D // 2, 0:P], wb2_diff[:, 0:1], None, ALU.mult))
            then(dve.tensor_tensor(m.half_bb2[:, :], bb2[:, 0:1], bb2[:, 1:2], ALU.subtract))
            then(dve.tensor_scalar(m.half_bb2[:, :], m.half_bb2[:, :], 0.5, None, ALU.mult))
            then(dve.tensor_scalar(m.half_bg2[:, :], m.half_bg2[:, :], 0.5, None, ALU.mult))
            then(dve.tensor_scalar(m.half_bias[:, :], m.ffn_bias[:, :], 0.5, None, ALU.mult))
            dve.wait_ge(phases_ps, 1)
            for arg, quarter in ((arg_sin, 0.0), (arg_cos, float(np.pi / 2))):
                then(dve.tensor_scalar(turns[:, :], bank[3][:, :], float(1 / (2 * np.pi)), MAGIC,
                                       ALU.mult, ALU.add))
                then(dve.tensor_scalar(turns[:, :], turns[:, :], MAGIC, None, ALU.subtract))
                then(dve.scalar_tensor_tensor(out=arg[:, :], in0=turns[:, :], scalar=-TWO_PI_HI,
                                              in1=bank[3][:, :], op0=ALU.mult, op1=ALU.add))
                then(dve.scalar_tensor_tensor(out=arg[:, :], in0=turns[:, :], scalar=-TWO_PI_MID,
                                              in1=arg[:, :], op0=ALU.mult, op1=ALU.add))
                then(dve.scalar_tensor_tensor(out=arg[:, :], in0=turns[:, :], scalar=-TWO_PI_LO,
                                              in1=arg[:, :], op0=ALU.mult, op1=ALU.add))
                if quarter:
                    then(dve.tensor_scalar(arg[:, :], arg[:, :], quarter, None, ALU.add))
                    then(dve.tensor_scalar(wrap[:, :], arg[:, :], PI, -2 * float(np.pi), ALU.is_gt, ALU.mult))
                    then(dve.tensor_tensor(arg[:, :], arg[:, :], wrap[:, :], ALU.add))
                then(dve.tensor_scalar(arg[:, :], arg[:, :], PI, -PI, ALU.min, ALU.max))
            dve.nop().then_inc(sin_args, 1)

        @block.scalar
        def _(act):
            act.wait_ge(loaded, 16 * len(loads))
            act.activation(w_abs[:, :], w_raw[:, :], ACT.Abs, accum_out=w_row[:, 0:1]).then_inc(abs_done, 1)
            act.wait_ge(sin_args, 1)
            act.activation(m.pos_sin[:, :], arg_sin[:, :], ACT.Sin).then_inc(tables, 1)
            act.activation(m.pos_cos[:, :], arg_cos[:, :], ACT.Sin).then_inc(tables, 1)

        @block.tensor
        def _(pe):
            pe.wait_ge(pool_done, 14)
            pe.wait_ge(abs_done, 1)
            pe.matmul(bank[0][:, 0:1], mean_w[:, :], w_row[:, :], start=True, stop=True).then_inc(mean_ps, 1)
            pe.wait_ge(loaded, 16 * len(loads))
            for i in range(NT):
                last = pe.transpose(bank[3][:, i * P:(i + 1) * P], phases[:, i, :], m.ident[:, :])
            last.then_inc(phases_ps, 1)
            for i in range(2):
                last = pe.transpose(bank[2][:, i * P:(i + 1) * P], lin_raw[:, i, :], m.ident[:, :])
            pe.transpose(bank[2][:, 2 * P:2 * P + E * NF], b1_raw[:, :], m.ident[0:E * NF, 0:E * NF])\
                .then_inc(lin_ps, 1)
            pe.wait_ge(dve_done, 10)
            pe.transpose(bank[1][:, 0:P], w_raw[:, :], m.ident[:, :]).then_inc(weff_ps, 1)


def phase_mixer(nc, a, m, signal):
    with ExitStack() as ctx:
        def sb(name, shape, dt=F32):
            return [ctx.enter_context(nc.sbuf_tensor(f"mx_{name}{s}", shape, dt)) for s in range(2)]

        bank = [[ctx.enter_context(nc.psum_tensor(f"mx_bank{s}{i}", [P, 512], F32)) for i in range(4)]
                for s in range(2)]
        st = sb("st", [P, NT, 6])
        mv = sb("mv", [P, NT, 2])
        rstd = sb("rstd", [P, NT])
        var = sb("var", [P, NT])
        z = sb("z", [P, NT, D])
        u = sb("u", [P, NT, D])
        pv = sb("pv", [P, S])
        kt = sb("kt", [P, S])
        kv = sb("kv", [P, S])
        gh = sb("gh", [P, S])
        bh = sb("bh", [D // 2, S])
        gate = sb("gate", [P, S])
        cos_in = sb("cos_in", [P, S])
        sin_in = sb("sin_in", [P, S])
        pos_c = sb("pos_c", [P, S])
        pos_s = sb("pos_s", [P, S])
        key_c = sb("key_c", [P, S])
        key_s = sb("key_s", [P, S])
        gm = sb("gm", [P, NT])
        gp = sb("gp", [P, NT])
        w0 = sb("w0", [P, NT])
        w1 = sb("w1", [P, NT])
        w1g = sb("w1g", [P, NT])
        w1_raw = ctx.enter_context(nc.sbuf_tensor("mx_w1_raw", [P, 1, F], F32))
        w2_raw = ctx.enter_context(nc.sbuf_tensor("mx_w2_raw", [P, 1, NF, D], F32))

        LN = ("a", "u", "bl", "c")

        used = []

        def each_slot(name, each=1):
            used.extend(f"{name}{s}" for s in range(2))
            return [signal(f"{name}{s}", each) for s in range(2)]

        def turns(name, keys):
            return [{k: Turn(step, i + 1) for i, k in enumerate(keys)}
                    for step in each_slot(name, len(keys))]

        stats = turns("stats", LN)
        mv_done = turns("mv", LN)
        var_done = turns("var", LN)
        rstd_done = turns("rstd", LN)
        z_done = turns("z", LN)
        zt_ps = turns("zt_ps", LN)
        zt_done = turns("zt", LN)
        biased = turns("biased", ("a", "c"))
        ffn_ps = turns("ffn_ps", ("a", "c"))
        x1_done = each_slot("x1")
        x3_done = each_slot("x3")
        proj_ps = each_slot("proj_ps", 5)
        gh_done = each_slot("gh", 2)
        gate_ps = each_slot("gate_ps", 2)
        gt_done = each_slot("gt", 2)
        kt_done = each_slot("kt")
        pv_done = each_slot("pv")
        kv_done = each_slot("kv")
        kabs_done = each_slot("kabs")
        key_done = each_slot("key", 2)
        vg_done = each_slot("vg")
        pos_in = each_slot("pos_in", 2)
        pos_mem = each_slot("pos_mem", 2)
        pos_mul = each_slot("pos_mul", 2)
        pos_done = each_slot("pos")
        gcum_done = each_slot("gcum")
        kvg_done = each_slot("kvg")
        key_in = each_slot("key_in", 2)
        key_mem = each_slot("key_mem", 2)
        key_mul = each_slot("key_mul", 2)
        kvr_done = each_slot("kvr")
        scal_ps = each_slot("scal_ps")
        scal_done = each_slot("scal", 3)
        gp_done = each_slot("gp")
        w1g_done = each_slot("w1g")
        ret_ps = each_slot("ret_ps", 2)
        pw_done = each_slot("pw")
        bl_done = each_slot("bl_sum")
        out_ps = each_slot("out_ps")
        xu_done = each_slot("xu")
        xub_done = each_slot("xub")
        x2_done = each_slot("x2")
        w_loaded = signal("w_loaded", 32)
        w_hi_done = signal("w_hi", 2)
        w_lo_done = signal("w_lo", 2)
        block = ctx.enter_context(nc.Block())

        def rows(b, s):
            return m.x[:, bass.ds((b * 2 + s) * NT, NT), :]

        @block.sync
        def _(sp):
            def load_expert(e):
                sp.dma_start(w1_raw[:, :, :], a["L1_ffn_W1"][bass.ds(e, 1), :, :].rearrange("e d f -> d e f"))\
                    .then_inc(w_loaded.sem, 16)
                sp.dma_start(w2_raw[:, :, :, :],
                             a["L1_ffn_W2"][bass.ds(e, 1), :, :].rearrange("e (c p) d -> p e c d", p=P))\
                    .then_inc(w_loaded.sem, 16)

            sp.wait_ge(m.late_loaded, m.late_count)
            load_expert(0)
            with sp.Fori(1, E) as e:
                sp.wait_ge(w_lo_done.sem, w_lo_done.at(e, 0))
                load_expert(e)

        @block.gpsimd
        def _(pool):
            def inverse_root(k, b, s):
                pool.wait_ge(mv_done[s][k].sem, mv_done[s][k].at(b))
                pool.tensor_tensor(var[s][:, :], mv[s][:, :, 1], m.eps[:, :], ALU.add)\
                    .then_inc(var_done[s][k].sem, 1)
                pool.wait_ge(var_done[s][k].sem, var_done[s][k].at(b))
                pool.tensor_tensor(rstd[s][:, :], var[s][:, :], m.half_pow[:, 0, :], ALU.pow)\
                    .then_inc(rstd_done[s][k].sem, 1)

            def half_bias(k, b, s):
                pool.wait_ge(z_done[s][k].sem, z_done[s][k].at(b))
                pool_fence(pool, m, (0 if k == "a" else 2) + s)
                pool.tensor_tensor(rows(b, s), rows(b, s), again(m.half_bias[:, :], NT), ALU.add)\
                    .then_inc(biased[s][k].sem, 1)

            def add_norm(b, s):
                pool.wait_ge(z_done[s]["u"].sem, z_done[s]["u"].at(b))
                pool_fence(pool, m, 4 + s)
                pool.tensor_tensor(rows(b, s), rows(b, s), u[s][:, :, :], ALU.add).then_inc(xu_done[s].sem, 1)

            def add_bias(b, s):
                pool.wait_ge(xu_done[s].sem, xu_done[s].at(b))
                pool_fence(pool, m, 6 + s)
                pool.tensor_tensor(rows(b, s), rows(b, s), again(m.bo[:, :], NT), ALU.add)\
                    .then_inc(xub_done[s].sem, 1)

            def key_weight(b, s):
                pool.wait_ge(scal_done[s].sem, scal_done[s].at(b))
                pool.tensor_tensor(gp[s][:, :], gm[s][:, :], m.half_pow[:, 0, :], ALU.pow).then_inc(gp_done[s].sem, 1)
                pool.wait_ge(gp_done[s].sem, gp_done[s].at(b))
                pool.tensor_tensor(w1g[s][:, :], w1[s][:, :], gp[s][:, :], ALU.mult).then_inc(w1g_done[s].sem, 1)

            def split_expert(e, slot):
                w1_full = w1_raw[:, :, :].rearrange("p e (c d) -> p (e c) d", d=D)
                w2_full = w2_raw[:, :, :, :].rearrange("p e c d -> p (e c) d")
                parts = [w[:, bass.ds(e, 1), :].rearrange("p e (c d) -> p (e c) d", d=D)
                         for w in (m.w1_hi, m.w1_lo, m.w2_hi, m.w2_lo)]
                pool.wait_ge(w_loaded.sem, w_loaded.at(e))
                pool_fence(pool, m, 8 + slot)
                pool.tensor_tensor(parts[0], w1_full, again(m.zero_bf[:, :], NF), ALU.add).then_inc(w_hi_done.sem, 1)
                pool.tensor_tensor(parts[2], w2_full, again(m.zero_bf[:, :], NF), ALU.add).then_inc(w_hi_done.sem, 1)
                pool.wait_ge(w_hi_done.sem, w_hi_done.at(e))
                pool_fence(pool, m, 10 + slot)
                pool.tensor_tensor(parts[1], w1_full, parts[0], ALU.subtract).then_inc(w_lo_done.sem, 1)
                pool.tensor_tensor(parts[3], w2_full, parts[2], ALU.subtract).then_inc(w_lo_done.sem, 1)

            pool.wait_ge(m.late_loaded, m.late_count)
            with pool.Fori(0, B // 2) as b:
                for s in range(2):
                    inverse_root("a", b, s)
                for s in range(2):
                    half_bias("a", b, s)
                for s in range(2):
                    inverse_root("u", b, s)
                for s in range(2):
                    add_norm(b, s)
                for s in range(2):
                    add_bias(b, s)
                split_expert(b * 2, 0)
                for s in range(2):
                    key_weight(b, s)
                for s in range(2):
                    inverse_root("bl", b, s)
                for s in range(2):
                    inverse_root("c", b, s)
                for s in range(2):
                    half_bias("c", b, s)
                split_expert(b * 2 + 1, 1)

        @block.vector
        def _(dve):
            def norm_stats(k, src, b, s):
                layer_stats(dve, m, src, st[s], mv[s], stats[s][k], mv_done[s][k], b, 2 * s)

            def norm_apply(k, src, dst, b, s):
                dve.wait_ge(rstd_done[s][k].sem, rstd_done[s][k].at(b))
                normalise(dve, dst, src, mv[s], rstd[s]).then_inc(z_done[s][k].sem, 1)

            def stats_a(b, s):
                norm_stats("a", rows(b, s), b, s)

            def norm_a(b, s):
                norm_apply("a", rows(b, s), z[s], b, s)

            def add_first_ffn(b, s):
                dve.wait_ge(ffn_ps[s]["a"].sem, ffn_ps[s]["a"].at(b))
                dve.wait_ge(biased[s]["a"].sem, biased[s]["a"].at(b))
                dve.scalar_tensor_tensor(out=rows(b, s), in0=tile3(bank[s][1][:, :]), scalar=0.5,
                                         in1=rows(b, s), op0=ALU.mult, op1=ALU.add).then_inc(x1_done[s].sem, 1)

            def stats_u(b, s):
                dve.wait_ge(x1_done[s].sem, x1_done[s].at(b))
                norm_stats("u", rows(b, s), b, s)

            def norm_u(b, s):
                norm_apply("u", rows(b, s), u[s], b, s)

            def position_inputs(b, s):
                dve.wait_ge(pv_done[s].sem, pv_done[s].at(b))
                dve.tensor_tensor(cos_in[s][:, :], pv[s][:, :], m.pos_cos[:, :], ALU.mult).then_inc(pos_in[s].sem, 1)
                dve.tensor_tensor(sin_in[s][:, :], pv[s][:, :], m.pos_sin[:, :], ALU.mult).then_inc(pos_in[s].sem, 1)

            def position_sums(b, s):
                dve.wait_ge(pos_in[s].sem, pos_in[s].at(b))
                dve.tensor_tensor_scan(pos_c[s][:, :], m.zeros[:, :], cos_in[s][:, :], 0.0, ALU.add, ALU.add)\
                    .then_inc(pos_mem[s].sem, 1)
                dve.tensor_tensor_scan(pos_s[s][:, :], m.zeros[:, :], sin_in[s][:, :], 0.0, ALU.add, ALU.add)\
                    .then_inc(pos_mem[s].sem, 1)

            def position_products(b, s):
                dve.wait_ge(pos_mem[s].sem, pos_mem[s].at(b))
                dve.tensor_tensor(cos_in[s][:, :], pos_c[s][:, :], m.pos_cos[:, :], ALU.mult)\
                    .then_inc(pos_mul[s].sem, 1)
                dve.tensor_tensor(sin_in[s][:, :], pos_s[s][:, :], m.pos_sin[:, :], ALU.mult)\
                    .then_inc(pos_mul[s].sem, 1)

            def position_retrieval(b, s):
                dve.wait_ge(pos_mul[s].sem, pos_mul[s].at(b))
                dve.tensor_tensor(pos_c[s][:, :], cos_in[s][:, :], sin_in[s][:, :], ALU.add)\
                    .then_inc(pos_done[s].sem, 1)

            def value_gate(b, s):
                dve.wait_ge(gt_done[s].sem, gt_done[s].at(b, 1))
                dve.tensor_scalar(gate[s][:, :], gate[s][:, :], 0.5, 0.5, ALU.mult, ALU.add)\
                    .then_inc(vg_done[s].sem, 1)

            def gated_values(b, s):
                dve.wait_ge(vg_done[s].sem, vg_done[s].at(b))
                dve.wait_ge(kv_done[s].sem, kv_done[s].at(b))
                dve.tensor_tensor(kv[s][:, :], kv[s][:, :], gate[s][:, :], ALU.mult).then_inc(kvg_done[s].sem, 1)

            def gate_sum(b, s):
                dve.tensor_tensor_scan(gh[s][0:1, :], m.zeros[0:1, :], gate[s][0:1, :], 0.0, ALU.add, ALU.add)\
                    .then_inc(gcum_done[s].sem, 1)

            def key_inputs(b, s):
                dve.wait_ge(kvg_done[s].sem, kvg_done[s].at(b))
                dve.wait_ge(key_done[s].sem, key_done[s].at(b))
                dve.tensor_tensor(cos_in[s][:, :], kv[s][:, :], m.key_cos[:, s, 0:S], ALU.mult)\
                    .then_inc(key_in[s].sem, 1)
                dve.tensor_tensor(sin_in[s][:, :], kv[s][:, :], m.key_sin[:, s, 0:S], ALU.mult)\
                    .then_inc(key_in[s].sem, 1)

            def key_sums(b, s):
                dve.wait_ge(key_in[s].sem, key_in[s].at(b))
                dve.tensor_tensor_scan(key_c[s][:, :], m.zeros[:, :], cos_in[s][:, :], 0.0, ALU.add, ALU.add)\
                    .then_inc(key_mem[s].sem, 1)
                dve.tensor_tensor_scan(key_s[s][:, :], m.zeros[:, :], sin_in[s][:, :], 0.0, ALU.add, ALU.add)\
                    .then_inc(key_mem[s].sem, 1)

            def key_products(b, s):
                dve.wait_ge(key_mem[s].sem, key_mem[s].at(b))
                dve.tensor_tensor(cos_in[s][:, :], key_c[s][:, :], m.key_cos[:, s, 1:S + 1], ALU.mult)\
                    .then_inc(key_mul[s].sem, 1)
                dve.tensor_tensor(sin_in[s][:, :], key_s[s][:, :], m.key_sin[:, s, 1:S + 1], ALU.mult)\
                    .then_inc(key_mul[s].sem, 1)

            def key_retrieval(b, s):
                dve.wait_ge(key_mul[s].sem, key_mul[s].at(b))
                dve.tensor_tensor(key_c[s][:, :], cos_in[s][:, :], sin_in[s][:, :], ALU.add)\
                    .then_inc(kvr_done[s].sem, 1)

            def token_weights(b, s):
                dve.wait_ge(scal_ps[s].sem, scal_ps[s].at(b))
                dve.tensor_scalar(gm[s][:, :], bank[s][3][:, 0:NT], 1.0, None, ALU.max).then_inc(scal_done[s].sem, 1)
                dve.tensor_scalar(w0[s][:, :], bank[s][3][:, NT:2 * NT], 0.5 * RSQRT_D, 0.5 * RSQRT_D,
                                  ALU.mult, ALU.add).then_inc(scal_done[s].sem, 1)
                dve.tensor_scalar(w1[s][:, :], bank[s][3][:, NT:2 * NT], -0.5 * RSQRT_D, 0.5 * RSQRT_D,
                                  ALU.mult, ALU.add).then_inc(scal_done[s].sem, 1)

            def blend(b, s):
                dve.wait_ge(pw_done[s].sem, pw_done[s].at(b))
                dve.wait_ge(w1g_done[s].sem, w1g_done[s].at(b))
                dve.wait_ge(ret_ps[s].sem, ret_ps[s].at(b))
                for i in range(NT):
                    last = dve.scalar_tensor_tensor(out=z[s][:, i, :], in0=bank[s][2][:, i * P:(i + 1) * P],
                                                    scalar=w1g[s][:, i:i + 1], in1=z[s][:, i, :],
                                                    op0=ALU.mult, op1=ALU.add)
                last.then_inc(bl_done[s].sem, 1)

            def stats_blend(b, s):
                dve.wait_ge(bl_done[s].sem, bl_done[s].at(b))
                norm_stats("bl", z[s], b, s)

            def norm_blend(b, s):
                norm_apply("bl", z[s], z[s], b, s)

            def add_retrieval(b, s):
                dve.wait_ge(out_ps[s].sem, out_ps[s].at(b))
                dve.wait_ge(xub_done[s].sem, xub_done[s].at(b))
                dve.tensor_tensor(rows(b, s), tile3(bank[s][1][:, :]), rows(b, s), ALU.add)\
                    .then_inc(x2_done[s].sem, 1)

            def stats_c(b, s):
                dve.wait_ge(x2_done[s].sem, x2_done[s].at(b))
                norm_stats("c", rows(b, s), b, s)

            def norm_c(b, s):
                norm_apply("c", rows(b, s), z[s], b, s)

            def add_second_ffn(b, s):
                dve.wait_ge(ffn_ps[s]["c"].sem, ffn_ps[s]["c"].at(b))
                dve.wait_ge(biased[s]["c"].sem, biased[s]["c"].at(b))
                dve.scalar_tensor_tensor(out=rows(b, s), in0=tile3(bank[s][3][:, :]), scalar=0.5,
                                         in1=rows(b, s), op0=ALU.mult, op1=ALU.add).then_inc(x3_done[s].sem, 1)

            with dve.Fori(0, B // 2) as b:
                for step in (stats_a, norm_a, add_first_ffn, stats_u, norm_u,
                             position_inputs, position_sums, position_products, position_retrieval,
                             value_gate, gated_values, gate_sum, key_inputs, key_sums, key_products,
                             key_retrieval, token_weights, blend, stats_blend, norm_blend,
                             add_retrieval, stats_c, norm_c, add_second_ffn):
                    for s in range(2):
                        step(b, s)

        @block.scalar
        def _(act):
            def norm_a(b, s):
                act.wait_ge(zt_ps[s]["a"].sem, zt_ps[s]["a"].at(b))
                act.activation(m.u_t[:, s, 1:S + 1], bank[s][0][:, :], ACT.Copy).then_inc(zt_done[s]["a"].sem, 1)

            def norm_u(b, s):
                act.wait_ge(zt_ps[s]["u"].sem, zt_ps[s]["u"].at(b))
                act.activation(m.u_t[:, s, 1:S + 1], bank[s][0][:, :], ACT.Copy).then_inc(zt_done[s]["u"].sem, 1)

            def hidden_gates(b, s):
                act.wait_ge(proj_ps[s].sem, proj_ps[s].at(b, 2))
                act.activation(gh[s][:, :], bank[s][2][:, :], ACT.Gelu, bias=m.b_g1[:, 0:1])\
                    .then_inc(gh_done[s].sem, 1)
                act.wait_ge(proj_ps[s].sem, proj_ps[s].at(b, 3))
                act.activation(bh[s][:, :], bank[s][3][0:D // 2, :], ACT.Gelu, bias=m.b_b1[:, 0:1])\
                    .then_inc(gh_done[s].sem, 1)

            def position_values(b, s):
                act.wait_ge(proj_ps[s].sem, proj_ps[s].at(b, 1))
                act.activation(pv[s][:, :], bank[s][0][:, :], ACT.Identity, bias=m.b_pv[:, 0:1])\
                    .then_inc(pv_done[s].sem, 1)

            def keys(b, s):
                act.wait_ge(proj_ps[s].sem, proj_ps[s].at(b, 4))
                act.activation(kt[s][:, :], bank[s][1][:, :], ACT.Tanh, bias=m.b_k[:, 0:1]).then_inc(kt_done[s].sem, 1)

            def gates(b, s):
                act.wait_ge(gate_ps[s].sem, gate_ps[s].at(b, 1))
                act.activation(gate[s][:, :], bank[s][3][:, :], ACT.Tanh, bias=m.half_bg2[:, 0:1], scale=0.5)\
                    .then_inc(gt_done[s].sem, 1)
                act.wait_ge(gate_ps[s].sem, gate_ps[s].at(b, 2))
                act.activation(bh[s][0:1, :], bank[s][0][0:1, :], ACT.Tanh, bias=m.half_bb2[0:1, 0:1], scale=0.5)\
                    .then_inc(gt_done[s].sem, 1)

            def key_values(b, s):
                act.wait_ge(proj_ps[s].sem, proj_ps[s].at(b, 5))
                act.activation(kv[s][:, :], bank[s][2][:, :], ACT.Identity, bias=m.b_kv[:, 0:1])\
                    .then_inc(kv_done[s].sem, 1)

            def key_size(b, s):
                act.wait_ge(kt_done[s].sem, kt_done[s].at(b))
                act.activation(m.key_cos[:, s, 1:S + 1], kt[s][:, :], ACT.Abs).then_inc(kabs_done[s].sem, 1)

            def key_angles(b, s):
                act.activation(m.key_sin[:, s, 1:S + 1], kt[s][:, :], ACT.Sin, scale=PI).then_inc(key_done[s].sem, 1)
                act.wait_ge(kabs_done[s].sem, kabs_done[s].at(b))
                act.activation(m.key_cos[:, s, 1:S + 1], m.key_cos[:, s, 1:S + 1], ACT.Sin,
                               bias=m.half_pi[:, 0:1], scale=-PI).then_inc(key_done[s].sem, 1)

            def weigh_position(b, s):
                act.wait_ge(ret_ps[s].sem, ret_ps[s].at(b, 1))
                act.wait_ge(scal_done[s].sem, scal_done[s].at(b))
                for i in range(NT):
                    last = act.activation(z[s][:, i, :], bank[s][1][:, i * P:(i + 1) * P], ACT.Copy,
                                          scale=w0[s][:, i:i + 1])
                last.then_inc(pw_done[s].sem, 1)

            def norm_blend(b, s):
                act.wait_ge(zt_ps[s]["bl"].sem, zt_ps[s]["bl"].at(b))
                act.activation(m.u_t[:, s, 1:S + 1], bank[s][0][:, :], ACT.Identity, bias=m.ln_b[:, 0:1],
                               scale=m.ln_g[:, 0:1]).then_inc(zt_done[s]["bl"].sem, 1)

            def norm_c(b, s):
                act.wait_ge(zt_ps[s]["c"].sem, zt_ps[s]["c"].at(b))
                act.activation(m.u_t[:, s, 1:S + 1], bank[s][2][:, :], ACT.Copy).then_inc(zt_done[s]["c"].sem, 1)

            act.wait_ge(m.late_loaded, m.late_count)
            with act.Fori(0, B // 2) as b:
                for step in (norm_a, norm_u, position_values, hidden_gates, key_values, keys, gates, key_size,
                             key_angles, weigh_position, norm_blend, norm_c):
                    for s in range(2):
                        step(b, s)

        @block.tensor
        def _(pe):
            def turn(k, src, out, b, s):
                pe.wait_ge(z_done[s][k].sem, z_done[s][k].at(b))
                transpose_tiles(pe, out, src, m.ident[:, :]).then_inc(zt_ps[s][k].sem, 1)

            def tokens_by(w, out, s):
                for i in range(NT):
                    last = pe.matmul(out[:, i * P:(i + 1) * P], m.u_t[:, s, 1 + i * P:1 + (i + 1) * P], w[:, :],
                                     start=True, stop=True)
                return last

            def turn_a(b, s):
                turn("a", z[s], bank[s][0], b, s)

            def first_ffn(b, s):
                pe.wait_ge(zt_done[s]["a"].sem, zt_done[s]["a"].at(b))
                tokens_by(m.w_eff, bank[s][1], s).then_inc(ffn_ps[s]["a"].sem, 1)

            def turn_u(b, s):
                turn("u", u[s], bank[s][0], b, s)

            def position_projection(b, s):
                pe.wait_ge(zt_done[s]["u"].sem, zt_done[s]["u"].at(b))
                pe.matmul(bank[s][0][:, :], m.w_pv[:, :], m.u_t[:, s, 1:S + 1], start=True, stop=True)\
                    .then_inc(proj_ps[s].sem, 1)

            def gate_projections(b, s):
                cur, shifted = m.u_t[:, s, 1:S + 1], m.u_t[:, s, 0:S]
                pe.matmul(bank[s][2][:, :], m.w_g1[:, 0, :], cur, start=True, stop=False)
                pe.matmul(bank[s][2][:, :], m.w_g1[:, 1, :], shifted, start=False, stop=True)\
                    .then_inc(proj_ps[s].sem, 1)
                pe.matmul(bank[s][3][0:D // 2, :], m.w_b1[:, :], cur, start=True, stop=True).then_inc(proj_ps[s].sem, 1)

            def value_projections(b, s):
                cur = m.u_t[:, s, 1:S + 1]
                pe.matmul(bank[s][1][:, :], m.w_k[:, :], cur, start=True, stop=True).then_inc(proj_ps[s].sem, 1)
                pe.wait_ge(gh_done[s].sem, gh_done[s].at(b, 1))
                pe.matmul(bank[s][2][:, :], m.w_kv[:, :], cur, start=True, stop=True).then_inc(proj_ps[s].sem, 1)

            def gates(b, s):
                pe.wait_ge(gh_done[s].sem, gh_done[s].at(b, 2))
                pe.matmul(bank[s][3][:, :], m.w_g2[:, :], gh[s][:, :], start=True, stop=True)\
                    .then_inc(gate_ps[s].sem, 1)
                pe.wait_ge(pv_done[s].sem, pv_done[s].at(b))
                pe.matmul(bank[s][0][:, :], m.w_b2[:, :], bh[s][:, :], start=True, stop=True)\
                    .then_inc(gate_ps[s].sem, 1)

            def turn_position(b, s):
                pe.wait_ge(pos_done[s].sem, pos_done[s].at(b))
                pe.wait_ge(kt_done[s].sem, kt_done[s].at(b))
                transpose_tiles(pe, bank[s][1], tile3(pos_c[s][:, :]), m.ident[:, :]).then_inc(ret_ps[s].sem, 1)

            def token_columns(b, s):
                pe.wait_ge(gcum_done[s].sem, gcum_done[s].at(b))
                pe.wait_ge(gt_done[s].sem, gt_done[s].at(b))
                for i in range(NT):
                    pe.matmul(bank[s][3][:, i:i + 1], gh[s][0:1, i * P:(i + 1) * P], m.ones[0:1, 0:1],
                              start=True, stop=True)
                for i in range(NT):
                    last = pe.matmul(bank[s][3][:, NT + i:NT + i + 1], bh[s][0:1, i * P:(i + 1) * P],
                                     m.ones[0:1, 0:1], start=True, stop=True)
                last.then_inc(scal_ps[s].sem, 1)

            def turn_keys(b, s):
                pe.wait_ge(kvr_done[s].sem, kvr_done[s].at(b))
                transpose_tiles(pe, bank[s][2], tile3(key_c[s][:, :]), m.ident[:, :]).then_inc(ret_ps[s].sem, 1)

            def turn_blend(b, s):
                turn("bl", z[s], bank[s][0], b, s)

            def output(b, s):
                pe.wait_ge(zt_done[s]["bl"].sem, zt_done[s]["bl"].at(b))
                tokens_by(m.w_o, bank[s][1], s).then_inc(out_ps[s].sem, 1)

            def turn_c(b, s):
                turn("c", z[s], bank[s][2], b, s)

            def second_ffn(b, s):
                pe.wait_ge(zt_done[s]["c"].sem, zt_done[s]["c"].at(b))
                tokens_by(m.w_eff, bank[s][3], s).then_inc(ffn_ps[s]["c"].sem, 1)

            pe.wait_ge(m.late_loaded, m.late_count)
            with pe.Fori(0, B // 2) as b:
                for step in (turn_a, first_ffn, turn_u, position_projection, gate_projections, value_projections, gates,
                             turn_position, token_columns, turn_keys, turn_blend, output, turn_c,
                             second_ffn):
                    for s in range(2):
                        step(b, s)

    return [(signal.found[name].sem, signal.found[name].each * (B // 2)) for name in used]


def phase_softmax(nc, m, signal, tag):
    STEPS = NG * 16
    SHIFT_LAG = 7
    VALUE_LAG = (15, 18, 21, 24)
    TAKE, TURN, DIVIDE = 25, 28, 29
    TURN_H, TURN_CTX, OUTPUT, TURN_M = 7, 18, 22, 48
    PROJECT, TURN_KEYS, TURN_QUERIES = (10, 14, 26, 30), (33, 39), (42, 45)
    TURN_SHIFTED = (3, 20, 36, 52)
    with ExitStack() as ctx:
        def sb(name, shape, dt=F32):
            return ctx.enter_context(nc.sbuf_tensor(tag + name, shape, dt))

        raw = [ctx.enter_context(nc.psum_tensor(f"{tag}raw{i}", [P, 512], F32)) for i in range(3)]
        low = [ctx.enter_context(nc.psum_tensor(f"{tag}low{i}", [P, 512], F32)) for i in range(3)]
        av = ctx.enter_context(nc.psum_tensor(tag + "av", [P, 512], F32))
        misc = ctx.enter_context(nc.psum_tensor(tag + "misc", [P, 512], F32))
        misc_bf = misc[:, :].bitcast(BF16)
        head_project = [misc] + raw
        head_turn = [t[:, :].bitcast(BF16) for t in low + [av]]
        st = sb("st", [P, NT, 6])
        mv = sb("mv", [P, NT, 2])
        va = sb("va", [P, 2, NT])
        rs = sb("rs", [P, 2, NT])
        st2 = sb("st2", [P, NT, 6])
        mv2 = sb("mv2", [P, NT, 2])
        va2 = sb("va2", [P, NT])
        rs2 = sb("rs2", [P, NT])
        z = sb("z", [P, NT, D])
        z2 = sb("z2", [P, NT, D])
        centred = sb("centred", [P, NT, D])
        h_t = sb("h_t", [P, S])
        k_t = sb("k_t", [P, NG, S], BF16)
        q1 = sb("q1", [P, 2, NG, S], BF16)
        q2 = sb("q2", [P, 2, S], BF16)
        mx = sb("mx", [P, NT, H])
        prob = sb("prob", [P, 16, S])
        av_s = sb("av_s", [P, S])
        rec = sb("rec", [P, NT, GH])
        ctx_s = sb("ctx_s", [P, NT, D])
        ctx_t = sb("ctx_t", [P, S])

        stats = signal("stats")
        mv_done = signal("mv_done")
        var_done = signal("var_done")
        rstd_done = signal("rstd_done")
        y_done = signal("y_done")
        centred_done = signal("centred")
        centred2_done = signal("centred2")
        z_done = signal("z_done")
        ht_ps = signal("ht_ps")
        ht_done = signal("ht_done")
        qkv_ps = signal("qkv_ps", NT)
        hi_done = signal("hi_done", NT)
        copy_done = signal("copy_done", NT)
        m_zero = signal("m_zero")
        lo_done = signal("lo_done", NT)
        v_done = signal("v_done", NT)
        kt_ps = signal("kt_ps", 2)
        kt_done = signal("kt_done", 2)
        q1_ps = signal("q1_ps", 2)
        q1_done = signal("q1_done", 2)
        kz_done = [signal(f"kz_done{c}", 16 * GH) for c in range(2)]
        s1_ps = signal("s1_ps", STEPS)
        max_done = signal("max_done", STEPS)
        mh_done = signal("mh_done", NG)
        ml_done = signal("ml_done", NG)
        q2_ps = signal("q2_ps", NG)
        q2_done = signal("q2_done", NG)
        s2_ps = signal("s2_ps", STEPS)
        exp_done = signal("exp_done", STEPS)
        av_part = signal("av_part", NG * NT)
        avs_done = signal("avs_done", NG)
        avt_ps = signal("avt_ps", NG)
        rec_done = signal("rec_done", NG)
        ctx_done = signal("ctx_done", NG)
        ct_ps = signal("ct_ps")
        ct_done = signal("ct_done")
        wo_ps = signal("wo_ps")
        y2_done = signal("y2_done")
        stats2 = signal("stats2")
        mv2_done = signal("mv2_done")
        var2_done = signal("var2_done")
        rstd2_done = signal("rstd2_done")
        z2_done = signal("z2_done")
        mt_ps = signal("mt_ps")
        mt_done = signal("mt_done")
        block = ctx.enter_context(nc.Block())

        def bank_of(n):
            return n % 3 if n < STEPS - 1 else 1

        def read_before(n):
            return {0: -3, 1: 0, 2: -1, STEPS - 1: STEPS - 2}.get(n, n - 2)

        def batches(eng, head, body, last):
            head()
            body(0, 0, False, True)
            with eng.Fori(0, (B - 2) // 2) as i:
                body(i * 2 + 1, 1, True, True)
                body(i * 2 + 2, 0, True, True)
            body(B - 1, 1, True, False)
            last()

        @block.sync
        def _(sp):
            def spread(b, p):
                for c in range(2):
                    sp.wait_ge(kt_done.sem, kt_done.at(b, c + 1))
                    for j in range(GH):
                        rows, groups = slice(HC * j, HC * (j + 1)), slice(2 * c, 2 * c + 2)
                        sp.dma_start(m.kz[rows, p, j, groups, :], k_t[rows, groups, :])\
                            .then_inc(kz_done[c].sem, 16)

            spread(0, 0)
            with sp.Fori(0, (B - 2) // 2) as i:
                spread(i * 2 + 1, 1)
                spread(i * 2 + 2, 0)
            spread(B - 1, 1)
            for c in range(2):
                sp.wait_ge(kz_done[c].sem, kz_done[c].at(B - 1))

        @block.gpsimd
        def _(pool):
            def rows(store, b):
                return store[:, bass.ds(b * NT, NT), :]

            def norm_x(b):
                pool.wait_ge(var_done.sem, var_done.at(b))
                pool.tensor_tensor(rs[:, :, :], va[:, :, :], m.half_pow[:, :, :], ALU.pow)\
                    .then_inc(rstd_done.sem, 1)
                pool.tensor_tensor(centred[:, :, :], rows(m.x, b), wide(mv[:, :, 0], D), ALU.subtract)\
                    .then_inc(centred_done.sem, 1)
                pool.wait_ge(rstd_done.sem, rstd_done.at(b))
                pool.wait_ge(centred_done.sem, centred_done.at(b))
                pool.tensor_tensor(z[:, :, :], centred[:, :, :], wide(rs[:, 1, :], D), ALU.mult)\
                    .then_inc(z_done.sem, 1)
                pool.tensor_tensor(rows(m.y, b), centred[:, :, :], wide(rs[:, 0, :], D), ALU.mult)\
                    .then_inc(y_done.sem, 1)

            def copies(b, p):
                for i in range(NT):
                    pool.wait_ge(hi_done.sem, hi_done.at(b, i + 1))
                    pool.tensor_tensor(m.q_split[:, p, i, :, 16:24], m.q_split[:, p, i, :, 0:8],
                                       m.zero_bf[:, :].rearrange("p (h d) -> p h d", d=DH), ALU.add)
                    pool.tensor_copy(m.k_split[:, i, :, 8:16], m.k_split[:, i, :, 0:8]).then_inc(copy_done.sem, 1)

            def head():
                norm_x(0)
                copies(0, 0)

            def norm_y(b):
                pool.wait_ge(var2_done.sem, var2_done.at(b))
                pool.tensor_tensor(rs2[:, :], va2[:, :], m.half_pow[:, 0, :], ALU.pow).then_inc(rstd2_done.sem, 1)
                pool.tensor_tensor(z2[:, :, :], rows(m.y, b), wide(mv2[:, :, 0], D), ALU.subtract)\
                    .then_inc(centred2_done.sem, 1)
                pool.wait_ge(rstd2_done.sem, rstd2_done.at(b))
                pool.wait_ge(centred2_done.sem, centred2_done.at(b))
                pool.tensor_tensor(z2[:, :, :], z2[:, :, :], wide(rs2[:, :], D), ALU.mult)\
                    .then_inc(z2_done.sem, 1)

            def body(b, p, before, behind):
                if behind:
                    norm_x(b + 1)
                    copies(b + 1, 1 - p)
                if before:
                    norm_y(b - 1)

            batches(pool, head, body, lambda: norm_y(B - 1))

        @block.vector
        def _(dve):
            def rows(store, b):
                return store[:, bass.ds(b * NT, NT), :]

            def stats_x(b):
                fence(dve, m)
                for i in range(NT):
                    last = dve.bn_stats(st[:, i, :], rows(m.x, b)[:, i, :])
                last.then_inc(stats.sem, 1)

            def mean_x(b):
                dve.wait_ge(stats.sem, stats.at(b))
                fence(dve, m, 1)
                for i in range(NT):
                    last = dve.bn_aggr(mv[:, i, :], st[:, i, :])
                last.then_inc(mv_done.sem, 1)

            def variances_x(b):
                dve.wait_ge(mv_done.sem, mv_done.at(b))
                dve.tensor_scalar(va[:, 0, :], mv[:, :, 1], EPS, None, ALU.add)
                dve.tensor_scalar(va[:, 1, :], mv[:, :, 1], 1.0 + EPS, EPS * EPS, ALU.mult, ALU.add)\
                    .then_inc(var_done.sem, 1)

            def clear_max(b, p):
                dve.memset(m.q_split[:, p, :, :, 24:26], 0.0).then_inc(m_zero.sem, 1)

            def low_parts(b, p, i, misc=misc):
                dve.wait_ge(hi_done.sem, hi_done.at(b, i + 1))
                heads = lambda lo: misc[:, lo:lo + D].rearrange("p (h d) -> p h d", d=DH)
                dve.scalar_tensor_tensor(out=m.q_split[:, p, i, :, 8:16], in0=heads(0), scalar=SCORE_SCALE,
                                         in1=m.q_split[:, p, i, :, 0:8], op0=ALU.mult, op1=ALU.subtract)
                dve.tensor_tensor(m.k_split[:, i, :, 16:24], heads(D), m.k_split[:, i, :, 0:8],
                                  ALU.subtract).then_inc(lo_done.sem, 1)
                dve.tensor_copy(m.v_wide[:, p, i, :, 0:DH], heads(2 * D)).then_inc(v_done.sem, 1)

            def row_max(b, n):
                g, n = n // 16, n % 16
                dve.wait_ge(s1_ps.sem, s1_ps.at(b, 16 * g + n + 1))
                h = GH * g + n % GH
                dve.tensor_reduce(mx[:, n // GH, h:h + 1], raw[bank_of(16 * g + n)][:, :], AX.X, ALU.max)\
                    .then_inc(max_done.sem, 1)

            def write_max(b, p, g):
                dve.wait_ge(max_done.sem, max_done.at(b, 16 * (g + 1)))
                dve.wait_ge(q1_ps.sem, q1_ps.at(b))
                heads = slice(GH * g, GH * (g + 1))
                dve.tensor_scalar(m.q_split[:, p, :, heads, 24], mx[:, :, heads], -1.0, None, ALU.mult)\
                    .then_inc(mh_done.sem, 1)
                dve.wait_ge(mh_done.sem, mh_done.at(b, g + 1))
                dve.scalar_tensor_tensor(out=m.q_split[:, p, :, heads, 25], in0=mx[:, :, heads], scalar=-1.0,
                                         in1=m.q_split[:, p, :, heads, 24], op0=ALU.mult, op1=ALU.subtract)\
                    .then_inc(ml_done.sem, 1)

            def divide(b, g, before):
                dve.wait_ge(avt_ps.sem, avt_ps.at(b, g + 1))
                t = av[:, :].rearrange("p (t h c) -> p t h c", t=NT, c=HC)
                dve.reciprocal(rec[:, :, :], t[:, :, :, DH]).then_inc(rec_done.sem, 1)
                dve.wait_ge(rec_done.sem, rec_done.at(b, g + 1))
                if g == 0 and before:
                    dve.wait_ge(ct_ps.sem, ct_ps.at(b - 1))
                dve.tensor_tensor(ctx_s[:, :, 32 * g:32 * (g + 1)].rearrange("p t (h d) -> p t h d", d=DH),
                                  t[:, :, :, 0:DH], rec[:, :, :].unsqueeze(3).to_broadcast([P, NT, GH, DH]),
                                  ALU.mult).then_inc(ctx_done.sem, 1)

            def add_output(b):
                dve.wait_ge(wo_ps.sem, wo_ps.at(b))
                dve.wait_ge(y_done.sem, y_done.at(b))
                dve.tensor_tensor(rows(m.y, b), tile3(misc[:, :]), rows(m.y, b), ALU.add)\
                    .then_inc(y2_done.sem, 1)

            def stats_y(b):
                dve.wait_ge(y2_done.sem, y2_done.at(b))
                fence(dve, m, 2)
                for i in range(NT):
                    last = dve.bn_stats(st2[:, i, :], rows(m.y, b)[:, i, :])
                last.then_inc(stats2.sem, 1)

            def mean_y(b):
                dve.wait_ge(stats2.sem, stats2.at(b))
                fence(dve, m, 3)
                for i in range(NT):
                    last = dve.bn_aggr(mv2[:, i, :], st2[:, i, :])
                last.then_inc(mv2_done.sem, 1)

            def variance_y(b):
                dve.wait_ge(mv2_done.sem, mv2_done.at(b))
                dve.tensor_scalar(va2[:, :], mv2[:, :, 1], EPS, None, ALU.add).then_inc(var2_done.sem, 1)

            def head():
                stats_x(0)
                mean_x(0)
                variances_x(0)
                clear_max(0, 0)
                for i in range(NT):
                    low_parts(0, 0, i, head_project[i])
                for n in range(16):
                    row_max(0, n)
                write_max(0, 0, 0)

            def body(b, p, before, behind):
                for t in range(STEPS):
                    if t < STEPS - 16:
                        row_max(b, t + 16)
                    elif behind:
                        row_max(b + 1, t + 16 - STEPS)
                    if behind:
                        if t == 0:
                            stats_x(b + 1)
                        if t == 1:
                            mean_x(b + 1)
                        if t == 2:
                            variances_x(b + 1)
                        if t == 4:
                            clear_max(b + 1, 1 - p)
                        if t - 2 in PROJECT:
                            low_parts(b + 1, 1 - p, PROJECT.index(t - 2))
                    if t % 16 == 15 and t < STEPS - 1:
                        write_max(b, p, t // 16 + 1)
                    if t == STEPS - 1 and behind:
                        write_max(b + 1, 1 - p, 0)
                    if t % 16 == DIVIDE % 16 and (t > 16 or before):
                        g = t // 16 - 1
                        divide(b if g >= 0 else b - 1, g % NG, before)
                    if before:
                        if t == OUTPUT + 2:
                            add_output(b - 1)
                        if t == OUTPUT + 3:
                            stats_y(b - 1)
                        if t == OUTPUT + 4:
                            mean_y(b - 1)
                        if t == OUTPUT + 5:
                            variance_y(b - 1)

            def last():
                divide(B - 1, NG - 1, True)
                add_output(B - 1)
                stats_y(B - 1)
                mean_y(B - 1)
                variance_y(B - 1)

            batches(dve, head, body, last)

        @block.scalar
        def _(act):
            def to_h(b):
                act.wait_ge(ht_ps.sem, ht_ps.at(b))
                act.activation(h_t[:, :], misc[:, :], ACT.Identity, bias=m.ln1_b[:, 0:1],
                               scale=m.ln1_g[:, 0:1]).then_inc(ht_done.sem, 1)

            def high_parts(b, p, i, misc=misc):
                act.wait_ge(qkv_ps.sem, qkv_ps.at(b, i + 1))
                heads = lambda lo: misc[:, lo:lo + D].rearrange("p (h d) -> p h d", d=DH)
                act.activation(m.q_split[:, p, i, :, 0:DH], heads(0), ACT.Copy, scale=SCORE_SCALE)
                act.activation(m.k_split[:, i, :, 0:DH], heads(D), ACT.Copy).then_inc(hi_done.sem, 1)

            def to_kt(b, c, misc_bf=misc_bf):
                act.wait_ge(kt_ps.sem, kt_ps.at(b, c + 1))
                act.activation(k_t[:, 2 * c:2 * c + 2, :], tile3(misc_bf, 2), ACT.Copy).then_inc(kt_done.sem, 1)

            def to_q1(b, p, c, misc_bf=misc_bf):
                act.wait_ge(q1_ps.sem, q1_ps.at(b, c + 1))
                act.activation(q1[:, p, 2 * c:2 * c + 2, :], tile3(misc_bf, 2), ACT.Copy).then_inc(q1_done.sem, 1)

            def to_q2(b, g):
                act.wait_ge(q2_ps.sem, q2_ps.at(b, g + 1))
                act.activation(q2[:, g % 2, :], misc_bf[:, 0:S], ACT.Copy).then_inc(q2_done.sem, 1)

            def exponentials(b, n, first):
                act.wait_ge(s2_ps.sem, s2_ps.at(b, n + 1))
                if n % 4 == 0 and not (first and n < 16):
                    act.wait_ge(av_part.sem, av_part.at(b, (n - 16) // 4 + 1))
                act.activation(prob[:, n % 16, :], low[bank_of(n)][:, :], ACT.Exp).then_inc(exp_done.sem, 1)

            def take_values(b, g):
                act.wait_ge(av_part.sem, av_part.at(b, NT * (g + 1)))
                act.activation(av_s[:, :], av[:, :], ACT.Copy).then_inc(avs_done.sem, 1)

            def to_ctx(b):
                act.wait_ge(ct_ps.sem, ct_ps.at(b))
                act.activation(ctx_t[:, :], misc[:, :], ACT.Copy).then_inc(ct_done.sem, 1)

            def to_m(b):
                act.wait_ge(mt_ps.sem, mt_ps.at(b))
                act.activation(m.m_t[:, bass.ds(b * S, S)], misc[:, :], ACT.Identity, bias=m.ln2_b[:, 0:1],
                               scale=m.ln2_g[:, 0:1]).then_inc(mt_done.sem, 1)

            def head():
                to_h(0)
                for i in range(NT):
                    high_parts(0, 0, i, head_project[i])
                for c in range(2):
                    to_kt(0, c, head_turn[c])
                for c in range(2):
                    to_q1(0, 0, c, head_turn[2 + c])

            def body(b, p, before, behind):
                for t in range(STEPS):
                    n = t - SHIFT_LAG
                    if n >= 0 or before:
                        exponentials(b if n >= 0 else b - 1, n % STEPS, not before)
                    if t % 16 == TAKE % 16 and (t > 16 or before):
                        g = t // 16 - 1
                        take_values(b if g >= 0 else b - 1, g % NG)
                    if t - 1 in TURN_SHIFTED:
                        to_q2(b, TURN_SHIFTED.index(t - 1))
                    if behind:
                        if t - 1 == TURN_H:
                            to_h(b + 1)
                        if t - 1 in PROJECT:
                            high_parts(b + 1, 1 - p, PROJECT.index(t - 1))
                        if t - 1 in TURN_KEYS:
                            to_kt(b + 1, TURN_KEYS.index(t - 1))
                        if t - 1 in TURN_QUERIES:
                            to_q1(b + 1, 1 - p, TURN_QUERIES.index(t - 1))
                    if before:
                        if t - 1 == TURN_CTX:
                            to_ctx(b - 1)
                        if t - 1 == TURN_M:
                            to_m(b - 1)

            def last():
                for n in range(STEPS - SHIFT_LAG, STEPS):
                    exponentials(B - 1, n, False)
                take_values(B - 1, NG - 1)
                to_ctx(B - 1)
                to_m(B - 1)

            batches(act, head, body, last)

        @block.tensor
        def _(pe):
            def h_tiles(b):
                pe.wait_ge(z_done.sem, z_done.at(b))
                transpose_tiles(pe, misc, z, m.ident[:, :]).then_inc(ht_ps.sem, 1)

            def project(b, i, misc=misc):
                pe.wait_ge(ht_done.sem, ht_done.at(b))
                pe.matmul(misc[:, 0:3 * D], h_t[:, i * P:(i + 1) * P], m.w_qkv[:, :],
                          start=True, stop=True).then_inc(qkv_ps.sem, 1)

            def turn(dst, src, g):
                for i in range(NT):
                    last = pe.transpose(dst[:, i * P:(i + 1) * P],
                                        src[:, i, GH * g:GH * (g + 1), :].rearrange("p h c -> p (h c)"),
                                        m.ident_bf[:, :])
                return last

            def turn_keys(b, c, misc_bf=misc_bf):
                pe.wait_ge(lo_done.sem, lo_done.at(b))
                pe.wait_ge(copy_done.sem, copy_done.at(b))
                turn(misc_bf[:, 0:S], m.k_split, 2 * c)
                turn(misc_bf[:, S:2 * S], m.k_split, 2 * c + 1).then_inc(kt_ps.sem, 1)

            def turn_queries(b, p, c, misc_bf=misc_bf):
                pe.wait_ge(m_zero.sem, m_zero.at(b))
                turn(misc_bf[:, 0:S], m.q_split[:, p, :, :, :], 2 * c)
                turn(misc_bf[:, S:2 * S], m.q_split[:, p, :, :, :], 2 * c + 1).then_inc(q1_ps.sem, 1)

            def turn_shifted(b, p, g):
                pe.wait_ge(ml_done.sem, ml_done.at(b, g + 1))
                turn(misc_bf[:, 0:S], m.q_split[:, p, :, :, :], g).then_inc(q2_ps.sem, 1)

            def scores_for_max(b, p, n, first):
                g, i, j = n // 16, n % 16 // GH, n % GH
                if n % 32 == 0:
                    pe.wait_ge(kz_done[g // 2].sem, kz_done[g // 2].at(b))
                pe.wait_ge(q1_done.sem, q1_done.at(b, g // 2 + 1))
                if not (first and n < 3):
                    pe.wait_ge(max_done.sem, max_done.at(b, read_before(n)))
                pe.matmul(raw[bank_of(n)][:, :], q1[:, p, g, i * P:(i + 1) * P], m.kz[:, p, j, g, :],
                          start=True, stop=True).then_inc(s1_ps.sem, 1)

            def scores_shifted(b, p, n, first):
                g, i, j = n // 16, n % 16 // GH, n % GH
                if n % 16 == 0:
                    pe.wait_ge(q2_done.sem, q2_done.at(b, g + 1))
                if not (first and n < 3):
                    pe.wait_ge(exp_done.sem, exp_done.at(b, read_before(n)))
                pe.matmul(low[bank_of(n)][:, :], m.kz[:, p, j, g, i * P:(i + 1) * P], q2[:, g % 2, :],
                          start=True, stop=True).then_inc(s2_ps.sem, 1)

            def values(b, p, g, i, first):
                pe.wait_ge(exp_done.sem, exp_done.at(b, 16 * g + 4 * i + 4))
                if i == 0:
                    if g == 0:
                        pe.wait_ge(v_done.sem, v_done.at(b))
                    if not (first and g == 0):
                        pe.wait_ge(ctx_done.sem, ctx_done.at(b, g))
                for j in range(GH):
                    last = pe.matmul(av[HC * j:HC * (j + 1), :], m.v_wide[:, p, i, GH * g + j, :],
                                     prob[:, GH * i + j, :], start=(i == 0), stop=(i == NT - 1))
                last.then_inc(av_part.sem, 1)

            def turn_values(b, g):
                pe.wait_ge(avs_done.sem, avs_done.at(b, g + 1))
                transpose_tiles(pe, av, tile3(av_s[:, :]), m.ident[:, :]).then_inc(avt_ps.sem, 1)

            def turn_ctx(b):
                pe.wait_ge(ctx_done.sem, ctx_done.at(b))
                transpose_tiles(pe, misc, ctx_s, m.ident[:, :]).then_inc(ct_ps.sem, 1)

            def output(b):
                pe.wait_ge(ct_done.sem, ct_done.at(b))
                for i in range(NT):
                    last = pe.matmul(misc[:, i * P:(i + 1) * P], ctx_t[:, i * P:(i + 1) * P], m.w_out[:, :],
                                     start=True, stop=True)
                last.then_inc(wo_ps.sem, 1)

            def turn_m(b):
                pe.wait_ge(z2_done.sem, z2_done.at(b))
                transpose_tiles(pe, misc, z2, m.ident[:, :]).then_inc(mt_ps.sem, 1)

            def head():
                h_tiles(0)
                for i in range(NT):
                    project(0, i, head_project[i])
                for c in range(2):
                    turn_keys(0, c, head_turn[c])
                for c in range(2):
                    turn_queries(0, 0, c, head_turn[2 + c])
                pe.wait_ge(v_done.sem, v_done.at(0))
                for n in range(16):
                    scores_for_max(0, 0, n, True)

            def body(b, p, before, behind):
                for t in range(STEPS):
                    if t < STEPS - 16:
                        scores_for_max(b, p, t + 16, False)
                    elif behind:
                        scores_for_max(b + 1, 1 - p, t + 16 - STEPS, False)
                    n = t - SHIFT_LAG
                    if n >= 0:
                        scores_shifted(b, p, n, not before)
                    elif before:
                        scores_shifted(b - 1, 1 - p, n + STEPS, False)
                    for i in range(NT):
                        n = t - VALUE_LAG[i]
                        if n % 16 == 0 and n >= 0:
                            values(b, p, n // 16, i, not before)
                        elif n % 16 == 0 and before:
                            values(b - 1, 1 - p, NG - 1, i, False)
                    if t % 16 == TURN % 16 and (t > 16 or before):
                        g = t // 16 - 1
                        turn_values(b if g >= 0 else b - 1, g % NG)
                    if t == TURN_SHIFTED[0]:
                        if before:
                            pe.wait_ge(q2_done.sem, q2_done.at(b - 1, 4))
                        else:
                            pe.wait_ge(q1_done.sem, q1_done.at(b))
                        turn_shifted(b, p, 0)
                    if t == TURN_H and behind:
                        pe.wait_ge(q2_done.sem, q2_done.at(b, 1))
                        h_tiles(b + 1)
                    if t == PROJECT[0] and behind:
                        project(b + 1, 0)
                    if t == PROJECT[1] and behind:
                        pe.wait_ge(v_done.sem, v_done.at(b + 1, 1))
                        project(b + 1, 1)
                    if t == TURN_CTX and before:
                        if behind:
                            pe.wait_ge(v_done.sem, v_done.at(b + 1, 2))
                        else:
                            pe.wait_ge(q2_done.sem, q2_done.at(b, 1))
                        turn_ctx(b - 1)
                    if t == TURN_SHIFTED[1]:
                        if before:
                            pe.wait_ge(ct_done.sem, ct_done.at(b - 1))
                        else:
                            pe.wait_ge(v_done.sem, v_done.at(b + 1, 2))
                        turn_shifted(b, p, 1)
                    if t == OUTPUT and before:
                        pe.wait_ge(q2_done.sem, q2_done.at(b, 2))
                        output(b - 1)
                    if t == PROJECT[2] and behind:
                        if before:
                            pe.wait_ge(y2_done.sem, y2_done.at(b - 1))
                        else:
                            pe.wait_ge(q2_done.sem, q2_done.at(b, 2))
                        project(b + 1, 2)
                    if t == PROJECT[3] and behind:
                        pe.wait_ge(v_done.sem, v_done.at(b + 1, 3))
                        project(b + 1, 3)
                    if t == TURN_KEYS[0] and behind:
                        pe.wait_ge(v_done.sem, v_done.at(b + 1, 4))
                        turn_keys(b + 1, 0)
                    if t == TURN_SHIFTED[2]:
                        if behind:
                            pe.wait_ge(kt_done.sem, kt_done.at(b + 1, 1))
                        else:
                            pe.wait_ge(y2_done.sem, y2_done.at(b - 1))
                        turn_shifted(b, p, 2)
                    if t == TURN_KEYS[1] and behind:
                        pe.wait_ge(q2_done.sem, q2_done.at(b, 3))
                        turn_keys(b + 1, 1)
                    if t == TURN_QUERIES[0] and behind:
                        pe.wait_ge(kt_done.sem, kt_done.at(b + 1, 2))
                        turn_queries(b + 1, 1 - p, 0)
                    if t == TURN_QUERIES[1] and behind:
                        pe.wait_ge(q1_done.sem, q1_done.at(b + 1, 1))
                        turn_queries(b + 1, 1 - p, 1)
                    if t == TURN_M and before:
                        if behind:
                            pe.wait_ge(q1_done.sem, q1_done.at(b + 1, 2))
                        else:
                            pe.wait_ge(q2_done.sem, q2_done.at(b, 3))
                        turn_m(b - 1)
                    if t == TURN_SHIFTED[3]:
                        if before:
                            pe.wait_ge(mt_done.sem, mt_done.at(b - 1))
                        else:
                            pe.wait_ge(q1_done.sem, q1_done.at(b + 1, 2))
                        turn_shifted(b, p, 3)

            def last():
                for t in range(STEPS, STEPS + 16):
                    n = t - SHIFT_LAG
                    if n < STEPS:
                        scores_shifted(B - 1, 1, n, False)
                    for i in range(NT):
                        if t - VALUE_LAG[i] == STEPS - 16:
                            values(B - 1, 1, NG - 1, i, False)
                turn_values(B - 1, NG - 1)
                pe.wait_ge(q2_done.sem, q2_done.at(B - 1))
                turn_ctx(B - 1)
                output(B - 1)
                turn_m(B - 1)

            batches(pe, head, body, last)


def phase_experts(nc, m, signal, tag, out=None):
    with ExitStack() as ctx:
        def sb(name, shape, dt=F32):
            return ctx.enter_context(nc.sbuf_tensor(tag + name, shape, dt))

        hid = [ctx.enter_context(nc.psum_tensor(f"{tag}hid{i}", [P, 512], F32)) for i in range(4)]
        yps = [ctx.enter_context(nc.psum_tensor(f"{tag}yps{i}", [P, 512], F32)) for i in range(2)]
        misc = [ctx.enter_context(nc.psum_tensor(f"{tag}misc{i}", [P, 512], F32)) for i in range(2)]
        h_full = sb("h_full", [P, NF, S])
        h_hi = sb("h_hi", [P, 2, NF, S], BF16)
        h_lo = sb("h_lo", [P, 2, NF, S], BF16)
        m_hi = sb("m_hi", [P, B * S], BF16)
        m_lo = sb("m_lo", [P, B * S], BF16)
        logit = sb("logit", [P, NT, E])
        top = sb("top", [P, NT, 8])
        top_i = sb("top_i", [P, NT, 8], U32)
        top_f = sb("top_f", [P, NT, 2])
        gap = sb("gap", [P, NT])
        gap_t = sb("gap_t", [P, NT])
        wts = sb("wts", [P, NT, 2])
        one1 = sb("one1", [P, NT, E])
        one2 = sb("one2", [P, NT, E])
        gates = sb("gates", [P, NT, E])
        gates_t = sb("gates_t", [E, S])
        acc = sb("acc", [P, NT, D])
        m_b = sb("m_b", [P, S])

        high_done = signal("high")
        low_done = signal("low")
        copied = signal("copied")
        lg_ps = signal("lg_ps")
        lg_done = signal("lg_done")
        top_done = signal("top_done")
        idx_done = signal("idx_done")
        idxf_done = signal("idxf_done")
        gap_done = signal("gap_done")
        gapt_done = signal("gapt_done")
        wts_done = signal("wts_done")
        one_done = signal("one_done")
        gates_done = signal("gates_done")
        gt_ps = signal("gt_ps")
        gt_done = signal("gt_done")
        b2_ps = signal("b2_ps")
        hid_ps = signal("hid_ps", E * NF)
        h_done = signal("h_done", E * NF)
        hlo_done = signal("hlo_done", E * (NF - 1))
        hlo_pool = signal("hlo_pool", E)
        y_ps = signal("y_ps", E)
        acc_done = signal("acc_done", E + 1)
        x_done = signal("x_done")
        stored = signal("stored", 16)
        stored.before = stored.stands_at
        block = ctx.enter_context(nc.Block())

        @block.sync
        def _(sp):
            if out is not None:
                with sp.Fori(0, B) as b:
                    sp.wait_ge(x_done.sem, x_done.at(b))
                    sp.dma_start(out[bass.ds(b, 1), :, :].rearrange("b (t p) d -> p (b t) d", p=P),
                                 m.x[:, bass.ds(b * NT, NT), :]).then_inc(stored.sem, 16)
                sp.wait_ge(stored.sem, stored.at(B - 1))

        @block.vector
        def _(dve):
            def low(b, e):
                for c in range(NF - 1):
                    n = e * NF + c
                    dve.wait_ge(h_done.sem, h_done.at(b, n + 1))
                    dve.tensor_tensor(h_lo[:, e % 2, c, :], h_full[:, c, :], h_hi[:, e % 2, c, :], ALU.subtract)\
                        .then_inc(hlo_done.sem, 1)

            def best_two(b):
                dve.wait_ge(lg_ps.sem, lg_ps.at(b))
                dve.tensor_copy(logit[:, :, :], tile3(misc[1][:, 0:NT * E])).then_inc(lg_done.sem, 1)
                dve.wait_ge(lg_done.sem, lg_done.at(b))
                fence(dve, m)
                for i in range(NT):
                    last = dve.max(top[:, i, :], logit[:, i, :])
                last.then_inc(top_done.sem, 1)
                dve.wait_ge(top_done.sem, top_done.at(b))
                fence(dve, m)
                dve.tensor_tensor(gap[:, :], top[:, :, 0], top[:, :, 1], ALU.subtract).then_inc(gap_done.sem, 1)
                for i in range(NT):
                    last = dve.max_index(top_i[:, i, :], top[:, i, :], logit[:, i, :])
                last.then_inc(idx_done.sem, 1)
                dve.wait_ge(idx_done.sem, idx_done.at(b))
                dve.tensor_copy(top_f[:, :, :], top_i[:, :, 0:2]).then_inc(idxf_done.sem, 1)

            def weights(b):
                dve.wait_ge(gapt_done.sem, gapt_done.at(b))
                dve.tensor_scalar(wts[:, :, 0], gap_t[:, :], 0.5, 0.5, ALU.mult, ALU.add)
                dve.tensor_scalar(wts[:, :, 1], gap_t[:, :], -0.5, 0.5, ALU.mult, ALU.add).then_inc(wts_done.sem, 1)
                dve.wait_ge(wts_done.sem, wts_done.at(b))
                dve.wait_ge(idxf_done.sem, idxf_done.at(b))
                for i in range(NT):
                    dve.tensor_scalar(one1[:, i, :], m.expert_id[:, :], top_f[:, i, 0:1], wts[:, i, 0:1],
                                      ALU.is_equal, ALU.mult)
                    last = dve.tensor_scalar(one2[:, i, :], m.expert_id[:, :], top_f[:, i, 1:2], wts[:, i, 1:2],
                                             ALU.is_equal, ALU.mult)
                last.then_inc(one_done.sem, 1)
                dve.wait_ge(one_done.sem, one_done.at(b))
                dve.tensor_tensor(gates[:, :, :], one1[:, :, :], one2[:, :, :], ALU.add).then_inc(gates_done.sem, 1)
                dve.wait_ge(gates_done.sem, gates_done.at(b))

            def accumulate(b, e):
                dve.wait_ge(y_ps.sem, y_ps.at(b, e + 1))
                if e > 0:
                    dve.wait_ge(acc_done.sem, acc_done.at(b, e))
                for i in range(NT):
                    under = acc[:, i, :] if e > 0 else m.y[:, bass.ds(b * NT + i, 1), :].rearrange("p t d -> p (t d)")
                    last = dve.scalar_tensor_tensor(out=acc[:, i, :], in0=yps[e % 2][:, i * P:(i + 1) * P],
                                                    scalar=gates[:, i, e:e + 1], in1=under,
                                                    op0=ALU.mult, op1=ALU.add)
                last.then_inc(acc_done.sem, 1)

            def one_batch(b, behind):
                x_b = m.x[:, bass.ds(b * NT, NT), :]
                for e in range(1, E):
                    low(b, e)
                    accumulate(b, e - 1)
                    if e == 2:
                        dve.wait_ge(gt_ps.sem, gt_ps.at(b))
                        dve.tensor_copy(gates_t[:, :], misc[1][0:E, :]).then_inc(gt_done.sem, 1)
                if behind:
                    best_two(b + 1)
                    low(b + 1, 0)
                accumulate(b, E - 1)
                dve.wait_ge(b2_ps.sem, b2_ps.at(b))
                dve.wait_ge(acc_done.sem, acc_done.at(b, E))
                dve.tensor_tensor(acc[:, :, :], tile3(misc[0][:, :]), acc[:, :, :], ALU.add).then_inc(acc_done.sem, 1)
                dve.wait_ge(acc_done.sem, acc_done.at(b))
                dve.scalar_tensor_tensor(out=x_b, in0=acc[:, :, :], scalar=0.5, in1=x_b, op0=ALU.mult,
                                         op1=ALU.add).then_inc(x_done.sem, 1)
                if behind:
                    weights(b + 1)

            best_two(0)
            low(0, 0)
            weights(0)
            with dve.Fori(0, B - 1) as b:
                one_batch(b, True)
            one_batch(B - 1, False)

        @block.scalar
        def _(act):
            def tanh(b):
                act.wait_ge(gap_done.sem, gap_done.at(b))
                act.activation(gap_t[:, :], gap[:, :], ACT.Tanh, scale=0.5).then_inc(gapt_done.sem, 1)

            def gelus(b, e, first=False):
                for c in range(NF):
                    n = e * NF + c
                    act.wait_ge(hid_ps.sem, hid_ps.at(b, n + 1))
                    if e >= 2 and c == 0:
                        act.wait_ge(y_ps.sem, y_ps.at(b, e - 1))
                    act.activation(h_hi[:, e % 2, c, :], hid[n % 4][:, :], ACT.Gelu_apprx_tanh,
                                   bias=m.b1[:, e, c:c + 1])
                    if not first and c < NF - 1:
                        act.wait_ge(hlo_done.sem, hlo_done.at(b, (e - 1) * (NF - 1) + c + 1))
                    elif not first:
                        act.wait_ge(hlo_pool.sem, hlo_pool.at(b, e))
                    act.activation(h_full[:, c, :], hid[n % 4][:, :], ACT.Gelu_apprx_tanh,
                                   bias=m.b1[:, e, c:c + 1]).then_inc(h_done.sem, 1)

            gelus(0, 0, True)
            tanh(0)
            with act.Fori(0, B - 1) as b:
                for e in range(1, E):
                    gelus(b, e)
                gelus(b + 1, 0)
                tanh(b + 1)
            for e in range(1, E):
                gelus(B - 1, e)

        @block.tensor
        def _(pe):
            def hidden(b, e, first=False):
                for c in range(NF):
                    n = e * NF + c
                    if not first:
                        pe.wait_ge(h_done.sem, h_done.at(b, n - 3))
                    w_hi = m.w1_hi[:, e, c * P:(c + 1) * P]
                    w_lo = m.w1_lo[:, e, c * P:(c + 1) * P]
                    high, low = m_hi[:, bass.ds(b * S, S)], m_lo[:, bass.ds(b * S, S)]
                    pe.matmul(hid[n % 4][:, :], w_hi, high, start=True, stop=False)
                    pe.matmul(hid[n % 4][:, :], w_hi, low, start=False, stop=False)
                    pe.matmul(hid[n % 4][:, :], w_lo, high, start=False, stop=True).then_inc(hid_ps.sem, 1)

            def outputs(b, e):
                if e >= 2:
                    pe.wait_ge(acc_done.sem, acc_done.at(b, e - 1))
                pe.wait_ge(hlo_done.sem, hlo_done.at(b, (NF - 1) * (e + 1)))
                pe.wait_ge(hlo_pool.sem, hlo_pool.at(b, e + 1))
                for i in range(NT):
                    tok = slice(i * P, (i + 1) * P)
                    for c in range(NF):
                        w_hi = m.w2_hi[:, e, c * P:(c + 1) * P]
                        w_lo = m.w2_lo[:, e, c * P:(c + 1) * P]
                        pe.matmul(yps[e % 2][:, tok], h_hi[:, e % 2, c, tok], w_hi, start=(c == 0), stop=False)
                        pe.matmul(yps[e % 2][:, tok], h_hi[:, e % 2, c, tok], w_lo, start=False, stop=False)
                        last = pe.matmul(yps[e % 2][:, tok], h_lo[:, e % 2, c, tok], w_hi,
                                         start=False, stop=(c == NF - 1))
                last.then_inc(y_ps.sem, 1)

            def turn_gates(b):
                pe.wait_ge(gates_done.sem, gates_done.at(b))
                for i in range(NT):
                    last = pe.transpose(misc[1][0:E, i * P:(i + 1) * P], gates[:, i, :], m.ident[:, :])
                last.then_inc(gt_ps.sem, 1)

            def output_bias(b):
                pe.wait_ge(gt_done.sem, gt_done.at(b))
                for i in range(NT):
                    last = pe.matmul(misc[0][:, i * P:(i + 1) * P], gates_t[:, i * P:(i + 1) * P], m.b2[:, :],
                                     start=True, stop=True)
                last.then_inc(b2_ps.sem, 1)

            def logits(b):
                pe.wait_ge(copied.sem, copied.at(b))
                for i in range(NT):
                    last = pe.matmul(misc[1][:, i * E:(i + 1) * E], m_b[:, i * P:(i + 1) * P],
                                     m.w_gate[:, :], start=True, stop=True)
                last.then_inc(lg_ps.sem, 1)
                pe.wait_ge(low_done.sem, low_done.at(b))

            def one_batch(b, behind):
                for e in range(E):
                    if e + 1 < E:
                        hidden(b, e + 1)
                    elif behind:
                        logits(b + 1)
                        hidden(b + 1, 0)
                    outputs(b, e)
                    if e == 1:
                        turn_gates(b)
                    if e == 3:
                        output_bias(b)

            logits(0)
            hidden(0, 0, True)
            with pe.Fori(0, B - 1) as b:
                one_batch(b, True)
            one_batch(B - 1, False)

        @block.gpsimd
        def _(pool):
            def parts(b):
                full, high, low = (t[:, bass.ds(b * S, S)].rearrange("p (t d) -> p t d", d=D)
                                   for t in (m.m_t, m_hi, m_lo))
                pool.tensor_tensor(high, full, again(m.zero_bf[:, :], NT), ALU.add).then_inc(high_done.sem, 1)
                pool.wait_ge(high_done.sem, high_done.at(b))
                pool.tensor_tensor(low, full, high, ALU.subtract).then_inc(low_done.sem, 1)

            def gate_copy(b):
                pool.tensor_tensor(tile3(m_b[:, :]), m.m_t[:, bass.ds(b * S, S)].rearrange("p (t d) -> p t d", d=D),
                                   again(m.zero_bf[:, :], NT), ALU.add).then_inc(copied.sem, 1)

            def low(b, e):
                pool.wait_ge(h_done.sem, h_done.at(b, NF * (e + 1)))
                pool.tensor_tensor(h_lo[:, e % 2, NF - 1, :], h_full[:, NF - 1, :], h_hi[:, e % 2, NF - 1, :],
                                   ALU.subtract).then_inc(hlo_pool.sem, 1)

            def one_batch(b, behind):
                low(b, 0)
                if behind:
                    pool.wait_ge(lg_ps.sem, lg_ps.at(b))
                    gate_copy(b + 1)
                low(b, 1)
                if behind:
                    parts(b + 1)
                for e in range(2, E):
                    low(b, e)

            parts(0)
            gate_copy(0)
            with pool.Fori(0, B - 1) as b:
                one_batch(b, True)
            one_batch(B - 1, False)


def phase_linear(nc, m, signal):
    STEPS = NG * 16
    VALUE_LAG = (10, 12, 15, 18)
    TAKE, TURN, STORE = 20, 23, 25
    NS, SLOTS = 4, 16
    with ExitStack() as ctx:
        def sb(name, shape, dt=F32):
            return ctx.enter_context(nc.sbuf_tensor("li_" + name, shape, dt))

        score = [ctx.enter_context(nc.psum_tensor(f"li_score{i}", [P, 512], F32)) for i in range(NS)]
        av = ctx.enter_context(nc.psum_tensor("li_av", [P, 512], F32))
        avt = ctx.enter_context(nc.psum_tensor("li_avt", [P, 512], F32))
        misc = [ctx.enter_context(nc.psum_tensor(f"li_misc{i}", [P, 512], F32)) for i in range(2)]
        misc_bf = [t[:, :].bitcast(BF16) for t in misc]
        st = sb("st", [P, NT, 6])
        mv = sb("mv", [P, NT, 2])
        var = sb("var", [P, NT])
        rstd = sb("rstd", [P, NT])
        y = sb("y", [P, NT, D])
        y_t = sb("y_t", [P, S])
        sq = sb("sq", [P, NT, 2 * D])
        ss = sb("ss", [P, NT, 2 * H])
        ms = sb("ms", [P, NT, 2 * H])
        root = sb("root", [P, NT, 2 * H])
        r0 = sb("r0", [P, NT, 2 * H])
        r1 = sb("r1", [P, NT, 2 * H])
        rr = sb("rr", [P, NT, 2 * H])
        qv = sb("qv", [P, NT, 2 * D])
        k_t = sb("k_t", [P, NG, S], BF16)
        q1 = sb("q1", [P, 2, NG, S], BF16)
        prob = sb("prob", [P, GH * sum(S - i * P for i in range(NT))])
        av_s = sb("av_s", [P, S])
        ctx_s = sb("ctx_s", [P, NT, D])

        stats = signal("stats")
        mv_done = signal("mv")
        var_done = signal("var")
        rstd_done = signal("rstd")
        y_done = signal("y")
        yt_ps = signal("yt_ps")
        yt_done = signal("yt")
        qv_ps = signal("qv_ps", 2)
        sq_done = signal("sq", 2)
        ss_done = signal("ss", 2)
        ms_done = signal("ms")
        root_done = signal("root")
        newton = signal("newton", 4)
        rr_done = signal("rr")
        qr_done = signal("qr", 2)
        qw_done = signal("qw")
        hi_done = signal("hi", 2)
        copy_done = signal("copy", 2)
        lo_done = signal("lo", 2)
        v_done = signal("v")
        kt_ps = signal("kt_ps", 2)
        kt_done = signal("kt", 2)
        q1_ps = signal("q1_ps", 2)
        q1_done = signal("q1", 2)
        kz_done = signal("kz", 16 * GH)
        s_ps = signal("s_ps", STEPS)
        mask_done = signal("mask", STEPS)
        rest_done = signal("rest", NG * 12)
        av_part = signal("av_part", NG * NT)
        avs_done = signal("avs", NG)
        avt_ps = signal("avt_ps", NG)
        ctx_done = signal("ctx", NG)
        x_done = signal("x")
        block = ctx.enter_context(nc.Block())

        def batches(eng, head, body, last):
            head()
            body(0, 0, False, True)
            with eng.Fori(0, (B - 2) // 2) as i:
                body(i * 2 + 1, 1, True, True)
                body(i * 2 + 2, 0, True, True)
            body(B - 1, 1, True, False)
            last()

        def weights_of(i, j):
            width = S - i * P
            start = GH * sum(S - k * P for k in range(i)) + j * width
            return prob[:, start:start + width]

        def per_head(ap):
            return ap.rearrange("p t (h d) -> p t h d", d=DH)

        @block.sync
        def _(sp):
            def spread(b, p):
                sp.wait_ge(kt_done.sem, kt_done.at(b))
                for j in range(GH):
                    rows = slice(HC * j, HC * (j + 1))
                    sp.dma_start(m.kz[rows, p, j, :, :], k_t[rows, :, :]).then_inc(kz_done.sem, 16)

            spread(0, 0)
            with sp.Fori(0, (B - 2) // 2) as i:
                spread(i * 2 + 1, 1)
                spread(i * 2 + 2, 0)
            spread(B - 1, 1)
            sp.wait_ge(kz_done.sem, kz_done.at(B - 1))

        @block.gpsimd
        def _(pool):
            def heads_of(t):
                return t.rearrange("p (h d) -> p h d", d=DH)

            def inverse_deviation(b):
                pool.wait_ge(var_done.sem, var_done.at(b))
                pool.tensor_tensor(rstd[:, :], var[:, :], m.half_pow[:, 0, :], ALU.pow).then_inc(rstd_done.sem, 1)

            def keys(b):
                pool.wait_ge(hi_done.sem, hi_done.at(b, 1))
                for i in range(NT):
                    last = pool.tensor_tensor(m.k_split[:, i, :, 8:16], m.k_split[:, i, :, 0:8],
                                              heads_of(m.zero_bf[:, :]), ALU.add)
                last.then_inc(copy_done.sem, 1)
                for i in range(NT):
                    last = pool.tensor_tensor(m.k_split[:, i, :, 16:24], heads_of(y[:, i, :]),
                                              m.k_split[:, i, :, 0:8], ALU.subtract)
                last.then_inc(lo_done.sem, 1)

            def queries_and_values(b, p):
                pool.wait_ge(qr_done.sem, qr_done.at(b))
                pool.tensor_tensor(qv[:, :, 0:D], qv[:, :, 0:D], again(m.norm_w[:, 0:D], NT), ALU.mult)\
                    .then_inc(qw_done.sem, 1)
                pool.tensor_tensor(m.v_wide[:, p, :, :, 0:DH], per_head(qv[:, :, D:2 * D]),
                                   per_head(again(m.norm_w[:, D:2 * D], NT)), ALU.mult).then_inc(v_done.sem, 1)
                pool.wait_ge(hi_done.sem, hi_done.at(b, 2))
                for i in range(NT):
                    last = pool.tensor_tensor(m.q_split[:, 0, i, :, 16:24], m.q_split[:, 0, i, :, 0:8],
                                              heads_of(m.zero_bf[:, :]), ALU.add)
                last.then_inc(copy_done.sem, 1)
                for i in range(NT):
                    last = pool.tensor_tensor(m.q_split[:, 0, i, :, 8:16], heads_of(qv[:, i, 0:D]),
                                              m.q_split[:, 0, i, :, 0:8], ALU.subtract)
                last.then_inc(lo_done.sem, 1)

            def head():
                inverse_deviation(0)
                keys(0)
                queries_and_values(0, 0)

            def body(b, p, before, behind):
                if behind:
                    inverse_deviation(b + 1)
                    keys(b + 1)
                    queries_and_values(b + 1, 1 - p)

            batches(pool, head, body, lambda: None)

        @block.vector
        def _(dve):
            def rows(b):
                return m.x[:, bass.ds(b * NT, NT), :]

            def stats_x(b):
                layer_stats(dve, m, rows(b), st, mv, stats, mv_done, b)
                dve.wait_ge(mv_done.sem, mv_done.at(b))
                dve.tensor_scalar(var[:, :], mv[:, :, 1], EPS, None, ALU.add).then_inc(var_done.sem, 1)

            def norm_x(b):
                dve.wait_ge(rstd_done.sem, rstd_done.at(b))
                normalise(dve, y, rows(b), mv, rstd).then_inc(y_done.sem, 1)

            def sum_squares(b, c):
                dve.wait_ge(sq_done.sem, sq_done.at(b, c + 1))
                dve.tensor_reduce(ss[:, 2 * c:2 * c + 2, :], per_head(sq[:, 2 * c:2 * c + 2, :]), AX.X, ALU.add)\
                    .then_inc(ss_done.sem, 1)

            def mean_square(b):
                dve.wait_ge(ss_done.sem, ss_done.at(b))
                dve.tensor_scalar(ms[:, :, :], ss[:, :, :], 1.0 / DH, EPS_RMS, ALU.mult, ALU.add)\
                    .then_inc(ms_done.sem, 1)

            def inverse_root(b):
                dve.wait_ge(root_done.sem, root_done.at(b))
                dve.reciprocal(r0[:, :, :], root[:, :, :]).then_inc(newton.sem, 1)

            def newton_square(b):
                dve.wait_ge(newton.sem, newton.at(b, 1))
                dve.tensor_tensor(r1[:, :, :], r0[:, :, :], r0[:, :, :], ALU.mult).then_inc(newton.sem, 1)

            def newton_product(b):
                dve.wait_ge(newton.sem, newton.at(b, 2))
                dve.tensor_tensor(r1[:, :, :], r1[:, :, :], ms[:, :, :], ALU.mult).then_inc(newton.sem, 1)

            def newton_factor(b):
                dve.wait_ge(newton.sem, newton.at(b, 3))
                dve.tensor_scalar(r1[:, :, :], r1[:, :, :], -0.5, 1.5, ALU.mult, ALU.add).then_inc(newton.sem, 1)

            def newton_step(b):
                dve.wait_ge(newton.sem, newton.at(b, 4))
                dve.tensor_tensor(rr[:, :, :], r0[:, :, :], r1[:, :, :], ALU.mult).then_inc(rr_done.sem, 1)

            def rms_norm(b, c):
                dve.wait_ge(rr_done.sem, rr_done.at(b))
                dve.tensor_tensor(
                    qv[:, 2 * c:2 * c + 2, :].rearrange("p t (h d) -> p (t h) d", d=DH),
                    misc[c][:, :].rearrange("p (h d) -> p h d", d=DH),
                    wide(rr[:, 2 * c:2 * c + 2, :].rearrange("p t h -> p (t h)"), DH), ALU.mult)\
                    .then_inc(qr_done.sem, 1)

            def mask(b, n, first):
                g, u, i = n // 16, n % 16, n % 16 // GH
                if u < 12:
                    dve.wait_ge(rest_done.sem, rest_done.at(b, 12 * g + u + 1))
                else:
                    dve.wait_ge(s_ps.sem, s_ps.at(b, n + 1))
                if n % 4 == 0 and not (first and n < SLOTS):
                    dve.wait_ge(av_part.sem, av_part.at(b, (n - SLOTS) // 4 + 1))
                dve.tensor_tensor(weights_of(i, n % GH)[:, 0:P], score[n % NS][:, i * P:(i + 1) * P],
                                  m.causal[:, :], ALU.mult).then_inc(mask_done.sem, 1)

            def store(b, g):
                dve.wait_ge(avt_ps.sem, avt_ps.at(b, g + 1))
                t = avt[:, :].rearrange("p (t h c) -> p t h c", t=NT, c=HC)
                dve.tensor_copy(ctx_s[:, :, 32 * g:32 * (g + 1)].rearrange("p t (h d) -> p t h d", d=DH),
                                t[:, :, :, 0:DH]).then_inc(ctx_done.sem, 1)

            def add_x(b):
                dve.wait_ge(ctx_done.sem, ctx_done.at(b))
                dve.tensor_tensor(rows(b), rows(b), ctx_s[:, :, :], ALU.add).then_inc(x_done.sem, 1)

            def head():
                dve.memset(m.q_split[:, 0, :, :, 24:26], 0.0)
                stats_x(0)
                norm_x(0)
                for c in range(2):
                    sum_squares(0, c)
                for step in (mean_square, inverse_root, newton_square, newton_product, newton_factor,
                             newton_step):
                    step(0)
                for c in range(2):
                    rms_norm(0, c)

            def body(b, p, before, behind):
                for t in range(STEPS):
                    if t >= 1:
                        mask(b, t - 1, not before)
                    elif before:
                        mask(b - 1, STEPS - 1, False)
                    if t % 16 == STORE % 16 and (t > 16 or before):
                        g = t // 16 - 1
                        store(b if g >= 0 else b - 1, g % NG)
                    if t == 12 and before:
                        add_x(b - 1)
                    if behind:
                        if t == 0:
                            stats_x(b + 1)
                        if t == 7:
                            norm_x(b + 1)
                        if t in (18, 20):
                            sum_squares(b + 1, (t - 18) // 2)
                        if t == 21:
                            mean_square(b + 1)
                        if t == 26:
                            inverse_root(b + 1)
                        if t == 27:
                            newton_square(b + 1)
                        if t == 28:
                            newton_product(b + 1)
                        if t == 29:
                            newton_factor(b + 1)
                        if t == 30:
                            newton_step(b + 1)
                        if t in (31, 33):
                            rms_norm(b + 1, (t - 31) // 2)

            def last():
                mask(B - 1, STEPS - 1, False)
                store(B - 1, NG - 1)
                add_x(B - 1)

            batches(dve, head, body, last)

        @block.scalar
        def _(act):
            def key_high(b):
                act.wait_ge(y_done.sem, y_done.at(b))
                act.activation(m.k_split[:, :, :, 0:DH], per_head(y[:, :, :]), ACT.Copy).then_inc(hi_done.sem, 1)

            def to_y(b):
                act.wait_ge(yt_ps.sem, yt_ps.at(b))
                act.activation(y_t[:, :], misc[0][:, :], ACT.Copy).then_inc(yt_done.sem, 1)

            def squares(b, c):
                act.wait_ge(qv_ps.sem, qv_ps.at(b, c + 1))
                act.activation(sq[:, 2 * c:2 * c + 2, :], tile3(misc[c][:, :], 2), ACT.Square)\
                    .then_inc(sq_done.sem, 1)

            def roots(b):
                act.wait_ge(ms_done.sem, ms_done.at(b))
                act.activation(root[:, :, :], ms[:, :, :], ACT.Sqrt).then_inc(root_done.sem, 1)

            def query_high(b):
                act.wait_ge(qw_done.sem, qw_done.at(b))
                act.activation(m.q_split[:, 0, :, :, 0:DH], per_head(qv[:, :, 0:D]), ACT.Copy)\
                    .then_inc(hi_done.sem, 1)

            def to_kt(b, c):
                act.wait_ge(kt_ps.sem, kt_ps.at(b, c + 1))
                act.activation(k_t[:, 2 * c:2 * c + 2, :], tile3(misc_bf[c], 2), ACT.Copy).then_inc(kt_done.sem, 1)

            def to_q1(b, p, c):
                act.wait_ge(q1_ps.sem, q1_ps.at(b, c + 1))
                act.activation(q1[:, p, 2 * c:2 * c + 2, :], tile3(misc_bf[c], 2), ACT.Copy)\
                    .then_inc(q1_done.sem, 1)

            def rest(b, n, first):
                i = n % 16 // GH
                act.wait_ge(s_ps.sem, s_ps.at(b, n + 1))
                if n % 4 == 0 and not (first and n < SLOTS):
                    act.wait_ge(av_part.sem, av_part.at(b, (n - SLOTS) // 4 + 1))
                act.activation(weights_of(i, n % GH)[:, P:], score[n % NS][:, (i + 1) * P:], ACT.Copy)\
                    .then_inc(rest_done.sem, 1)

            def take_values(b, g):
                act.wait_ge(av_part.sem, av_part.at(b, NT * (g + 1)))
                act.activation(av_s[:, :], av[:, :], ACT.Copy).then_inc(avs_done.sem, 1)

            def head():
                key_high(0)
                to_y(0)
                for c in range(2):
                    squares(0, c)
                roots(0)
                query_high(0)
                for c in range(2):
                    to_kt(0, c)
                for c in range(2):
                    to_q1(0, 0, c)

            def body(b, p, before, behind):
                for t in range(STEPS):
                    if t % 16 < 12:
                        rest(b, t, not before)
                    if t % 16 == TAKE % 16 and (t > 16 or before):
                        g = t // 16 - 1
                        take_values(b if g >= 0 else b - 1, g % NG)
                    if behind:
                        if t == 9:
                            key_high(b + 1)
                        if t == 11:
                            to_y(b + 1)
                        if t in (15, 17):
                            squares(b + 1, (t - 15) // 2)
                        if t == 23:
                            roots(b + 1)
                        if t == 42:
                            query_high(b + 1)
                        if t in (38, 41):
                            to_kt(b + 1, (t - 38) // 3)
                        if t in (56, 59):
                            to_q1(b + 1, 1 - p, (t - 56) // 3)

            def last():
                take_values(B - 1, NG - 1)

            batches(act, head, body, last)

        @block.tensor
        def _(pe):
            def y_tiles(b):
                pe.wait_ge(y_done.sem, y_done.at(b))
                transpose_tiles(pe, misc[0], y, m.ident[:, :]).then_inc(yt_ps.sem, 1)

            def project(b, c):
                pe.wait_ge(yt_done.sem, yt_done.at(b))
                for i in (2 * c, 2 * c + 1):
                    o = (i % 2) * 2 * D
                    last = pe.matmul(misc[c][:, o:o + 2 * D], y_t[:, i * P:(i + 1) * P], m.w_lin[:, :],
                                     start=True, stop=True)
                last.then_inc(qv_ps.sem, 1)

            def turn(dst, src, g):
                for i in range(NT):
                    last = pe.transpose(dst[:, i * P:(i + 1) * P],
                                        src[:, i, GH * g:GH * (g + 1), :].rearrange("p h c -> p (h c)"),
                                        m.ident_bf[:, :])
                return last

            def turn_keys(b, c):
                pe.wait_ge(qr_done.sem, qr_done.at(b, c + 1))
                pe.wait_ge(lo_done.sem, lo_done.at(b, 1))
                pe.wait_ge(copy_done.sem, copy_done.at(b, 1))
                turn(misc_bf[c][:, 0:S], m.k_split, 2 * c)
                turn(misc_bf[c][:, S:2 * S], m.k_split, 2 * c + 1).then_inc(kt_ps.sem, 1)

            def turn_queries(b, c):
                pe.wait_ge(kt_done.sem, kt_done.at(b, c + 1))
                pe.wait_ge(lo_done.sem, lo_done.at(b, 2))
                pe.wait_ge(copy_done.sem, copy_done.at(b, 2))
                turn(misc_bf[c][:, 0:S], m.q_split[:, 0, :, :, :], 2 * c)
                turn(misc_bf[c][:, S:2 * S], m.q_split[:, 0, :, :, :], 2 * c + 1).then_inc(q1_ps.sem, 1)

            def scores(b, p, n, first):
                g, i, j = n // 16, n % 16 // GH, n % GH
                if n == 0:
                    pe.wait_ge(kz_done.sem, kz_done.at(b))
                    pe.wait_ge(q1_done.sem, q1_done.at(b))
                if not (first and n < NS):
                    pe.wait_ge(mask_done.sem, mask_done.at(b, n - NS + 1))
                pe.matmul(score[n % NS][:, i * P:], m.kz[:, p, j, g, i * P:(i + 1) * P], q1[:, p, g, i * P:],
                          start=True, stop=True).then_inc(s_ps.sem, 1)

            def values(b, p, g, i, first):
                pe.wait_ge(mask_done.sem, mask_done.at(b, 16 * g + 4 * (i + 1)))
                if i == 0:
                    if g == 0:
                        pe.wait_ge(v_done.sem, v_done.at(b))
                    if not (first and g == 0):
                        pe.wait_ge(avs_done.sem, avs_done.at(b, g))
                for j in range(GH):
                    last = pe.matmul(av[HC * j:HC * (j + 1), i * P:], m.v_wide[:, p, i, GH * g + j, :],
                                     weights_of(i, j), start=(i == 0), stop=(i == NT - 1))
                last.then_inc(av_part.sem, 1)

            def turn_values(b, g, first):
                pe.wait_ge(avs_done.sem, avs_done.at(b, g + 1))
                if not (first and g == 0):
                    pe.wait_ge(ctx_done.sem, ctx_done.at(b, g))
                transpose_tiles(pe, avt, tile3(av_s[:, :]), m.ident[:, :]).then_inc(avt_ps.sem, 1)

            def head():
                y_tiles(0)
                for c in range(2):
                    project(0, c)
                for c in range(2):
                    turn_keys(0, c)
                for c in range(2):
                    turn_queries(0, c)

            def body(b, p, before, behind):
                for t in range(STEPS):
                    scores(b, p, t, not before)
                    for i in range(NT):
                        n = t - VALUE_LAG[i]
                        if n % 16 == 0 and n >= 0:
                            values(b, p, n // 16, i, not before)
                        elif n % 16 == 0 and before:
                            values(b - 1, 1 - p, NG - 1, i, False)
                    if t % 16 == TURN % 16 and (t > 16 or before):
                        g = t // 16 - 1
                        turn_values(b if g >= 0 else b - 1, g % NG, not before)
                    if behind:
                        if t == 10:
                            y_tiles(b + 1)
                        if t in (14, 16):
                            project(b + 1, (t - 14) // 2)
                        if t in (37, 40):
                            turn_keys(b + 1, (t - 37) // 3)
                        if t in (55, 58):
                            turn_queries(b + 1, (t - 55) // 3)

            def last():
                for i in range(NT):
                    if VALUE_LAG[i] >= 16:
                        values(B - 1, 1, NG - 1, i, False)
                turn_values(B - 1, NG - 1, False)

            batches(pe, head, body, last)


def macaron_kernel(nc, a, out):
    with ExitStack() as ctx:
        m = Memory()

        def keep_in(where, name, shape, dt=F32):
            return where.enter_context(nc.sbuf_tensor("m_" + name, shape, dt))

        def keep(name, shape, dt=F32):
            return keep_in(ctx, name, shape, dt)

        m.x = keep("x", [P, B * NT, D])
        m.ident = keep("ident", [P, P])
        m.ident_bf = keep("ident_bf", [P, P], BF16)
        m.causal = keep("causal", [P, P])
        m.expert_id = keep("expert_id", [P, E])
        m.half_pow = keep("half_pow", [P, 2, NT])
        m.eps = keep("eps", [P, NT])
        m.zero_bf = keep("zero_bf", [P, D], BF16)
        m.fence = keep("fence", [1, 4])
        m.pool_fence = keep("pool_fence", [1, 12])
        m.half_pi = keep("half_pi", [P, 1])
        m.w_out = keep("w_out", [P, D])
        m.w_lin = keep("w_lin", [P, 2 * D])
        m.w_qkv = keep("w_qkv", [P, 3 * D])
        m.w_gate = keep("w_gate", [P, E])
        m.w1_hi = keep("w1_hi", [P, E, F], BF16)
        m.w1_lo = keep("w1_lo", [P, E, F], BF16)
        m.w2_hi = keep("w2_hi", [P, E, F], BF16)
        m.w2_lo = keep("w2_lo", [P, E, F], BF16)
        m.b1 = keep("b1", [P, E, NF])
        m.b2 = keep("b2", [E, D])
        m.b_pv = keep("b_pv", [P, 1])
        m.b_k = keep("b_k", [P, 1])
        m.b_kv = keep("b_kv", [P, 1])
        m.b_g1 = keep("b_g1", [P, 1])
        m.b_b1 = keep("b_b1", [D // 2, 1])
        m.ln_g = keep("ln_g", [P, 1])
        m.ln_b = keep("ln_b", [P, 1])
        m.ln1_g = keep("ln1_g", [P, 1])
        m.ln1_b = keep("ln1_b", [P, 1])
        m.ln2_g = keep("ln2_g", [P, 1])
        m.ln2_b = keep("ln2_b", [P, 1])
        m.half_bg2 = keep("half_bg2", [P, 1])
        m.half_bb2 = keep("half_bb2", [P, 1])
        m.norm_w = keep("norm_w", [P, 2 * D])
        m.kz = keep("kz", [P, 2, GH, NG, S], BF16)
        m.q_split = keep("q_split", [P, 2, NT, H, HC], BF16)
        m.k_split = keep("k_split", [P, NT, H, HC], BF16)
        m.v_wide = keep("v_wide", [P, 2, NT, H, HC])

        mixer = Signals(nc, ctx, "mx_")
        softmax = Signals(nc, ctx, "sm_")
        with ExitStack() as early:
            m.ones = keep_in(early, "ones", [P, P])
            m.w_pv = keep_in(early, "w_pv", [P, D])
            m.w_k = keep_in(early, "w_k", [P, D])
            m.w_kv = keep_in(early, "w_kv", [P, D])
            m.w_o = keep_in(early, "w_o", [P, D])
            m.w_eff = keep_in(early, "w_eff", [P, D])
            m.w_g2 = keep_in(early, "w_g2", [P, D])
            m.w_g1 = keep_in(early, "w_g1", [P, 2, D])
            m.w_b1 = keep_in(early, "w_b1", [P, D // 2])
            m.w_b2 = keep_in(early, "w_b2", [D // 2, P])
            m.ffn_bias = keep_in(early, "ffn_bias", [P, D])
            m.half_bias = keep_in(early, "half_bias", [P, D])
            m.bo = keep_in(early, "bo", [P, D])
            m.late_loaded = ctx.enter_context(nc.semaphore("late_loaded"))
            m.zeros = keep_in(early, "zeros", [P, S])
            m.pos_cos = keep_in(early, "pos_cos", [P, S])
            m.pos_sin = keep_in(early, "pos_sin", [P, S])
            m.key_cos = keep_in(early, "key_cos", [P, 2, S + 1])
            m.key_sin = keep_in(early, "key_sin", [P, 2, S + 1])
            m.u_t = keep_in(early, "u_t", [P, 2, S + 1])
            phase_load(nc, a, m, ctx)
            spare = phase_mixer(nc, a, m, mixer.run())
        experts = Signals(nc, ctx, "ex_", spare[:len(spare) // 2])
        linear = Signals(nc, ctx, "li_", spare[len(spare) // 2:])
        m.y = keep("y", [P, B * NT, D])
        m.m_t = keep("m_t", [P, B * S])
        phase_softmax(nc, m, softmax.run(), "s1_")
        phase_experts(nc, m, experts.run(), "e1_")
        phase_linear(nc, m, linear.run())
        phase_softmax(nc, m, softmax.run(), "s2_")
        phase_experts(nc, m, experts.run(), "e2_", out)


def kernel(**inputs):
    import concourse.bacc as bacc
    from concourse.bass_utils import run_bass_kernel_spmd

    nc = bacc.Bacc("TRN2", target_bir_lowering=False, num_devices=1)
    arrays, args = {}, {}
    for name in INS:
        a = np.ascontiguousarray(inputs[name])
        arrays[f"in_{name}"] = a
        args[name] = nc.dram_tensor(f"in_{name}", a.shape, mybir.dt.from_np(a.dtype), kind="ExternalInput").ap()
    out = nc.dram_tensor("out_x", (B, S, D), F32, kind="ExternalOutput").ap()
    macaron_kernel(nc, args, out)
    r = run_bass_kernel_spmd(nc, [arrays], core_ids=[0])
    return r.results[0]["out_x"]
```
